# Optimizing a Trainium2 kernel written in Bass

```python
import numpy as np
import jax
import jax.numpy as jnp

def _softmax(x, axis=-1):
    return jax.nn.softmax(x, axis=axis)

def _gelu(x):
    return jax.nn.gelu(x, approximate=True)

def _silu(x):
    return jax.nn.silu(x)

def _sigmoid(x):
    return jax.nn.sigmoid(x)

def _layernorm(x, axis=-1, eps=1e-05):
    m = jnp.mean(x, axis=axis, keepdims=True)
    v = jnp.var(x, axis=axis, keepdims=True)
    return (x - m) / jnp.sqrt(v + eps)

def _scatter_add(tgt, idx, src, axis=0):
    return tgt.at[idx].add(src)

def _segment_sum(src, seg, n):
    return jax.ops.segment_sum(src, seg, n)
kernel_name = 'mk_seq_postln_d1_jaxref_r4_711e97'

def setup_inputs(seed: int=0):
    np.random.seed(seed)
    _w = jnp.asarray

    def _L0_attn_setup():
        import jax, jax.numpy as jnp
        import numpy as np
        import math
        DIM = 256
        NUM_HEADS = 16
        HEAD_DIM = DIM // NUM_HEADS
        LAYER_IDX = 12
        LAMBDA_INIT = 0.8 - 0.6 * math.exp(-0.3 * (LAYER_IDX - 1))
        LN_EPS = 1e-05
        key = jax.random.key(seed)
        ks = jax.random.split(key, 11)
        B, S = (2, 512)
        x = jax.random.normal(ks[0], (B, S, DIM), dtype=jnp.float32)
        s = 1.0 / math.sqrt(DIM)
        Wq = jax.random.normal(ks[1], (DIM, 2 * DIM), dtype=jnp.float32) * s
        Wk = jax.random.normal(ks[2], (DIM, 2 * DIM), dtype=jnp.float32) * s
        Wv = jax.random.normal(ks[3], (DIM, DIM), dtype=jnp.float32) * s
        Wo = jax.random.normal(ks[4], (DIM, DIM), dtype=jnp.float32) * s
        lambda_q1 = jax.random.normal(ks[5], (HEAD_DIM,), dtype=jnp.float32) * 0.1
        lambda_k1 = jax.random.normal(ks[6], (HEAD_DIM,), dtype=jnp.float32) * 0.1
        lambda_q2 = jax.random.normal(ks[7], (HEAD_DIM,), dtype=jnp.float32) * 0.1
        lambda_k2 = jax.random.normal(ks[8], (HEAD_DIM,), dtype=jnp.float32) * 0.1
        gamma = jnp.ones((DIM,), dtype=jnp.float32)
        beta = jnp.zeros((DIM,), dtype=jnp.float32)
        return {'x': x, 'Wq': Wq, 'Wk': Wk, 'Wv': Wv, 'Wo': Wo, 'lambda_q1': lambda_q1, 'lambda_k1': lambda_k1, 'lambda_q2': lambda_q2, 'lambda_k2': lambda_k2, 'gamma': gamma, 'beta': beta}
    _L0_attn_in = _L0_attn_setup()

    def _L0_ffn_setup():
        import jax, jax.numpy as jnp
        import numpy as np
        B, L, D, I, E, K = (2, 512, 256, 1024, 8, 2)
        LN_EPS = 1e-05

        def _layernorm(x, g, b):
            m = jnp.mean(x, axis=-1, keepdims=True)
            v = jnp.mean(jnp.square(x - m), axis=-1, keepdims=True)
            return (x - m) * jax.lax.rsqrt(v + LN_EPS) * g + b
        key = jax.random.key(seed)
        ks = jax.random.split(key, 4)
        return {'hidden_states': jax.random.normal(ks[0], (B, L, D), dtype=jnp.float32), 'rn_g': jnp.ones((D,), jnp.float32), 'rn_b': jnp.zeros((D,), jnp.float32), 'router_w': jax.random.normal(ks[1], (E, D), jnp.float32) * 0.02, 'router_b': jnp.zeros((E,), jnp.float32), 'ln_g': jnp.ones((E, D), jnp.float32), 'ln_b': jnp.zeros((E, D), jnp.float32), 'w1': jax.random.normal(ks[2], (E, D, I), jnp.float32) * 0.02, 'b1': jnp.zeros((E, I), jnp.float32), 'w2': jax.random.normal(ks[3], (E, I, D), jnp.float32) * 0.02, 'b2': jnp.zeros((E, D), jnp.float32)}
    _L0_ffn_in = _L0_ffn_setup()
    _d = {'L0_attn_x': _L0_attn_in['x'], 'L0_attn_Wq': _L0_attn_in['Wq'], 'L0_attn_Wk': _L0_attn_in['Wk'], 'L0_attn_Wv': _L0_attn_in['Wv'], 'L0_attn_Wo': _L0_attn_in['Wo'], 'L0_attn_lambda_q1': _L0_attn_in['lambda_q1'], 'L0_attn_lambda_k1': _L0_attn_in['lambda_k1'], 'L0_attn_lambda_q2': _L0_attn_in['lambda_q2'], 'L0_attn_lambda_k2': _L0_attn_in['lambda_k2'], 'L0_attn_gamma': _L0_attn_in['gamma'], 'L0_attn_beta': _L0_attn_in['beta'], 'L0_ffn_rn_g': _L0_ffn_in['rn_g'], 'L0_ffn_rn_b': _L0_ffn_in['rn_b'], 'L0_ffn_router_w': _L0_ffn_in['router_w'], 'L0_ffn_router_b': _L0_ffn_in['router_b'], 'L0_ffn_ln_g': _L0_ffn_in['ln_g'], 'L0_ffn_ln_b': _L0_ffn_in['ln_b'], 'L0_ffn_w1': _L0_ffn_in['w1'], 'L0_ffn_b1': _L0_ffn_in['b1'], 'L0_ffn_w2': _L0_ffn_in['w2'], 'L0_ffn_b2': _L0_ffn_in['b2']}
    _x0 = _d['L0_attn_x']
    _d['L0_attn_x'] = jax.random.normal(jax.random.fold_in(jax.random.key(seed), 1), (2, 2048, 256), dtype=_x0.dtype)
    del _x0
    return _d

def reference(L0_attn_x, L0_attn_Wq, L0_attn_Wk, L0_attn_Wv, L0_attn_Wo, L0_attn_lambda_q1, L0_attn_lambda_k1, L0_attn_lambda_q2, L0_attn_lambda_k2, L0_attn_gamma, L0_attn_beta, L0_ffn_rn_g, L0_ffn_rn_b, L0_ffn_router_w, L0_ffn_router_b, L0_ffn_ln_g, L0_ffn_ln_b, L0_ffn_w1, L0_ffn_b1, L0_ffn_w2, L0_ffn_b2):

    def _L0_attn_ref(x, Wq, Wk, Wv, Wo, lambda_q1, lambda_k1, lambda_q2, lambda_k2, gamma, beta):
        import jax, jax.numpy as jnp
        import numpy as np
        import math
        DIM = 256
        NUM_HEADS = 16
        HEAD_DIM = DIM // NUM_HEADS
        LAYER_IDX = 12
        LAMBDA_INIT = 0.8 - 0.6 * math.exp(-0.3 * (LAYER_IDX - 1))
        LN_EPS = 1e-05
        B, S, _ = x.shape
        scaling = HEAD_DIM ** (-0.5)
        Q = (x @ Wq).reshape(B, S, NUM_HEADS, 2 * HEAD_DIM).transpose(0, 2, 1, 3)
        K = (x @ Wk).reshape(B, S, NUM_HEADS, 2 * HEAD_DIM).transpose(0, 2, 1, 3)
        V = (x @ Wv).reshape(B, S, NUM_HEADS, HEAD_DIM).transpose(0, 2, 1, 3)
        lamb = jnp.exp(jnp.sum(lambda_q1 * lambda_k1)) - jnp.exp(jnp.sum(lambda_q2 * lambda_k2)) + LAMBDA_INIT
        Q1, Q2 = jnp.split(Q, 2, axis=-1)
        K1, K2 = jnp.split(K, 2, axis=-1)
        A1 = jnp.einsum('bhqd,bhkd->bhqk', Q1, K1) * scaling
        A2 = jnp.einsum('bhqd,bhkd->bhqk', Q2, K2) * scaling
        attn = jax.nn.softmax(A1, axis=-1) - lamb * jax.nn.softmax(A2, axis=-1)
        out = jnp.einsum('bhqk,bhkd->bhqd', attn, V)
        out = out.transpose(0, 2, 1, 3).reshape(B, S, DIM)
        out = out @ Wo
        mu = jnp.mean(out, axis=-1, keepdims=True)
        var = jnp.var(out, axis=-1, keepdims=True)
        out = (out - mu) * jax.lax.rsqrt(var + LN_EPS) * gamma + beta
        return out

    def _L0_ffn_ref(hidden_states, rn_g, rn_b, router_w, router_b, ln_g, ln_b, w1, b1, w2, b2):
        import jax, jax.numpy as jnp
        import numpy as np
        B, L, D, I, E, K = (2, 512, 256, 1024, 8, 2)
        LN_EPS = 1e-05

        def _layernorm(x, g, b):
            m = jnp.mean(x, axis=-1, keepdims=True)
            v = jnp.mean(jnp.square(x - m), axis=-1, keepdims=True)
            return (x - m) * jax.lax.rsqrt(v + LN_EPS) * g + b
        normed = _layernorm(hidden_states, rn_g, rn_b)
        logits = (jnp.einsum('bld,ed->ble', normed, router_w) + router_b).astype(jnp.float32)
        top_w, top_idx = jax.lax.top_k(logits, K)
        top_w = jax.nn.softmax(top_w, axis=-1).astype(hidden_states.dtype)
        onehot = jax.nn.one_hot(top_idx, E, dtype=top_w.dtype)
        combine = jnp.einsum('blke,blk->ble', onehot, top_w)
        out = jnp.zeros_like(hidden_states)
        for e in range(E):
            h = _layernorm(hidden_states, ln_g[e], ln_b[e])
            h = jax.nn.gelu(jnp.einsum('bld,di->bli', h, w1[e]) + b1[e], approximate=False)
            h = jnp.einsum('bli,id->bld', h, w2[e]) + b2[e]
            out = out + combine[..., e:e + 1] * h
        return out
    x = L0_attn_x
    x = _layernorm(x + _L0_attn_ref(x, L0_attn_Wq, L0_attn_Wk, L0_attn_Wv, L0_attn_Wo, L0_attn_lambda_q1, L0_attn_lambda_k1, L0_attn_lambda_q2, L0_attn_lambda_k2, L0_attn_gamma, L0_attn_beta), axis=-1)
    x = _layernorm(x + _L0_ffn_ref(x, L0_ffn_rn_g, L0_ffn_rn_b, L0_ffn_router_w, L0_ffn_router_b, L0_ffn_ln_g, L0_ffn_ln_b, L0_ffn_w1, L0_ffn_b1, L0_ffn_w2, L0_ffn_b2), axis=-1)
    return x

_drawn_inputs = setup_inputs


def setup_inputs(seed=0):
    import zlib

    import numpy as np

    out = dict(_drawn_inputs(seed))
    spreads = {'L0_attn_gamma': (1.0, 0.2),
     'L0_attn_beta': (0.0, 0.1),
     'L0_ffn_rn_g': (1.0, 0.2),
     'L0_ffn_rn_b': (0.0, 0.1),
     'L0_ffn_router_b': (0.0, 0.1),
     'L0_ffn_ln_g': (1.0, 0.6),
     'L0_ffn_ln_b': (0.0, 0.8),
     'L0_ffn_b1': (0.0, 0.304),
     'L0_ffn_b2': (0.0, 0.1)}
    factors = {'L0_attn_lambda_q1': 6.448, 'L0_attn_lambda_q2': 4.54, 'L0_attn_lambda_k2': 3.248}
    for name, (base, spread) in spreads.items():
        noise = np.random.default_rng([zlib.crc32(name.encode()), seed]).standard_normal(out[name].shape)
        drawn = base * np.exp(spread * noise) if base else spread * noise
        out[name] = jnp.asarray(drawn.astype(out[name].dtype))
    for name, factor in factors.items():
        out[name] = (out[name] * factor).astype(out[name].dtype)
    return out
```

```python
import math
from contextlib import ExitStack

import concourse.bass as bass
from concourse import mybir

ALU = mybir.AluOpType
ACT = mybir.ActivationFunctionType
AX = mybir.AxisListType
F32 = mybir.dt.float32
BF16 = mybir.dt.bfloat16

P = 128
TC = 512
TPC = TC // P
EPS = 1e-5
HD = 16
UNITS = 4
GF = UNITS * HD
LAMBDA_INIT = 0.8 - 0.6 * math.exp(-0.3 * 11)
Q_PARTS = (0, 0, 0, 1, 1, 2)
K_PARTS = (0, 1, 2, 0, 1, 0)
KR = 16 * len(Q_PARTS)
KM = KR + 3


def diff_attention_moe(nc, x, Wq, Wk, Wv, Wo, lq1, lk1, lq2, lk2, gamma, beta, rn_g, rn_b,
                       router_w, router_b, ln_g, ln_b, w1, b1, w2, b2, out):
    NB, S, D = x.shape
    T = NB * S
    KD = D // P
    E, _, I = w1.shape
    IC = I // P
    G = D // HD // 2
    CH = S // TC
    KB = S // P
    NT = T // P
    NCH = T // TC
    assert D == 256 and S == 2048 and E == 8 and I == 1024 and KB == 16 and CH == 4

    qd = nc.dram_tensor("q_parts", (NB * G, 3, CH, HD * UNITS, TC), BF16, kind="Internal").ap()
    kd = nc.dram_tensor("k_parts", (NB * G, 3, HD * UNITS, S), BF16, kind="Internal").ap()
    vd = nc.dram_tensor("v_groups", (NB * G, P, KB, 64), F32, kind="Internal").ap()
    od = nc.dram_tensor("attended", (NB * G, P, S), F32, kind="Internal").ap()
    x1d = nc.dram_tensor("x1", (T, D), F32, kind="Internal").ap()
    xhd = nc.dram_tensor("xh", (T, D), F32, kind="Internal").ap()
    lgd = nc.dram_tensor("logits", (P, NT, E), F32, kind="Internal").ap()

    TS = 512
    NTL = -(-(2 * T // TS + E - 1) // 2) * 2
    xgd = nc.dram_tensor("slot_rows", (NTL * TS, D), F32, kind="Internal").ap()
    ygd = nc.dram_tensor("slot_results", (NTL * TS, D), F32, kind="Internal").ap()
    cold = nc.dram_tensor("expert_columns", (E, P, IC + 2 * KD), F32, kind="Internal").ap()
    expd = nc.dram_tensor("tile_owners", (1, NTL), mybir.dt.int32, kind="Internal").ap()

    with ExitStack() as top:
        ident = top.enter_context(nc.sbuf_tensor("ident", [P, P], F32))
        identb = top.enter_context(nc.sbuf_tensor("identb", [P, P], BF16))

        stage_project(nc, locals())
        stage_attend(nc, locals())
        stage_join(nc, locals())
        slot = [top.enter_context(nc.sbuf_tensor(f"slot{r}", [P, NT], mybir.dt.int32)) for r in range(2)]
        share = [top.enter_context(nc.sbuf_tensor(f"share{r}", [P, NT], F32)) for r in range(2)]
        stage_route(nc, locals())
        stage_scatter(nc, locals())
        stage_experts(nc, locals())
        stage_finish(nc, locals())


def opener(nc, ctx):
    return (lambda n, s, d: ctx.enter_context(nc.sbuf_tensor(n, s, d)),
            lambda n, s, d: ctx.enter_context(nc.psum_tensor(n, s, d)),
            lambda n: ctx.enter_context(nc.semaphore(n)))


def stage_project(nc, a):
    x, Wq, Wk, Wv, qd, kd, vd = (a[n] for n in ("x", "Wq", "Wk", "Wv", "qd", "kd", "vd"))
    NB, CH, KD, G, D, ident, identb = (a[n] for n in ("NB", "CH", "KD", "G", "D", "ident", "identb"))
    MC = 2 * D // P
    ITEMS = 2 * MC
    with ExitStack() as ctx:
        sb, ps, sem = opener(nc, ctx)
        wraw = sb("wraw", [P, KD, 2, 2 * D], F32)
        wqk = sb("wqk", [P, KD, 2, 2 * D], F32)
        wv = sb("wv", [P, KD, D], F32)
        xs = sb("xs", [P, TPC, D], F32)
        xT = sb("xT", [P, KD, TC], F32)
        parts = sb("parts", [P, 4, 3, TC], BF16)
        rest = sb("rest", [P, 4, TC], F32)
        vst = sb("vst", [P, G, TPC, 2, 32], F32)
        pxT = [ps(f"pxT{i}", [P, TC], F32) for i in range(KD)]
        pj = [ps(f"pj{i}", [P, TC], F32) for i in range(4)]
        pv = [ps(f"pv{i}", [P, 2, D], F32) for i in range(2)]
        names = ("w_loaded", "zeroed", "ident_ready", "identb_ready", "wqk_ready", "vst_preset", "x_loaded",
                 "x_turned", "xT_ready", "proj_ready", "hi_ready", "rest_ready", "mid_ready", "lo_ready",
                 "v_ready", "vst_ready", "v_stored")
        (w_loaded, zeroed, ident_ready, identb_ready, wqk_ready, vst_preset, x_loaded, x_turned, xT_ready,
         proj_ready, hi_ready, rest_ready, mid_ready, lo_ready, v_ready, vst_ready,
         v_stored) = (sem(n) for n in names)
        parts_stored = [sem(f"parts_stored{i}") for i in range(4)]
        gate_pool = sem("gate_pool")
        block = ctx.enter_context(nc.Block())

        @block.sync
        def _(sp):
            for s in (x_turned, xT_ready, v_stored, v_ready, vst_ready, rest_ready, lo_ready,
                      *parts_stored):
                sp.sem_inc(s, 1)
            sp.dma_start(wraw[:, :, 0, :], Wq.rearrange("(k p) f -> p k f", p=P)).then_inc(w_loaded, 16)
            sp.dma_start(wraw[:, :, 1, :], Wk.rearrange("(k p) f -> p k f", p=P)).then_inc(w_loaded, 16)
            sp.dma_start(wv[:], Wv.rearrange("(k p) f -> p k f", p=P)).then_inc(w_loaded, 16)
            with sp.Fori(0, NB) as b:
                with sp.Fori(0, CH) as c:
                    n = b * CH + c
                    sp.wait_ge(x_turned, n + 1)
                    sp.dma_start(xs[:], x.rearrange("b (c j p) d -> b c p j d", j=TPC, p=P)[b, c]).then_inc(x_loaded, 16)
                    for i in range(ITEMS):
                        sp.wait_ge(lo_ready, n * ITEMS + i + 2)
                        if i < MC:
                            dst = qd.rearrange("(b g) s c r t -> b c g r s t", b=NB)
                        else:
                            dst = kd.rearrange("(b g) s r (c t) -> b c g r s t", b=NB, c=CH)
                        for h in range(2):
                            g = 2 * (i % MC) + h
                            sp.dma_start(
                                dst[b, c, g], parts[64 * h:64 * h + 64, i % 4, :, :]).then_inc(parts_stored[i % 4], 16)
                    sp.wait_ge(vst_ready, 4 * (n + 1) + 1)
                    sp.dma_start(vd.rearrange("(b g) p (c k) f -> b c p g (k f)", b=NB, c=CH)[b, c],
                                 vst[:].rearrange("p g k h f -> p g (k h f)")).then_inc(v_stored, 16)
            for stored in parts_stored:
                sp.wait_ge(stored, 32 * NB * CH * (ITEMS // 4) + 1)
            sp.wait_ge(v_stored, 16 * NB * CH + 1)

        @block.gpsimd
        def _(pool):
            nc.gpsimd.memset(ident[:], 0.0).then_inc(zeroed, 1)
            nc.gpsimd.memset(vst[:], 0.0).then_inc(zeroed, 1)
            pool.wait_ge(zeroed, 2)
            nc.gpsimd.affine_select(out=ident[:], in_=ident[:], compare_op=ALU.not_equal, fill=1.0, base=0,
                                    pattern=[[-1, P]], channel_multiplier=1).then_inc(ident_ready, 1)
            nc.gpsimd.memset(vst[:, :, :, :, HD:HD + 1], 1.0).then_inc(vst_preset, 1)
            pool.wait_ge(ident_ready, 1)
            nc.gpsimd.tensor_copy(identb[:], ident[:]).then_inc(identb_ready, 1)
            with pool.Fori(0, NB * CH) as n:
                for i in range(ITEMS):
                    pool.wait_ge(rest_ready, n * ITEMS + i + 2)
                    pool.sem_inc(gate_pool, 1)
                    nc.gpsimd.tensor_copy(parts[:, i % 4, 1, :], rest[:, i % 4, :]).then_inc(mid_ready, 1)

        @block.scalar
        def _(act):
            with act.Fori(0, NB * CH) as n:
                act.wait_ge(x_turned, n + 2)
                act.wait_ge(v_ready, 2 * n + 1)
                for k in range(KD):
                    nc.scalar.copy(xT[:, k, :], pxT[k][:]).then_inc(xT_ready, 1)
                for i in range(ITEMS):
                    act.wait_ge(proj_ready, n * ITEMS + i + 1)
                    act.wait_ge(parts_stored[i % 4], 32 * (n * (ITEMS // 4) + i // 4) + 1)
                    nc.scalar.copy(parts[:, i % 4, 0, :], pj[i % 4][:]).then_inc(hi_ready, 1)
                act.wait_ge(v_stored, 16 * n + 1)
                act.wait_ge(vst_preset, 1)
                for j in range(TPC):
                    act.wait_ge(v_ready, 2 * n + j // 2 + 2)
                    nc.scalar.copy(vst[:, :, j, :, 0:HD],
                                   pv[j // 2][:, j % 2, :].rearrange("p (g h d) -> p g h d", h=2, d=HD)
                                   ).then_inc(vst_ready, 1)

        @block.tensor
        def _(pe):
            pe.wait_ge(ident_ready, 1)
            pe.wait_ge(wqk_ready, 2 * KD)
            with pe.Fori(0, NB * CH) as n:
                pe.wait_ge(x_loaded, 16 * (n + 1))
                pe.wait_ge(xT_ready, KD * n + 1)
                for k in range(KD):
                    for j in range(TPC):
                        mm = nc.tensor.transpose(pxT[k][:, j * P:(j + 1) * P], xs[:, j, k * P:(k + 1) * P], ident[:])
                mm.then_inc(x_turned, 1)
                pe.wait_ge(xT_ready, KD * (n + 1) + 1)
                for i in range(ITEMS):
                    pe.wait_ge(rest_ready, n * ITEMS + max(i - 3, 0) + 1)
                    for k in range(KD):
                        mm = nc.tensor.matmul(pj[i % 4][:], wqk[:, k, i // MC, (i % MC) * P:(i % MC + 1) * P],
                                              xT[:, k, :], start=(k == 0), stop=(k == KD - 1))
                    mm.then_inc(proj_ready, 1)
                pe.wait_ge(vst_ready, TPC * n + 1)
                for j in range(TPC):
                    for k in range(KD):
                        mm = nc.tensor.matmul(pv[j // 2][:, j % 2, :], xT[:, k, j * P:(j + 1) * P], wv[:, k, :],
                                              start=(k == 0), stop=(k == KD - 1), skip_group_check=True)
                    if j % 2 == 1:
                        mm.then_inc(v_ready, 1)

        @block.vector
        def _(dve):
            dve.wait_ge(w_loaded, 48)
            for k in range(KD):
                for m in range(2):
                    nc.vector.tensor_copy(
                        wqk[:, k, m, :].rearrange("p (g d u) -> p g d u", d=HD, u=UNITS),
                        wraw[:, k, m, :].rearrange("p (g u d) -> p g d u", d=HD, u=UNITS)).then_inc(wqk_ready, 1)
            with dve.Fori(0, NB * CH) as n:
                for i in range(ITEMS + 1):
                    if i < ITEMS:
                        dve.wait_ge(lo_ready, n * ITEMS + max(i - 3, 0) + 1)
                        dve.wait_ge(hi_ready, n * ITEMS + i + 1)
                        nc.vector.tensor_tensor(rest[:, i % 4, :], pj[i % 4][:], parts[:, i % 4, 0, :],
                                                ALU.subtract).then_inc(rest_ready, 1)
                    if i > 0:
                        j = i - 1
                        dve.wait_ge(mid_ready, n * ITEMS + j + 1)
                        nc.vector.tensor_tensor(parts[:, j % 4, 2, :], rest[:, j % 4, :], parts[:, j % 4, 1, :],
                                                ALU.subtract).then_inc(lo_ready, 1)


def stage_attend(nc, a):
    qd, kd, vd, od = (a[n] for n in ("qd", "kd", "vd", "od"))
    NB, CH, G, KB, S, identb = (a[n] for n in ("NB", "CH", "G", "KB", "S", "identb"))
    PAIRS = NB * G // 2
    RC = 2 * CH
    RS = RC * KB
    AHEAD = 2
    SH = S // 2
    with ExitStack() as ctx:
        sb, ps, sem = opener(nc, ctx)
        Q = [sb(f"Q{i}", [KM, CH, UNITS, TC], BF16) for i in range(2)]
        K = [sb(f"K{i}", [KM, UNITS, S], BF16) for i in range(2)]
        V = [sb(f"V{i}", [P, KB, 2, 32], F32) for i in range(2)]
        probs = sb("probs", [P, 2 * UNITS, TC], F32)
        att = [sb(f"att{i}", [P, TC], F32) for i in range(2)]
        half_max = [sb(f"half_max{i}", [P, 2, 16], F32) for i in range(2)]
        row_max = sb("row_max", [P, 16], F32)
        max_rest = sb("max_rest", [P, 16], F32)
        max_parts = sb("max_parts", [P, 3, 16], BF16)
        max_rows = [sb(f"max_rows{i}", [48, P], BF16) for i in range(2)]
        scores = ps("scores", [P, S], F32)
        scoresT = [ps(f"scoresT{i}", [P, TC], F32) for i in range(3)]
        attT = ps("attT", [P, TC], F32)
        names = ("ones_set", "first_max", "parts_chain", "max_parts_ready", "max_rows_turned", "max_rows_copied",
                 "scoresA_ready", "scoresB_ready", "maxA_done", "maxB_done", "scoresT_ready", "exp_done",
                 "pv_done", "att_copied")
        (ones_set, first_max, parts_chain, max_parts_ready, max_rows_turned, max_rows_copied,
         scoresA_ready, scoresB_ready, maxA_done, maxB_done, scoresT_ready, exp_done,
         pv_done, att_copied) = (sem(n) for n in names)
        qk_loaded = [sem(f"qk_loaded{i}") for i in range(2)]
        v_loaded = [sem(f"v_loaded{i}") for i in range(2)]
        max_loaded = [sem(f"max_loaded{i}") for i in range(2)]
        att_stored = [sem(f"att_stored{i}") for i in range(2)]
        gate_pe, zeros_set, zeroed = sem("gate_pe"), sem("zeros_set"), sem("slots_zeroed")
        xgd, TS, NTL, D = (a[n] for n in ("xgd", "TS", "NTL", "D"))
        zeros = sb("zeros", [P, TS // P * D], F32)
        QKD = 16 * 2 * len(Q_PARTS)
        MXD = 16 * 3
        turned = scores[0:48, 0:P // 2].bitcast(BF16)
        block = ctx.enter_context(nc.Block())

        @block.sync
        def _(sp):
            for s in (pv_done, att_copied, maxA_done, maxB_done, *max_loaded, *att_stored):
                sp.sem_inc(s, 1)
            def load_qk(p, g):
                for i in range(len(Q_PARTS)):
                    sp.dma_start(Q[p][16 * i:16 * i + 16].rearrange("d c u t -> d c (u t)"),
                                 qd.rearrange("g s c (d u) t -> g s d c (u t)", u=UNITS)[g, Q_PARTS[i]]
                                 ).then_inc(qk_loaded[p], 16)
                    sp.dma_start(K[p][16 * i:16 * i + 16],
                                 kd.rearrange("g s (d u) t -> g s d u t", u=UNITS)[g, K_PARTS[i]]
                                 ).then_inc(qk_loaded[p], 16)

            def load_v(p, g):
                sp.dma_start(V[p][:], vd.rearrange("g p k (h f) -> g p k h f", h=2)[g]).then_inc(v_loaded[p], 16)

            def load_max(done, lc):
                p, c = lc // CH % 2, lc % CH
                sp.wait_ge(max_rows_copied, done)
                for s in range(3):
                    sp.dma_start(Q[p][KR + s:KR + s + 1, c, :, :].rearrange("o u (t q) -> o (u t) q", q=P),
                                 max_rows[lc % 2][16 * s:16 * s + 16, :]
                                 ).then_inc(max_loaded[lc % 2], 16)

            load_qk(0, 0)
            load_v(0, 0)
            load_max(1, 0)
            with sp.Fori(0, PAIRS) as it:
                def store_att(lc):
                    sp.wait_ge(att_copied, it * RC + lc + 2)
                    sp.dma_start(od.rearrange("(i p) r (c t) -> i p c r t", p=2, c=CH)[it, lc // CH, lc % CH],
                                 att[lc % 2][:]).then_inc(att_stored[lc % 2], 16)

                sp.wait_ge(pv_done, it * RS + 1)
                load_qk(1, it * 2 + 1)
                load_v(1, it * 2 + 1)
                for lc in range(RC):
                    if lc > 0:
                        store_att(lc - 1)
                    if lc == CH:
                        load_qk(0, (it * 2 + 2) % (NB * G))
                        load_v(0, (it * 2 + 2) % (NB * G))
                    load_max(it * RC + lc + 2, lc + 1)
                store_att(RC - 1)
            for p in range(2):
                sp.wait_ge(att_stored[p], 16 * PAIRS * CH + 1)
                sp.wait_ge(v_loaded[p], 16 * (PAIRS + (p == 0)))
                sp.wait_ge(max_loaded[p], MXD * (PAIRS * CH + (p == 0)) + 1)

        @block.gpsimd
        def _(pool):
            for i in range(2):
                nc.gpsimd.memset(K[i][KR:KM], 1.0).then_inc(ones_set, 1)
            pool.wait_ge(ones_set, 2)
            nc.gpsimd.memset(zeros[:], 0.0).then_inc(zeros_set, 1)
            pool.wait_ge(zeros_set, 1)
            with pool.Fori(0, NTL) as n:
                pool.dma_start(xgd.rearrange("(n p j) d -> n p (j d)", n=NTL, p=P)[n], zeros[:]).then_inc(zeroed, 16)
            pool.wait_ge(zeroed, 16 * NTL)

        @block.tensor
        def _(pe):
            def score_rows(item, lc, i):
                p, c, u, t = lc // CH % 2, lc % CH, i // 4, i % 4
                lhsT = Q[p][0:KR, c, u, t * P:(t + 1) * P]
                for h, ready, used in ((0, scoresA_ready, maxA_done), (1, scoresB_ready, maxB_done)):
                    pe.wait_ge(used, item + 1)
                    for k in range(2):
                        at = h * SH + k * TC
                        mm = nc.tensor.matmul(scores[:, at:at + TC], lhsT, K[p][0:KR, u, at:at + TC],
                                              start=True, stop=True)
                    mm.then_inc(ready, 1)

            def turn_maxima(done, item):
                pe.wait_ge(max_parts_ready, done)
                pe.wait_ge(maxA_done, item + 1)
                pe.sem_inc(gate_pe, 1)
                nc.tensor.transpose(turned, max_parts[:].rearrange("p s i -> p (s i)"), identb[:]
                                    ).then_inc(max_rows_turned, 1)
                pe.wait_ge(max_rows_copied, done)

            pe.wait_ge(ones_set, 2)
            pe.wait_ge(qk_loaded[0], QKD)
            for lc in range(AHEAD):
                for i in range(16):
                    score_rows(lc * 16 + i, lc, i)
            turn_maxima(1, 32)
            with pe.Fori(0, PAIRS) as it:
                for lc in range(RC):
                    p, c = lc // CH, lc % CH
                    for kb in range(KB):
                        ls = lc * KB + kb
                        item = it * RS + ls + AHEAD * 16
                        if kb == 0:
                            pe.wait_ge(max_loaded[lc % 2], MXD * (it * CH + lc // 2 + 1) + 1)
                            if lc == CH - AHEAD:
                                pe.wait_ge(qk_loaded[1], QKD * (it + 1))
                            if lc == 2 * CH - AHEAD:
                                pe.wait_ge(qk_loaded[0], QKD * (it + 2))
                            if c == 0:
                                pe.wait_ge(v_loaded[p], 16 * (it + 1))
                        if kb == 2:
                            turn_maxima(it * RC + lc + 2, item)

                        def scores_of(u):
                            i = 4 * ls + u
                            if i >= 3:
                                pe.wait_ge(exp_done, it * 4 * RS + i - 2)
                            nc.tensor.matmul(scoresT[i % 3][:], K[p][:, u, kb * P:(kb + 1) * P], Q[p][:, c, u, :],
                                             start=True, stop=True).then_inc(scoresT_ready, 1)

                        def weigh(s):
                            wp, wk = s // KB // CH, s % KB
                            pe.wait_ge(exp_done, it * 4 * RS + 4 * s + 4)
                            if wk == 0:
                                pe.wait_ge(att_copied, it * RC + s // KB + 1)
                            for u in range(UNITS):
                                mm = nc.tensor.matmul(attT[32 * u:32 * u + 32, :], V[wp][:, wk, u // 2, :],
                                                      probs[:, 4 * (s % 2) + u, :],
                                                      start=(wk == 0), stop=(wk == KB - 1), skip_group_check=True)
                            mm.then_inc(pv_done, 1)

                        for u in range(3):
                            scores_of(u)
                        score_rows(item, (lc + AHEAD) % RC, kb)
                        scores_of(3)
                        if ls > 0:
                            weigh(ls - 1)
                weigh(RS - 1)

        @block.scalar
        def _(act):
            with act.Fori(0, PAIRS) as it:
                for ls in range(RS):
                    act.wait_ge(pv_done, it * RS + max(ls - 1, 0) + 1)
                    for u in range(UNITS):
                        i = 4 * ls + u
                        act.wait_ge(scoresT_ready, it * 4 * RS + i + 1)
                        nc.scalar.activation(probs[:, i % 8, :], scoresT[i % 3][:], ACT.Exp,
                                             scale=HD ** -0.5).then_inc(exp_done, 1)

        @block.vector
        def _(dve):
            def maxima(item, lc, i):
                for h, ready, done in ((0, scoresA_ready, maxA_done), (1, scoresB_ready, maxB_done)):
                    dve.wait_ge(ready, item + 1)
                    nc.vector.tensor_reduce(half_max[lc % 2][:, h, i:i + 1], scores[:, h * SH:(h + 1) * SH],
                                            AX.X, ALU.max).then_inc(done, 1)

            def cut_maxima(done, lc):
                hm, chain = half_max[lc % 2], 4 * (done - 1)
                nc.vector.tensor_tensor(row_max[:], hm[:, 0, :], hm[:, 1, :], ALU.max).then_inc(parts_chain, 1)
                dve.wait_ge(parts_chain, chain + 1)
                nc.vector.tensor_scalar(max_parts[:, 0, :], row_max[:], -1.0, None, ALU.mult).then_inc(parts_chain, 1)
                dve.wait_ge(parts_chain, chain + 2)
                nc.vector.scalar_tensor_tensor(max_rest[:], row_max[:], -1.0, max_parts[:, 0, :],
                                               ALU.mult, ALU.subtract).then_inc(parts_chain, 1)
                dve.wait_ge(parts_chain, chain + 3)
                nc.vector.tensor_copy(max_parts[:, 1, :], max_rest[:]).then_inc(parts_chain, 1)
                dve.wait_ge(parts_chain, chain + 4)
                nc.vector.tensor_tensor(max_parts[:, 2, :], max_rest[:], max_parts[:, 1, :],
                                        ALU.subtract).then_inc(max_parts_ready, 1)

            def copy_rows(done, lc, loaded):
                dve.wait_ge(max_rows_turned, done)
                dve.wait_ge(max_loaded[lc % 2], loaded + 1)
                nc.vector.tensor_copy(max_rows[lc % 2][:], turned).then_inc(max_rows_copied, 1)

            for lc in range(AHEAD):
                for i in range(16):
                    maxima(lc * 16 + i, lc, i)
            dve.wait_ge(maxA_done, 32 + 1)
            dve.wait_ge(maxB_done, 32 + 1)
            cut_maxima(1, 0)
            copy_rows(1, 0, 0)
            with dve.Fori(0, PAIRS) as it:
                def copy_att(lc):
                    dve.wait_ge(pv_done, it * RS + (lc + 1) * KB + 1)
                    dve.wait_ge(att_stored[lc % 2], 16 * (it * CH + lc // 2) + 1)
                    nc.vector.tensor_copy(att[lc % 2][:], attT[:]).then_inc(att_copied, 1)

                for lc in range(RC):
                    for kb in range(KB):
                        item = it * RS + lc * KB + kb + AHEAD * 16
                        if kb == 0:
                            dve.wait_ge(maxA_done, item + 1)
                            dve.wait_ge(maxB_done, item + 1)
                            cut_maxima(it * RC + lc + 2, lc + 1)
                        if kb == 1 and lc > 0:
                            copy_att(lc - 1)
                        if kb == 2:
                            copy_rows(it * RC + lc + 2, lc + 1, MXD * (it * CH + (lc + 1) // 2))
                        maxima(item, lc + AHEAD, kb)
                copy_att(RC - 1)


class Chain:

    def __init__(self, eng, sem, base=0):
        self.eng, self.sem, self.base, self.n = eng, sem, base, 0

    def add(self, ins):
        ins.then_inc(self.sem, 1)
        self.n += 1

    def wait(self):
        self.eng.wait_ge(self.sem, self.base + self.n)


def stage_join(nc, a):
    x, Wo, od, x1d, xhd, lgd = (a[n] for n in ("x", "Wo", "od", "x1d", "xhd", "lgd"))
    lams = [a[n] for n in ("lq1", "lk1", "lq2", "lk2")]
    gamma, beta, rn_g, rn_b, router_w, router_b = (a[n] for n in ("gamma", "beta", "rn_g", "rn_b", "router_w", "router_b"))
    NB, CH, KD, G, D, E, ident = (a[n] for n in ("NB", "CH", "KD", "G", "D", "E", "ident"))
    NU = G * UNITS
    NL = 4 + 1 + 3 + 4
    with ExitStack() as ctx:
        sb, ps, sem = opener(nc, ctx)
        wo = sb("wo", [P, KD, D], F32)
        lam_in = sb("lam_in", [P, 4, HD], F32)
        lam_mul = sb("lam_mul", [P, 2, HD], F32)
        lam_sum = sb("lam_sum", [P, 2], F32)
        lam_exp = sb("lam_exp", [P, 2], F32)
        lam_neg = sb("lam_neg", [P, 1], F32)
        coef = sb("coef", [P, NU], F32)
        gam = sb("gam", [P, D], F32)
        bet = sb("bet", [P, D], F32)
        rnb = sb("rnb", [P, D], F32)
        rw_all = sb("rw_all", [P, E, D], F32)
        rbias = sb("rbias", [P, E], F32)
        rbias_in = sb("rbias_in", [P, E], F32)
        rw_rows = sb("rw_rows", [E, D], F32)
        rg_rows = sb("rg_rows", [E, D], F32)
        rw_T = sb("rw_T", [P, KD, E], F32)
        xs = sb("join_x", [P, TPC, D], F32)
        xb = sb("join_xb", [P, TPC, D], F32)
        heads = sb("heads", [P, G, TC], F32)
        rcp = sb("rcp", [P, TPC, NU], F32)
        rcc = sb("rcc", [P, TPC, NU], F32)
        scaled = sb("scaled", [P, 2, NU, HD], F32)
        att = sb("join_att", [P, TPC, D], F32)
        attT = sb("join_attT", [P, TPC, D], F32)
        z = sb("z", [P, TPC, D], F32)
        zg = sb("zg", [P, TPC, D], F32)
        zs = sb("zs", [P, TPC, D], F32)
        x1 = sb("x1s", [P, TPC, D], F32)
        xh = sb("join_xh", [P, TPC, D], F32)
        xhT = sb("join_xhT", [P, KD, TC], F32)
        lgs = sb("lgs", [P, TPC, E], F32)
        st = [sb(f"st{i}", [P, TPC, 6], F32) for i in range(3)]
        mv = [sb(f"mv{i}", [P, TPC, 2], F32) for i in range(3)]
        rs = [sb(f"rs{i}", [P, TPC], F32) for i in range(3)]
        ve = [sb(f"ve{i}", [P, TPC], F32) for i in range(3)]
        minus_half = sb("minus_half", [P, TPC], F32)
        token_major = [ps(f"token_major{i}", [P, NU, 32], F32) for i in range(2)]
        turn = [ps(f"turn{i}", [P, TC], F32) for i in range(2)]
        prod = [ps(f"prod{i}", [P, TC], F32) for i in range(2)]
        names = ("consts_loaded", "setup_chain", "coef_ones", "lam_summed", "lam_exped", "coef_ready", "rw_scaled",
                 "rw_turned", "rw_ready", "rbias_ready", "in_loaded", "x_used", "turned", "scaled_ready", "att_ready",
                 "att_turned", "attT_ready", "y_ready", "z_ready", "pool_chain", "zs_ready", "ln_chain", "x1_ready",
                 "xh_ready", "xh_turned", "xhT_ready", "logits_ready", "lgs_ready", "out_stored")
        (consts_loaded, setup_chain, coef_ones, lam_summed, lam_exped, coef_ready, rw_scaled, rw_turned, rw_ready,
         rbias_ready, in_loaded, x_used, turned, scaled_ready, att_ready, att_turned, attT_ready, y_ready, z_ready,
         pool_chain, zs_ready, ln_chain, x1_ready, xh_ready, xh_turned, xhT_ready, logits_ready, lgs_ready,
         out_stored) = (sem("j_" + n) for n in names)
        half_set, j_gate_pool, j_gate_dve = sem("j_half_set"), sem("j_gate_pool"), sem("j_gate_dve")
        var_ready, ve_ready, rs_ready = ([sem(f"j_{n}{i}") for i in range(3)] for n in ("var", "ve", "rs"))
        NC = NB * CH
        block = ctx.enter_context(nc.Block())

        @block.sync
        def _(sp):
            for s in (turned, x_used, scaled_ready, zs_ready, att_ready, attT_ready, z_ready,
                      lgs_ready, xhT_ready, out_stored, logits_ready):
                sp.sem_inc(s, 1)
            def row(v, n, parts=P):
                return v.rearrange("(o d) -> o d", o=1).to_broadcast((parts, n))
            consts = [(wo[:], Wo.rearrange("(k p) f -> p k f", p=P)), (rw_rows[:], router_w),
                      (gam[:], row(gamma, D)), (bet[:], row(beta, D)), (rnb[:], row(rn_b, D)),
                      (rbias_in[:], row(router_b, E)), (rg_rows[:], row(rn_g, D, E)),
                      (rw_all[:].rearrange("p e d -> p (e d)"),
                       router_w.rearrange("(o e) d -> o (e d)", o=1).to_broadcast((P, E * D)))]
            consts += [(lam_in[:, i, :], row(l, HD)) for i, l in enumerate(lams)]
            assert len(consts) == NL
            for dst, src in consts:
                sp.dma_start(dst, src).then_inc(consts_loaded, 16)
            with sp.Fori(0, NB) as b:
                with sp.Fori(0, CH) as c:
                    n = b * CH + c
                    sp.wait_ge(turned, TPC * n + 1)
                    sp.wait_ge(x_used, TPC * n + 1)
                    sp.dma_start(heads[:], od.rearrange("(b g) p (c t) -> b c p g t", b=NB, c=CH)[b, c]
                                 ).then_inc(in_loaded, 16)
                    sp.dma_start(xs[:], x.rearrange("b (c j p) d -> b c p j d", j=TPC, p=P)[b, c]
                                 ).then_inc(in_loaded, 16)
                    sp.wait_ge(x1_ready, TPC * (n + 1))
                    sp.dma_start(x1d.rearrange("(b c j p) d -> b c p j d", b=NB, j=TPC, p=P)[b, c], x1[:]
                                 ).then_inc(out_stored, 16)
                    sp.wait_ge(xh_ready, TPC * (n + 1))
                    sp.dma_start(xhd.rearrange("(b c j p) d -> b c p j d", b=NB, j=TPC, p=P)[b, c], xh[:]
                                 ).then_inc(out_stored, 16)
                    sp.wait_ge(lgs_ready, TPC * (n + 1) + 1)
                    sp.dma_start(lgd.rearrange("p (b c j) e -> b c p j e", b=NB, c=CH)[b, c], lgs[:]
                                 ).then_inc(out_stored, 16)
            sp.wait_ge(out_stored, 48 * NC + 1)

        @block.gpsimd
        def _(pool):
            nc.gpsimd.memset(coef[:], 1.0).then_inc(coef_ones, 1)
            nc.gpsimd.memset(minus_half[:], -0.5).then_inc(half_set, 1)
            pool.wait_ge(half_set, 1)
            pool.wait_ge(consts_loaded, 16 * NL)
            with pool.Fori(0, NC) as n:
                chain = Chain(pool, pool_chain, n * TPC)
                pool.wait_ge(in_loaded, 32 * (n + 1))
                pool.wait_ge(zs_ready, TPC * n + 1)
                for j in range(TPC):
                    nc.gpsimd.tensor_tensor(xb[:, j, :], xs[:, j, :], bet[:], ALU.add).then_inc(x_used, 1)
                for j in range(TPC):
                    pool.wait_ge(scaled_ready, TPC * n + j + 2)
                    s = scaled[:, j % 2].rearrange("p (h c) d -> p h c d", c=2)
                    nc.gpsimd.tensor_tensor(att[:, j, :].rearrange("p (h d) -> p h d", d=HD), s[:, :, 0, :],
                                            s[:, :, 1, :], ALU.add).then_inc(att_ready, 1)
                def rsqrt(i, tiles):
                    pool.wait_ge(var_ready[i], TPC * n + tiles.stop)
                    pool.sem_inc(j_gate_pool, 1)
                    nc.gpsimd.tensor_scalar(ve[i][:, tiles.start:tiles.stop], mv[i][:, tiles.start:tiles.stop, 1],
                                            EPS, None, ALU.add).then_inc(ve_ready[i], 1)
                    pool.wait_ge(ve_ready[i], TPC // len(tiles) * n + tiles.stop // len(tiles))
                    nc.gpsimd.tensor_tensor(rs[i][:, tiles.start:tiles.stop], ve[i][:, tiles.start:tiles.stop],
                                            minus_half[:, tiles.start:tiles.stop], ALU.pow).then_inc(rs_ready[i], 1)

                for j in range(TPC):
                    if j % 2 == 0:
                        rsqrt(0, range(j, j + 2))
                    pool.wait_ge(z_ready, TPC * n + j + 2)
                    chain.add(nc.gpsimd.tensor_tensor(zg[:, j, :], z[:, j, :], gam[:], ALU.mult))
                    chain.wait()
                    pool.wait_ge(x_used, TPC * n + j + 2)
                    nc.gpsimd.tensor_tensor(zs[:, j, :], zg[:, j, :], xb[:, j, :], ALU.add).then_inc(zs_ready, 1)
                for i in (1, 2):
                    rsqrt(i, range(TPC))

        @block.scalar
        def _(act):
            act.wait_ge(lam_summed, 1)
            nc.scalar.activation(lam_exp[:], lam_sum[:], ACT.Exp).then_inc(lam_exped, 1)
            with act.Fori(0, NC) as n:
                for j in range(TPC):
                    act.wait_ge(att_turned, TPC * n + j + 1)
                    nc.scalar.copy(attT[:, j, :], turn[j % 2][:, 0:D]).then_inc(attT_ready, 1)
                act.wait_ge(out_stored, 48 * n + 1)
                act.wait_ge(logits_ready, TPC * n + 1)
                for j in range(TPC):
                    act.wait_ge(xh_turned, TPC * n + j + 1)
                    nc.scalar.copy(xhT[:, :, j * P:(j + 1) * P],
                                   turn[j % 2][:, 0:D].rearrange("p (k t) -> p k t", k=KD)).then_inc(xhT_ready, 1)

        @block.tensor
        def _(pe):
            pe.wait_ge(rw_scaled, 1)
            for k in range(KD):
                mm = nc.tensor.transpose(turn[0][:, k * E:(k + 1) * E], rw_rows[:, k * P:(k + 1) * P], ident[0:E, 0:E])
            mm.then_inc(rw_turned, 1)
            pe.wait_ge(rw_ready, 1)
            with pe.Fori(0, NC) as n:
                pe.wait_ge(in_loaded, 32 * (n + 1))
                for j in range(TPC):
                    pe.wait_ge(scaled_ready, TPC * n + max(j - 1, 0) + 1)
                    for g in range(G):
                        mm = nc.tensor.transpose(token_major[j % 2][:, g * UNITS:(g + 1) * UNITS, :],
                                                 heads[:, g, j * P:(j + 1) * P], ident[:])
                    mm.then_inc(turned, 1)
                pe.wait_ge(xhT_ready, TPC * n + 1)
                pe.wait_ge(lgs_ready, TPC * n + 1)
                for j in range(TPC):
                    pe.wait_ge(att_ready, TPC * n + j + 2)
                    pe.wait_ge(attT_ready, TPC * n + max(j - 1, 0) + 1)
                    for k in range(KD):
                        mm = nc.tensor.transpose(turn[j % 2][:, k * P:(k + 1) * P], att[:, j, k * P:(k + 1) * P],
                                                 ident[:])
                    mm.then_inc(att_turned, 1)
                    pe.wait_ge(attT_ready, TPC * n + j + 2)
                    pe.wait_ge(z_ready, TPC * n + max(j - 1, 0) + 1)
                    for k in range(KD):
                        mm = nc.tensor.matmul(prod[j % 2][:, 0:D], attT[:, j, k * P:(k + 1) * P], wo[:, k, :],
                                              start=(k == 0), stop=(k == KD - 1))
                    mm.then_inc(y_ready, 1)
                pe.wait_ge(z_ready, TPC * (n + 1) + 1)
                for j in range(TPC):
                    pe.wait_ge(xh_ready, TPC * n + j + 1)
                    pe.wait_ge(xhT_ready, TPC * n + max(j - 1, 0) + 1)
                    for k in range(KD):
                        mm = nc.tensor.transpose(turn[j % 2][:, k * P:(k + 1) * P], xh[:, j, k * P:(k + 1) * P],
                                                 ident[:])
                    mm.then_inc(xh_turned, 1)
                    pe.wait_ge(xhT_ready, TPC * n + j + 2)
                    pe.wait_ge(lgs_ready, TPC * n + max(j - 1, 0) + 1)
                    for k in range(KD):
                        mm = nc.tensor.matmul(prod[j % 2][:, 0:E], xhT[:, k, j * P:(j + 1) * P], rw_T[:, k, :],
                                              start=(k == 0), stop=(k == KD - 1))
                    mm.then_inc(logits_ready, 1)

        @block.vector
        def _(dve):
            setup = Chain(dve, setup_chain)
            dve.wait_ge(consts_loaded, 16 * NL)
            setup.add(nc.vector.tensor_tensor(lam_mul[:], lam_in[:, 0:4:2, :], lam_in[:, 1:4:2, :], ALU.mult))
            setup.wait()
            nc.vector.tensor_reduce(lam_sum[:], lam_mul[:], AX.X, ALU.add).then_inc(lam_summed, 1)
            dve.wait_ge(lam_exped, 1)
            setup.add(nc.vector.tensor_tensor(lam_neg[:], lam_exp[:, 1:2], lam_exp[:, 0:1], ALU.subtract))
            dve.wait_ge(coef_ones, 1)
            setup.wait()
            setup.add(nc.vector.tensor_scalar(lam_neg[:], lam_neg[:], LAMBDA_INIT, None, ALU.subtract))
            setup.wait()
            setup.add(nc.vector.tensor_scalar(coef[:, 1:NU:2], coef[:, 1:NU:2], lam_neg[:, 0:1], None, ALU.mult))
            setup.add(nc.vector.tensor_tensor(rw_all[:], rw_all[:], rnb[:].rearrange("p (o d) -> p o d", o=1)
                                              .to_broadcast((P, E, D)), ALU.mult))
            setup.wait()
            setup.add(nc.vector.tensor_reduce(rbias[:], rw_all[:], AX.X, ALU.add))
            nc.vector.tensor_tensor(rw_rows[:], rw_rows[:], rg_rows[:], ALU.mult).then_inc(rw_scaled, 1)
            setup.wait()
            setup.add(nc.vector.tensor_tensor(rbias[:], rbias[:], rbias_in[:], ALU.add))
            dve.wait_ge(rw_turned, 1)
            nc.vector.tensor_copy(rw_T[:].rearrange("p k e -> p (k e)"), turn[0][:, 0:KD * E]).then_inc(rw_ready, 1)
            setup.wait()

            LINKS = 5 * TPC
            with dve.Fori(0, NC) as n:
                chain = Chain(dve, ln_chain, n * LINKS)

                def layernorm(i, src, dst, done, before, tiles=range(TPC)):
                    for j in tiles:
                        before(j)
                        chain.add(nc.vector.bn_stats(st[i][:, j, :], src(j)))
                    chain.wait()
                    dve.sem_inc(j_gate_dve, 1)
                    for j in tiles:
                        nc.vector.bn_aggr(mv[i][:, j, :], st[i][:, j, :]).then_inc(var_ready[i], 1)
                    dve.wait_ge(var_ready[i], TPC * n + tiles[-1] + 1)
                    dve.wait_ge(rs_ready[i], TPC // len(tiles) * n + tiles.stop // len(tiles))
                    for j in tiles:
                        nc.vector.tensor_scalar(dst[:, j, :], src(j), mv[i][:, j, 0:1], rs[i][:, j:j + 1],
                                                ALU.subtract, ALU.mult).then_inc(done, 1)

                for j in range(TPC):
                    dve.wait_ge(turned, TPC * n + j + 2)
                    tm = token_major[j % 2]
                    chain.add(nc.vector.reciprocal(rcp[:, j, :], tm[:, :, HD]))
                    chain.wait()
                    chain.add(nc.vector.tensor_tensor(rcc[:, j, :], rcp[:, j, :], coef[:], ALU.mult))
                    chain.wait()
                    dve.wait_ge(att_ready, TPC * n + max(j - 1, 0) + 1)
                    nc.vector.tensor_tensor(scaled[:, j % 2], tm[:, :, 0:HD],
                                            rcc[:, j, :].rearrange("p (u o) -> p u o", o=1).to_broadcast((P, NU, HD)),
                                            ALU.mult).then_inc(scaled_ready, 1)
                for j0 in range(0, TPC, 2):
                    layernorm(0, lambda j: prod[j % 2][:, 0:D], z, z_ready,
                              lambda j: dve.wait_ge(y_ready, TPC * n + j + 1), range(j0, j0 + 2))
                dve.wait_ge(out_stored, 48 * n + 1)
                layernorm(1, lambda j: zs[:, j, :], x1, x1_ready, lambda j: dve.wait_ge(zs_ready, TPC * n + j + 2))
                layernorm(2, lambda j: x1[:, j, :], xh, xh_ready, lambda j: dve.wait_ge(x1_ready, TPC * n + j + 1))
                for j in range(TPC):
                    dve.wait_ge(logits_ready, TPC * n + j + 2)
                    nc.vector.tensor_tensor(lgs[:, j, :], prod[j % 2][:, 0:E], rbias[:], ALU.add).then_inc(lgs_ready, 1)
                assert chain.n == LINKS, chain.n


def stage_route(nc, a):
    lgd, cold, expd, b1, ln_g, ln_b = (a[n] for n in ("lgd", "cold", "expd", "b1", "ln_g", "ln_b"))
    NT, KD, IC, D, E, T, TS, NTL, ident = (a[n] for n in ("NT", "KD", "IC", "D", "E", "T", "TS", "NTL", "ident"))
    share, slot = a["share"], a["slot"]
    TM = T // TS
    NC = IC + 2 * KD
    with ExitStack() as ctx:
        sb, ps, sem = opener(nc, ctx)
        lg = sb("lg", [P, NT, E], F32)
        lg2 = sb("lg2", [P, NT, E], F32)
        order = sb("order", [P, E], F32)
        thr = sb("thr", [P, TM], F32)
        tau = sb("tau", [P, NTL], F32)
        upper = sb("upper", [P, P], F32)
        ones = sb("ones", [P, P], F32)
        pick = [sb(f"pick{i}", [P, NT, E], F32) for i in range(2)]
        rank = [sb(f"rank{i}", [P, NT, E], F32) for i in range(2)]
        hot = [sb(f"hot{i}", [P, NT, E], F32) for i in range(2)]
        best = [sb(f"best{i}", [P, NT], F32) for i in range(2)]
        first = [sb(f"first{i}", [P, NT], F32) for i in range(2)]
        gap = sb("gap", [P, NT], F32)
        eg = sb("eg", [P, NT], F32)
        den = sb("den", [P, NT], F32)
        both = sb("both", [P, NT, E], F32)
        total = sb("total", [P, NT, E], F32)
        run = [sb(f"run{i}", [P, NT, E], F32) for i in range(2)]
        place = sb("place", [P, NT, E], F32)
        over = sb("over", [P, E, TM], F32)
        tiles = sb("tiles", [P, E], F32)
        ends = [sb(f"ends{i}", [P, E], F32) for i in range(2)]
        base = sb("base", [P, E], F32)
        past = sb("past", [P, NTL, E], F32)
        owner = sb("owner", [P, NTL], F32)
        owner_i = sb("owner_i", [P, NTL], mybir.dt.int32)
        took = [sb(f"took{i}", [P, NT, E], F32) for i in range(2)]
        slot_f = [sb(f"slot_f{i}", [P, NT], F32) for i in range(2)]
        b1_rows = sb("b1_rows", [E * IC, P], F32)
        ln_rows = sb("ln_rows", [2 * E * KD, P], F32)
        cols = sb("cols", [P, E, NC], F32)
        counted = ps("counted", [P, NT * E], F32)
        totals = ps("totals", [P, NT * E], F32)
        turned = ps("cols_turned", [P, 3 * E * IC], F32)
        names = ("loaded", "rows_loaded", "ones_set", "upper_set", "consts_set", "chain", "gap_ready",
                 "eg_ready", "both_ready", "counted_ready", "turned_ready", "cols_ready", "owner_ready",
                 "slots_ready", "stored")
        (loaded, rows_loaded, ones_set, upper_set, consts_set, chain_sem, gap_ready, eg_ready,
         both_ready, counted_ready, turned_ready, cols_ready, owner_ready, slots_ready, stored) = (sem("r_" + n) for n in names)
        block = ctx.enter_context(nc.Block())

        @block.sync
        def _(sp):
            sp.dma_start(lg[:], lgd).then_inc(loaded, 16)
            sp.dma_start(b1_rows[:], b1.rearrange("e (c i) -> (e c) i", i=P)).then_inc(rows_loaded, 16)
            sp.dma_start(ln_rows[0:E * KD], ln_g.rearrange("e (k d) -> (e k) d", d=P)).then_inc(rows_loaded, 16)
            sp.dma_start(ln_rows[E * KD:2 * E * KD], ln_b.rearrange("e (k d) -> (e k) d", d=P)).then_inc(rows_loaded, 16)
            sp.wait_ge(cols_ready, 2)
            sp.dma_start(cold.rearrange("e p c -> p e c"), cols[:]).then_inc(stored, 16)
            sp.wait_ge(owner_ready, 1)
            sp.dma_start(expd, owner_i[0:1, :]).then_inc(stored, 16)
            sp.wait_ge(stored, 32)

        @block.gpsimd
        def _(pool):
            nc.gpsimd.memset(ones[:], 1.0).then_inc(ones_set, 1)
            pool.wait_ge(ones_set, 1)
            nc.gpsimd.affine_select(out=upper[:], in_=ones[:], compare_op=ALU.is_gt, fill=0.0, base=0,
                                    pattern=[[1, P]], channel_multiplier=-1).then_inc(upper_set, 1)
            for e in range(E):
                nc.gpsimd.memset(order[:, e:e + 1], float(E - e)).then_inc(consts_set, 1)
            for m in range(TM):
                nc.gpsimd.memset(thr[:, m:m + 1], float(m * TS)).then_inc(consts_set, 1)
            for m in range(NTL):
                nc.gpsimd.memset(tau[:, m:m + 1], float(m)).then_inc(consts_set, 1)

        @block.scalar
        def _(act):
            act.wait_ge(gap_ready, 1)
            nc.scalar.activation(eg[:], gap[:], ACT.Exp).then_inc(eg_ready, 1)
            act.wait_ge(turned_ready, 1)
            nc.scalar.copy(cols[:, :, 0:IC], turned[:, 0:E * IC].rearrange("p (e c) -> p e c", e=E)
                           ).then_inc(cols_ready, 1)
            nc.scalar.copy(cols[:, :, IC:NC].rearrange("p e (w k) -> p w e k", w=2),
                           turned[:, E * IC:E * IC + 2 * E * KD].rearrange("p (w e k) -> p w e k", w=2, e=E)
                           ).then_inc(cols_ready, 1)

        @block.tensor
        def _(pe):
            pe.wait_ge(rows_loaded, 48)
            nc.tensor.transpose(turned[:, 0:E * IC], b1_rows[:], ident[0:E * IC, 0:E * IC])
            nc.tensor.transpose(turned[:, E * IC:E * IC + 2 * E * KD], ln_rows[:],
                                ident[0:2 * E * KD, 0:2 * E * KD]).then_inc(turned_ready, 1)
            pe.wait_ge(upper_set, 1)
            pe.wait_ge(both_ready, 1)
            rhs = both[:].rearrange("p t e -> p (t e)")
            nc.tensor.matmul(counted[:], upper[:], rhs, start=True, stop=True)
            nc.tensor.matmul(totals[:], ones[:], rhs, start=True, stop=True).then_inc(counted_ready, 1)

        @block.vector
        def _(dve):
            chain = Chain(dve, chain_sem)

            def step(ins):
                chain.add(ins)
                chain.wait()

            def over_e(v):
                return v.rearrange("p (t o) -> p t o", o=1).to_broadcast((P, NT, E))

            dve.wait_ge(loaded, 16)
            dve.wait_ge(consts_set, E + TM + NTL)
            order_b = order[:].rearrange("p (o e) -> p o e", o=1).to_broadcast((P, NT, E))
            for r, src in ((0, lg), (1, lg2)):
                step(nc.vector.tensor_reduce(best[r][:], src[:], AX.X, ALU.max))
                step(nc.vector.tensor_tensor(pick[r][:], src[:], over_e(best[r][:]), ALU.is_equal))
                step(nc.vector.tensor_tensor(rank[r][:], pick[r][:], order_b, ALU.mult))
                step(nc.vector.tensor_reduce(first[r][:], rank[r][:], AX.X, ALU.max))
                step(nc.vector.tensor_tensor(hot[r][:], rank[r][:], over_e(first[r][:]), ALU.is_equal))
                if r == 0:
                    step(nc.vector.scalar_tensor_tensor(lg2[:], hot[0][:], -3.0e38, lg[:], ALU.mult, ALU.add))
            nc.vector.tensor_tensor(both[:], hot[0][:], hot[1][:], ALU.add).then_inc(both_ready, 1)
            nc.vector.tensor_tensor(gap[:], best[1][:], best[0][:], ALU.subtract).then_inc(gap_ready, 1)
            dve.wait_ge(eg_ready, 1)
            step(nc.vector.tensor_scalar(den[:], eg[:], 1.0, None, ALU.add))
            step(nc.vector.reciprocal(share[0][:], den[:]))
            step(nc.vector.tensor_tensor(share[1][:], share[0][:], eg[:], ALU.mult))
            dve.wait_ge(counted_ready, 1)
            step(nc.vector.tensor_copy(total[:].rearrange("p t e -> p (t e)"), totals[:]))
            src, d, i = total, 1, 0
            while d < NT:
                chain.add(nc.vector.tensor_copy(run[i][:, 0:d, :], src[:, 0:d, :]))
                step(nc.vector.tensor_tensor(run[i][:, d:NT, :], src[:, d:NT, :], src[:, 0:NT - d, :], ALU.add))
                src, d, i = run[i], 2 * d, 1 - i
            count = src[:, NT - 1, :].rearrange("p (e o) -> p e o", o=1).to_broadcast((P, E, TM))
            step(nc.vector.tensor_tensor(over[:], count, thr[:].rearrange("p (o m) -> p o m", o=1)
                                         .to_broadcast((P, E, TM)), ALU.is_gt))
            step(nc.vector.tensor_reduce(tiles[:], over[:], AX.X, ALU.add))
            end, d, i = tiles, 1, 0
            while d < E:
                chain.add(nc.vector.tensor_copy(ends[i][:, 0:d], end[:, 0:d]))
                step(nc.vector.tensor_tensor(ends[i][:, d:E], end[:, d:E], end[:, 0:E - d], ALU.add))
                end, d, i = ends[i], 2 * d, 1 - i
            step(nc.vector.tensor_tensor(past[:], end[:].rearrange("p (o e) -> p o e", o=1).to_broadcast((P, NTL, E)),
                                         tau[:].rearrange("p (m o) -> p m o", o=1).to_broadcast((P, NTL, E)),
                                         ALU.is_le))
            step(nc.vector.tensor_reduce(owner[:], past[:], AX.X, ALU.add))
            nc.vector.tensor_scalar(owner_i[:], owner[:], float(E - 1), None, ALU.min).then_inc(owner_ready, 1)
            step(nc.vector.tensor_tensor(base[:], end[:], tiles[:], ALU.subtract))
            step(nc.vector.tensor_tensor(place[:], src[:], total[:], ALU.subtract))
            step(nc.vector.scalar_tensor_tensor(place[:], base[:].rearrange("p (o e) -> p o e", o=1)
                                                .to_broadcast((P, NT, E)), float(TS), place[:], ALU.mult, ALU.add))
            step(nc.vector.tensor_tensor(place[:], counted[:].rearrange("p (t e) -> p t e", e=E), place[:], ALU.add))
            for r in range(2):
                step(nc.vector.tensor_tensor(took[r][:], hot[r][:], place[:], ALU.mult))
                step(nc.vector.tensor_reduce(slot_f[r][:], took[r][:], AX.X, ALU.add))
                nc.vector.tensor_copy(slot[r][:], slot_f[r][:]).then_inc(slots_ready, 1)


def stage_scatter(nc, a):
    xhd, xgd, slot, NT, D, NCH = (a[n] for n in ("xhd", "xgd", "slot", "NT", "D", "NCH"))
    with ExitStack() as ctx:
        sb, ps, sem = opener(nc, ctx)
        xh = sb("scatter_xh", [P, 2, TPC, D], F32)
        cur = sb("scatter_cur", [P, 2, 2, TPC], mybir.dt.int32)
        cur_ready, gate, buffer_free = sem("s_cur_ready"), sem("s_gate"), sem("s_buffer_free")
        xh_loaded = [sem(f"s_xh_loaded{i}") for i in range(2)]
        scattered = [sem(f"s_scattered{i}") for i in range(2)]
        SC = 16 * 2 * TPC
        block = ctx.enter_context(nc.Block())

        @block.sync
        def _(sp):
            sp.sem_inc(buffer_free, 2)
            with sp.Fori(0, NCH // 2) as it:
                for h in range(2):
                    sp.wait_ge(buffer_free, 2 * (it + 1))
                    sp.dma_start(xh[:, h], xhd.rearrange("(i h j p) d -> i h p j d", h=2, j=TPC, p=P)[it, h]
                                 ).then_inc(xh_loaded[h], 16)

        @block.gpsimd
        def _(pool):
            with pool.Fori(0, NCH // 2) as it:
                for h in range(2):
                    for r in range(2):
                        nc.gpsimd.tensor_copy(cur[:, h, r, :], slot[r][:, bass.ds((2 * it + h) * TPC, TPC)]
                                              ).then_inc(cur_ready, 1)
                    pool.wait_ge(cur_ready, 2 * (2 * it + h + 1))
                    pool.wait_ge(xh_loaded[h], 16 * (it + 1))
                    pool.sem_inc(gate, 1)
                    for j in range(TPC):
                        for r in range(2):
                            nc.gpsimd.indirect_dma_start(
                                xgd, bass.IndirectOffsetOnAxis(ap=cur[:, h, r, j:j + 1], axis=0),
                                xh[:, h, j, :], None).then_inc(scattered[h], 16)
                for h in range(2):
                    pool.wait_ge(scattered[h], SC * (it + 1))
                    pool.sem_inc(buffer_free, 1)


def stage_experts(nc, a):
    xgd, ygd, cold, expd, w1, w2, b2 = (a[n] for n in ("xgd", "ygd", "cold", "expd", "w1", "w2", "b2"))
    KD, IC, D, E, I, TS, NTL, ident = (a[n] for n in ("KD", "IC", "D", "E", "I", "TS", "NTL", "ident"))
    NC = IC + 2 * KD
    TT = TS // P
    NI = NTL // 2
    with ExitStack() as ctx:
        sb, ps, sem = opener(nc, ctx)
        W1 = [sb(f"W1_{i}", [P, KD, I], F32) for i in range(2)]
        W1g = [sb(f"W1g_{i}", [P, KD, I], F32) for i in range(2)]
        W2 = [sb(f"W2_{i}", [P, IC, D], F32) for i in range(2)]
        col = [sb(f"col{i}", [P, NC], F32) for i in range(2)]
        b2b = [sb(f"b2b{i}", [P, D], F32) for i in range(2)]
        xg = [sb(f"xg{i}", [P, TT, D], F32) for i in range(2)]
        xgT = [sb(f"xgT{i}", [P, KD, TS], F32) for i in range(2)]
        bias = [sb(f"bias{i}", [P, IC], F32) for i in range(2)]
        hT = [sb(f"hT{i}", [P, IC, TS], F32) for i in range(2)]
        y = [sb(f"y{i}", [P, TT, D], F32) for i in range(2)]
        owners = sb("owners", [1, NTL], mybir.dt.int32)
        pxT = [ps(f"e_xT{k}", [P, TC], F32) for k in range(KD)]
        pbias = ps("e_bias", [P, TC], F32)
        pre = [ps(f"pre{i}", [P, TC], F32) for i in range(3)]
        py = [ps(f"py{i}", [P, TC], F32) for i in range(2)]
        names = ("xgT_ready", "bias_ready", "pre_ready", "hT_ready", "py_ready", "y_ready")
        from_one = xgT_ready, bias_ready, pre_ready, hT_ready, py_ready, y_ready = [sem("e_" + n) for n in names]
        y_stored = [sem(f"e_y_stored{i}") for i in range(2)]
        gate_sp = sem("e_gate_sp")
        owners_loaded, turned, W1g_ready, pbias_ready = (
            sem("e_" + n) for n in ("owners_loaded", "turned", "W1g_ready", "pbias_ready"))
        in_loaded = [sem(f"e_in_loaded{i}") for i in range(2)]
        w2_loaded = [sem(f"e_w2_loaded{i}") for i in range(2)]
        block = ctx.enter_context(nc.Block())

        @block.sync
        def _(sp):
            for s in from_one + y_stored:
                sp.sem_inc(s, 1)
            sp.dma_start(owners[:], expd).then_inc(owners_loaded, 16)
            sp.wait_ge(owners_loaded, 16)

            def owner(tile):
                return sp.value_load(owners[0:1, bass.ds(tile, 1)], min_val=0, max_val=E - 1)

            def load_in(tile, p):
                e = owner(tile)
                sp.dma_start(xg[p][:], xgd.rearrange("(n j p) d -> n p j d", j=TT, p=P)[tile]).then_inc(in_loaded[p], 16)
                sp.dma_start(W1[p][:], w1.rearrange("e (k p) i -> e p k i", p=P)[e]).then_inc(in_loaded[p], 16)
                sp.dma_start(col[p][:], cold[e]).then_inc(in_loaded[p], 16)

            def load_w2(tile, p):
                e = owner(tile)
                sp.dma_start(W2[p][:], w2.rearrange("e (c p) d -> e p c d", p=P)[e]).then_inc(w2_loaded[p], 16)
                sp.dma_start(b2b[p][:], b2.rearrange("e (o d) -> e o d", o=1)[e].to_broadcast((P, D))
                             ).then_inc(w2_loaded[p], 16)

            def round_(it, more):
                if more:
                    for p in range(2):
                        n = 2 * it + p
                        sp.wait_ge(turned, n + 1)
                        sp.sem_inc(gate_sp, 1)
                        sp.wait_ge(W1g_ready, KD * (n + 1))
                        sp.sem_inc(gate_sp, 1)
                        sp.wait_ge(bias_ready, n + 2)
                        sp.sem_inc(gate_sp, 1)
                        load_in(n + 2, p)
                for p in range(2):
                    n = 2 * it + p
                    sp.wait_ge(y_ready, TT * (n + 1) + 1)
                    sp.dma_start(ygd.rearrange("(n j p) d -> n p j d", j=TT, p=P)[n], y[p][:]
                                 ).then_inc(y_stored[p], 16)
                    if more:
                        load_w2(n + 2, p)

            for p in range(2):
                load_in(p, p)
                load_w2(p, p)
            with sp.Fori(0, NI - 1) as it:
                round_(it, True)
            round_(NI - 1, False)
            for p in range(2):
                sp.wait_ge(y_stored[p], 16 * NI + 1)

        @block.tensor
        def _(pe):
            with pe.Fori(0, NI) as it:
                for p in range(2):
                    n = 2 * it + p
                    pe.wait_ge(in_loaded[p], 48 * (it + 1))
                    pe.wait_ge(xgT_ready, KD * n + 1)
                    for k in range(KD):
                        for j in range(TT):
                            mm = nc.tensor.transpose(pxT[k][:, j * P:(j + 1) * P], xg[p][:, j, k * P:(k + 1) * P],
                                                     ident[:])
                    mm.then_inc(turned, 1)
                    pe.wait_ge(bias_ready, n + 1)
                    for c in range(IC):
                        for k in range(KD):
                            mm = nc.tensor.matmul(pbias[:, c:c + 1], W1[p][:, k, c * P:(c + 1) * P],
                                                  col[p][:, IC + KD + k:IC + KD + k + 1],
                                                  start=(k == 0), stop=(k == KD - 1))
                    mm.then_inc(pbias_ready, 1)
                    pe.wait_ge(xgT_ready, KD * (n + 1) + 1)
                    pe.wait_ge(W1g_ready, KD * (n + 1))
                    for c in range(IC):
                        i = p * IC + c
                        pe.wait_ge(hT_ready, 2 * IC * it + max(i - 2, 0) + 1)
                        for k in range(KD):
                            mm = nc.tensor.matmul(pre[i % 3][:, 0:TS], W1g[p][:, k, c * P:(c + 1) * P],
                                                  xgT[p][:, k, :], start=(k == 0), stop=(k == KD - 1))
                        mm.then_inc(pre_ready, 1)
                for p in range(2):
                    n = 2 * it + p
                    pe.wait_ge(hT_ready, IC * (n + 1) + 1)
                    pe.wait_ge(w2_loaded[p], 32 * (it + 1))
                    for j in range(TT):
                        i = p * TT + j
                        pe.wait_ge(y_ready, 2 * TT * it + max(i - 1, 0) + 1)
                        for c in range(IC):
                            mm = nc.tensor.matmul(py[i % 2][:, 0:D], hT[p][:, c, j * P:(j + 1) * P], W2[p][:, c, :],
                                                  start=(c == 0), stop=(c == IC - 1))
                        mm.then_inc(py_ready, 1)

        @block.scalar
        def _(act):
            with act.Fori(0, NI) as it:
                for p in range(2):
                    n = 2 * it + p
                    act.wait_ge(turned, n + 1)
                    for k in range(KD):
                        nc.scalar.copy(xgT[p][:, k, :], pxT[k][:, 0:TS]).then_inc(xgT_ready, 1)
                    act.wait_ge(bias_ready, n + 2)
                    act.wait_ge(py_ready, 2 * TT * it + 1)
                    for c in range(IC):
                        i = p * IC + c
                        act.wait_ge(pre_ready, 2 * IC * it + i + 2)
                        nc.scalar.activation(hT[p][:, c, :], pre[i % 3][:, 0:TS], ACT.Gelu,
                                             bias=bias[p][:, c:c + 1]).then_inc(hT_ready, 1)

        @block.vector
        def _(dve):
            with dve.Fori(0, NI) as it:
                for p in range(2):
                    n = 2 * it + p
                    dve.wait_ge(in_loaded[p], 48 * (it + 1))
                    dve.wait_ge(pre_ready, 2 * IC * it + 1)
                    for k in range(KD):
                        nc.vector.tensor_scalar(W1g[p][:, k, :], W1[p][:, k, :], col[p][:, IC + k:IC + k + 1], None,
                                                ALU.mult).then_inc(W1g_ready, 1)
                    dve.wait_ge(pbias_ready, n + 1)
                    dve.wait_ge(hT_ready, 2 * IC * it + 1)
                    nc.vector.tensor_tensor(bias[p][:], pbias[:, 0:IC], col[p][:, 0:IC], ALU.add
                                            ).then_inc(bias_ready, 1)
                for p in range(2):
                    dve.wait_ge(y_stored[p], 16 * it + 1)
                    dve.wait_ge(w2_loaded[p], 32 * (it + 1))
                    for j in range(TT):
                        i = p * TT + j
                        dve.wait_ge(py_ready, 2 * TT * it + i + 2)
                        nc.vector.tensor_tensor(y[p][:, j, :], py[i % 2][:, 0:D], b2b[p][:], ALU.add
                                                ).then_inc(y_ready, 1)


def stage_finish(nc, a):
    x1d, ygd, out, slot, share = (a[n] for n in ("x1d", "ygd", "out", "slot", "share"))
    NCH, D = a["NCH"], a["D"]
    with ExitStack() as ctx:
        sb, ps, sem = opener(nc, ctx)
        x1 = sb("f_x1", [P, TPC, D], F32)
        got = sb("f_got", [P, TPC, 2, D], F32)
        cur = sb("f_cur", [P, 2, TPC], mybir.dt.int32)
        part = sb("f_part", [P, 2, TPC], F32)
        one = sb("f_one", [P, TPC, D], F32)
        two = sb("f_two", [P, TPC, D], F32)
        fin = sb("f_fin", [P, TPC, D], F32)
        st, mv = sb("f_st", [P, TPC, 6], F32), sb("f_mv", [P, TPC, 2], F32)
        ve, rs = sb("f_ve", [P, TPC], F32), sb("f_rs", [P, TPC], F32)
        minus_half = sb("f_minus_half", [P, TPC], F32)
        names = ("cur_ready", "part_ready", "half_set", "gate_pool", "gate_dve", "one_ready", "two_ready", "st_ready",
                 "var_ready", "ve_ready", "rs_ready", "fin_ready")
        (cur_ready, part_ready, half_set, gate_pool, gate_dve, one_ready, two_ready, st_ready,
         var_ready, ve_ready, rs_ready, fin_ready) = (sem("f_" + n) for n in names)
        x1_loaded, gathered, stored = ([sem(f"f_{n}{j}") for j in range(TPC)] for n in ("x1_loaded", "gathered", "stored"))
        block = ctx.enter_context(nc.Block())

        @block.sync
        def _(sp):
            for s in (two_ready, fin_ready, *stored):
                sp.sem_inc(s, 1)

            def load(n, j):
                sp.dma_start(x1[:, j, :], x1d.rearrange("(n j p) d -> n j p d", j=TPC, p=P)[n, j]
                             ).then_inc(x1_loaded[j], 16)

            def store(n, j):
                sp.wait_ge(fin_ready, TPC * n + j + 2)
                sp.dma_start(out.rearrange("b (c j p) d -> (b c) j p d", j=TPC, p=P)[n, j], fin[:, j, :]
                             ).then_inc(stored[j], 16)

            for j in range(TPC):
                load(0, j)
            with sp.Fori(0, NCH - 1) as n:
                for j in range(TPC):
                    sp.wait_ge(two_ready, TPC * n + j + 2)
                    load(n + 1, j)
                for j in range(TPC):
                    store(n, j)
            for j in range(TPC):
                store(NCH - 1, j)
            for j in range(TPC):
                sp.wait_ge(stored[j], 16 * NCH + 1)

        @block.gpsimd
        def _(pool):
            nc.gpsimd.memset(minus_half[:], -0.5).then_inc(half_set, 1)
            pool.wait_ge(half_set, 1)

            def gather(n, free):
                if free:
                    pool.wait_ge(one_ready, TPC * n)
                    pool.wait_ge(two_ready, TPC * n + 1)
                    pool.sem_inc(gate_pool, 1)
                for r in range(2):
                    nc.gpsimd.tensor_copy(cur[:, r, :], slot[r][:, bass.ds(n * TPC, TPC)]).then_inc(cur_ready, 1)
                pool.wait_ge(cur_ready, 2 * (n + 1))
                pool.sem_inc(gate_pool, 1)
                for j in range(TPC):
                    for r in range(2):
                        nc.gpsimd.indirect_dma_start(
                            got[:, j, r, :], None, ygd,
                            bass.IndirectOffsetOnAxis(ap=cur[:, r, j:j + 1], axis=0)).then_inc(gathered[j], 16)

            def rsqrt(n):
                pool.wait_ge(var_ready, TPC * (n + 1))
                pool.sem_inc(gate_pool, 1)
                nc.gpsimd.tensor_scalar(ve[:], mv[:, :, 1], EPS, None, ALU.add).then_inc(ve_ready, 1)
                pool.wait_ge(ve_ready, n + 1)
                nc.gpsimd.tensor_tensor(rs[:], ve[:], minus_half[:], ALU.pow).then_inc(rs_ready, 1)

            gather(0, False)
            with pool.Fori(0, NCH - 1) as n:
                gather(n + 1, True)
                rsqrt(n)
            rsqrt(NCH - 1)

        @block.vector
        def _(dve):
            with dve.Fori(0, NCH) as n:
                dve.wait_ge(fin_ready, TPC * n + 1)
                for r in range(2):
                    nc.vector.tensor_copy(part[:, r, :], share[r][:, bass.ds(n * TPC, TPC)]).then_inc(part_ready, 1)
                dve.wait_ge(part_ready, 2 * (n + 1))
                for j in range(TPC):
                    dve.wait_ge(x1_loaded[j], 16 * (n + 1))
                    dve.wait_ge(gathered[j], 32 * (n + 1))
                    nc.vector.scalar_tensor_tensor(one[:, j, :], got[:, j, 0, :], part[:, 0, j:j + 1], x1[:, j, :],
                                                   ALU.mult, ALU.add).then_inc(one_ready, 1)
                    dve.wait_ge(one_ready, TPC * n + j + 1)
                    nc.vector.scalar_tensor_tensor(two[:, j, :], got[:, j, 1, :], part[:, 1, j:j + 1], one[:, j, :],
                                                   ALU.mult, ALU.add).then_inc(two_ready, 1)
                for j in range(TPC):
                    dve.wait_ge(two_ready, TPC * n + j + 2)
                    nc.vector.bn_stats(st[:, j, :], two[:, j, :]).then_inc(st_ready, 1)
                dve.wait_ge(st_ready, TPC * (n + 1))
                dve.sem_inc(gate_dve, 1)
                for j in range(TPC):
                    nc.vector.bn_aggr(mv[:, j, :], st[:, j, :]).then_inc(var_ready, 1)
                dve.wait_ge(var_ready, TPC * (n + 1))
                dve.wait_ge(rs_ready, n + 1)
                for j in range(TPC):
                    dve.wait_ge(stored[j], 16 * n + 1)
                    nc.vector.tensor_scalar(fin[:, j, :], two[:, j, :], mv[:, j, 0:1], rs[:, j:j + 1],
                                            ALU.subtract, ALU.mult).then_inc(fin_ready, 1)


_INS = ["L0_attn_x", "L0_attn_Wq", "L0_attn_Wk", "L0_attn_Wv", "L0_attn_Wo", "L0_attn_lambda_q1",
        "L0_attn_lambda_k1", "L0_attn_lambda_q2", "L0_attn_lambda_k2", "L0_attn_gamma", "L0_attn_beta",
        "L0_ffn_rn_g", "L0_ffn_rn_b", "L0_ffn_router_w", "L0_ffn_router_b", "L0_ffn_ln_g", "L0_ffn_ln_b",
        "L0_ffn_w1", "L0_ffn_b1", "L0_ffn_w2", "L0_ffn_b2"]


def kernel(**inputs):
    import numpy as _np
    import concourse.bacc as _bacc
    from concourse import mybir as _mybir
    from concourse.bass_utils import run_bass_kernel_spmd as _run

    nc = _bacc.Bacc("TRN2", target_bir_lowering=False, num_devices=1)
    arrays, args = {}, []
    for name in _INS:
        a = _np.ascontiguousarray(inputs[name])
        arrays[f"in_{name}_dram"] = a
        args.append(nc.dram_tensor(f"in_{name}_dram", a.shape, _mybir.dt.from_np(a.dtype), kind="ExternalInput").ap())
    shape = inputs["L0_attn_x"].shape
    args.append(nc.dram_tensor("out_0_dram", shape, _mybir.dt.float32, kind="ExternalOutput").ap())
    diff_attention_moe(nc, *args)
    r = _run(nc, [arrays], core_ids=[0])
    return r.results[0]["out_0_dram"]
```

```python
import math
from contextlib import ExitStack

import concourse.bass as bass
from concourse import mybir

ALU = mybir.AluOpType
ACT = mybir.ActivationFunctionType
AX = mybir.AxisListType
F32 = mybir.dt.float32
BF16 = mybir.dt.bfloat16

P = 128
TC = 512
TPC = TC // P
EPS = 1e-5
HD = 16
UNITS = 4
GF = UNITS * HD
LAMBDA_INIT = 0.8 - 0.6 * math.exp(-0.3 * 11)
Q_PARTS = (0, 0, 0, 1, 1, 2)
K_PARTS = (0, 1, 2, 0, 1, 0)
KR = 16 * len(Q_PARTS)
KM = KR + 3


def diff_attention_moe(nc, x, Wq, Wk, Wv, Wo, lq1, lk1, lq2, lk2, gamma, beta, rn_g, rn_b,
                       router_w, router_b, ln_g, ln_b, w1, b1, w2, b2, out):
    NB, S, D = x.shape
    T = NB * S
    KD = D // P
    E, _, I = w1.shape
    IC = I // P
    G = D // HD // 2
    CH = S // TC
    KB = S // P
    NT = T // P
    NCH = T // TC
    assert D == 256 and S == 2048 and E == 8 and I == 1024 and KB == 16 and CH == 4

    qd = nc.dram_tensor("q_parts", (NB * G, 3, CH, HD * UNITS, TC), BF16, kind="Internal").ap()
    kd = nc.dram_tensor("k_parts", (NB * G, 3, HD * UNITS, S), BF16, kind="Internal").ap()
    vd = nc.dram_tensor("v_groups", (NB * G, P, KB, 64), F32, kind="Internal").ap()
    od = nc.dram_tensor("attended", (NB * G, P, S), F32, kind="Internal").ap()
    x1d = nc.dram_tensor("x1", (T, D), F32, kind="Internal").ap()
    xhd = nc.dram_tensor("xh", (T, D), F32, kind="Internal").ap()
    lgd = nc.dram_tensor("logits", (P, NT, E), F32, kind="Internal").ap()

    TS = P
    NTL = (2 * T + E * (TS - 1)) // TS
    NTL += NTL % 2
    xgd = nc.dram_tensor("slot_rows", (NTL * TS, D), F32, kind="Internal").ap()
    ygd = nc.dram_tensor("slot_results", (NTL * TS, D), F32, kind="Internal").ap()

    with ExitStack() as top:
        ident = top.enter_context(nc.sbuf_tensor("ident", [P, P], F32))
        identb = top.enter_context(nc.sbuf_tensor("identb", [P, P], BF16))

        stage_project(nc, locals())
        stage_attend(nc, locals())
        W2 = top.enter_context(nc.sbuf_tensor("W2", [P, E, IC, D], F32))
        stage_join(nc, locals())
        W1 = top.enter_context(nc.sbuf_tensor("W1", [P, E, KD, I], F32))
        b1s = top.enter_context(nc.sbuf_tensor("b1s", [P, E, I], F32))
        b2s = top.enter_context(nc.sbuf_tensor("b2s", [P, E, D], F32))
        owner_i = top.enter_context(nc.sbuf_tensor("owner_i", [P, NTL], mybir.dt.int32))
        slot = [top.enter_context(nc.sbuf_tensor(f"slot{r}", [P, NT], mybir.dt.int32)) for r in range(2)]
        share = [top.enter_context(nc.sbuf_tensor(f"share{r}", [P, NT], F32)) for r in range(2)]
        ln_cols = top.enter_context(nc.sbuf_tensor("ln_cols", [P, 2, E, KD], F32))
        stage_route(nc, locals())
        stage_scatter(nc, locals())
        stage_experts(nc, locals())
        stage_finish(nc, locals())


def opener(nc, ctx):
    return (lambda n, s, d: ctx.enter_context(nc.sbuf_tensor(n, s, d)),
            lambda n, s, d: ctx.enter_context(nc.psum_tensor(n, s, d)),
            lambda n: ctx.enter_context(nc.semaphore(n)))


def stage_project(nc, a):
    x, Wq, Wk, Wv, qd, kd, vd = (a[n] for n in ("x", "Wq", "Wk", "Wv", "qd", "kd", "vd"))
    NB, CH, KD, G, D, ident, identb = (a[n] for n in ("NB", "CH", "KD", "G", "D", "ident", "identb"))
    MC = 2 * D // P
    ITEMS = 2 * MC
    with ExitStack() as ctx:
        sb, ps, sem = opener(nc, ctx)
        wraw = sb("wraw", [P, KD, 2, 2 * D], F32)
        wqk = sb("wqk", [P, KD, 2, 2 * D], F32)
        wv = sb("wv", [P, KD, D], F32)
        xs = sb("xs", [P, TPC, D], F32)
        xT = sb("xT", [P, KD, TC], F32)
        parts = sb("parts", [P, 4, 3, TC], BF16)
        rest = sb("rest", [P, 4, TC], F32)
        vst = sb("vst", [P, G, TPC, 2, 32], F32)
        pxT = [ps(f"pxT{i}", [P, TC], F32) for i in range(KD)]
        pj = [ps(f"pj{i}", [P, TC], F32) for i in range(4)]
        pv = [ps(f"pv{i}", [P, 2, D], F32) for i in range(2)]
        names = ("w_loaded", "zeroed", "ident_ready", "identb_ready", "wqk_ready", "vst_preset", "x_loaded",
                 "x_turned", "xT_ready", "proj_ready", "hi_ready", "rest_ready", "mid_ready", "lo_ready",
                 "v_ready", "vst_ready", "v_stored")
        (w_loaded, zeroed, ident_ready, identb_ready, wqk_ready, vst_preset, x_loaded, x_turned, xT_ready,
         proj_ready, hi_ready, rest_ready, mid_ready, lo_ready, v_ready, vst_ready,
         v_stored) = (sem(n) for n in names)
        parts_stored = [sem(f"parts_stored{i}") for i in range(4)]
        gate_pool = sem("gate_pool")
        block = ctx.enter_context(nc.Block())

        @block.sync
        def _(sp):
            for s in (x_turned, xT_ready, v_stored, v_ready, vst_ready, rest_ready, lo_ready,
                      *parts_stored):
                sp.sem_inc(s, 1)
            sp.dma_start(wraw[:, :, 0, :], Wq.rearrange("(k p) f -> p k f", p=P)).then_inc(w_loaded, 16)
            sp.dma_start(wraw[:, :, 1, :], Wk.rearrange("(k p) f -> p k f", p=P)).then_inc(w_loaded, 16)
            sp.dma_start(wv[:], Wv.rearrange("(k p) f -> p k f", p=P)).then_inc(w_loaded, 16)

            def load_x(n):
                sp.dma_start(xs[:], x.rearrange("b (c j p) d -> (b c) p j d", j=TPC, p=P)[n]).then_inc(x_loaded, 16)

            load_x(0)
            with sp.Fori(0, NB) as b:
                with sp.Fori(0, CH) as c:
                    n = b * CH + c
                    sp.wait_ge(x_turned, n + 2)
                    load_x((n + 1) % (NB * CH))
                    for i in range(ITEMS):
                        sp.wait_ge(lo_ready, n * ITEMS + i + 2)
                        if i < MC:
                            dst = qd.rearrange("(b g) s c r t -> b c g r s t", b=NB)
                        else:
                            dst = kd.rearrange("(b g) s r (c t) -> b c g r s t", b=NB, c=CH)
                        for h in range(2):
                            g = 2 * (i % MC) + h
                            sp.dma_start(
                                dst[b, c, g], parts[64 * h:64 * h + 64, i % 4, :, :]).then_inc(parts_stored[i % 4], 16)
                    sp.wait_ge(vst_ready, 4 * (n + 1) + 1)
                    sp.dma_start(vd.rearrange("(b g) p (c k) f -> b c p g (k f)", b=NB, c=CH)[b, c],
                                 vst[:].rearrange("p g k h f -> p g (k h f)")).then_inc(v_stored, 16)
            for stored in parts_stored:
                sp.wait_ge(stored, 32 * NB * CH * (ITEMS // 4) + 1)
            sp.wait_ge(v_stored, 16 * NB * CH + 1)
            sp.wait_ge(x_loaded, 16 * (NB * CH + 1))

        @block.gpsimd
        def _(pool):
            nc.gpsimd.memset(ident[:], 0.0).then_inc(zeroed, 1)
            nc.gpsimd.memset(vst[:], 0.0).then_inc(zeroed, 1)
            pool.wait_ge(zeroed, 2)
            nc.gpsimd.affine_select(out=ident[:], in_=ident[:], compare_op=ALU.not_equal, fill=1.0, base=0,
                                    pattern=[[-1, P]], channel_multiplier=1).then_inc(ident_ready, 1)
            nc.gpsimd.memset(vst[:, :, :, :, HD:HD + 1], 1.0).then_inc(vst_preset, 1)
            pool.wait_ge(ident_ready, 1)
            nc.gpsimd.tensor_copy(identb[:], ident[:]).then_inc(identb_ready, 1)
            with pool.Fori(0, NB * CH) as n:
                for i in range(ITEMS):
                    pool.wait_ge(rest_ready, n * ITEMS + i + 2)
                    pool.sem_inc(gate_pool, 1)
                    nc.gpsimd.tensor_copy(parts[:, i % 4, 1, :], rest[:, i % 4, :]).then_inc(mid_ready, 1)

        @block.scalar
        def _(act):
            with act.Fori(0, NB * CH) as n:
                act.wait_ge(x_turned, n + 2)
                act.wait_ge(v_ready, 2 * n + 1)
                for k in range(KD):
                    nc.scalar.copy(xT[:, k, :], pxT[k][:]).then_inc(xT_ready, 1)
                for i in range(ITEMS):
                    act.wait_ge(proj_ready, n * ITEMS + i + 1)
                    act.wait_ge(parts_stored[i % 4], 32 * (n * (ITEMS // 4) + i // 4) + 1)
                    nc.scalar.copy(parts[:, i % 4, 0, :], pj[i % 4][:]).then_inc(hi_ready, 1)
                act.wait_ge(v_stored, 16 * n + 1)
                act.wait_ge(vst_preset, 1)
                for j in range(TPC):
                    act.wait_ge(v_ready, 2 * n + j // 2 + 2)
                    nc.scalar.copy(vst[:, :, j, :, 0:HD],
                                   pv[j // 2][:, j % 2, :].rearrange("p (g h d) -> p g h d", h=2, d=HD)
                                   ).then_inc(vst_ready, 1)

        @block.tensor
        def _(pe):
            pe.wait_ge(ident_ready, 1)
            pe.wait_ge(wqk_ready, 2 * KD)
            with pe.Fori(0, NB * CH) as n:
                pe.wait_ge(x_loaded, 16 * (n + 1))
                pe.wait_ge(xT_ready, KD * n + 1)
                for k in range(KD):
                    for j in range(TPC):
                        mm = nc.tensor.transpose(pxT[k][:, j * P:(j + 1) * P], xs[:, j, k * P:(k + 1) * P], ident[:])
                mm.then_inc(x_turned, 1)
                pe.wait_ge(xT_ready, KD * (n + 1) + 1)
                for i in range(ITEMS):
                    pe.wait_ge(rest_ready, n * ITEMS + max(i - 3, 0) + 1)
                    for k in range(KD):
                        mm = nc.tensor.matmul(pj[i % 4][:], wqk[:, k, i // MC, (i % MC) * P:(i % MC + 1) * P],
                                              xT[:, k, :], start=(k == 0), stop=(k == KD - 1))
                    mm.then_inc(proj_ready, 1)
                pe.wait_ge(vst_ready, TPC * n + 1)
                for j in range(TPC):
                    for k in range(KD):
                        mm = nc.tensor.matmul(pv[j // 2][:, j % 2, :], xT[:, k, j * P:(j + 1) * P], wv[:, k, :],
                                              start=(k == 0), stop=(k == KD - 1), skip_group_check=True)
                    if j % 2 == 1:
                        mm.then_inc(v_ready, 1)

        @block.vector
        def _(dve):
            dve.wait_ge(w_loaded, 48)
            for k in range(KD):
                for m in range(2):
                    nc.vector.tensor_copy(
                        wqk[:, k, m, :].rearrange("p (g d u) -> p g d u", d=HD, u=UNITS),
                        wraw[:, k, m, :].rearrange("p (g u d) -> p g d u", d=HD, u=UNITS)).then_inc(wqk_ready, 1)
            with dve.Fori(0, NB * CH) as n:
                for i in range(ITEMS + 1):
                    if i < ITEMS:
                        dve.wait_ge(lo_ready, n * ITEMS + max(i - 3, 0) + 1)
                        dve.wait_ge(hi_ready, n * ITEMS + i + 1)
                        nc.vector.tensor_tensor(rest[:, i % 4, :], pj[i % 4][:], parts[:, i % 4, 0, :],
                                                ALU.subtract).then_inc(rest_ready, 1)
                    if i > 0:
                        j = i - 1
                        dve.wait_ge(mid_ready, n * ITEMS + j + 1)
                        nc.vector.tensor_tensor(parts[:, j % 4, 2, :], rest[:, j % 4, :], parts[:, j % 4, 1, :],
                                                ALU.subtract).then_inc(lo_ready, 1)


def stage_attend(nc, a):
    qd, kd, vd, od = (a[n] for n in ("qd", "kd", "vd", "od"))
    NB, CH, G, KB, S, identb = (a[n] for n in ("NB", "CH", "G", "KB", "S", "identb"))
    PAIRS = NB * G // 2
    RC = 2 * CH
    RS = RC * KB
    AHEAD = KB + 4
    CUT = 2 * KB - AHEAD
    SH = S // 2
    with ExitStack() as ctx:
        sb, ps, sem = opener(nc, ctx)
        Q = [sb(f"Q{i}", [KM, CH, UNITS, TC], BF16) for i in range(2)]
        K = [sb(f"K{i}", [KM, UNITS, S], BF16) for i in range(2)]
        V = [sb(f"V{i}", [P, KB, 2, 32], F32) for i in range(2)]
        probs = sb("probs", [P, 2 * UNITS, TC], F32)
        att = [sb(f"att{i}", [P, TC], F32) for i in range(2)]
        half_max = [sb(f"half_max{i}", [P, 2, 16], F32) for i in range(2)]
        row_max = sb("row_max", [P, 16], F32)
        max_rest = sb("max_rest", [P, 16], F32)
        max_parts = sb("max_parts", [P, 3, 16], BF16)
        max_rows = [sb(f"max_rows{i}", [48, P], BF16) for i in range(2)]
        scores = ps("scores", [P, S], F32)
        scoresT = [ps(f"scoresT{i}", [P, TC], F32) for i in range(3)]
        attT = ps("attT", [P, TC], F32)
        names = ("ones_set", "parts_chain", "max_parts_ready", "max_rows_turned", "max_rows_copied",
                 "scoresA_ready", "scoresB_ready", "maxA_done", "maxB_done", "scoresT_ready", "exp_done",
                 "pv_done", "att_copied")
        (ones_set, parts_chain, max_parts_ready, max_rows_turned, max_rows_copied,
         scoresA_ready, scoresB_ready, maxA_done, maxB_done, scoresT_ready, exp_done,
         pv_done, att_copied) = (sem(n) for n in names)
        qk_loaded = [sem(f"qk_loaded{i}") for i in range(2)]
        v_loaded = [sem(f"v_loaded{i}") for i in range(2)]
        max_loaded = [sem(f"max_loaded{i}") for i in range(2)]
        att_stored = [sem(f"att_stored{i}") for i in range(2)]
        first_loaded = sem("first_loaded")
        gate_pe, gate_pool, zeros_set, zeroed = sem("gate_pe"), sem("gate_pool"), sem("zeros_set"), sem("slots_zeroed")
        xgd, TS, NTL, D = (a[n] for n in ("xgd", "TS", "NTL", "D"))
        ZT = 2
        NZ = NTL // ZT
        zeros = sb("zeros", [P, ZT * TS // P * D], F32)
        QKD = 16 * 2 * len(Q_PARTS)
        MXD = 16 * 3
        turned = [s[0:48, 0:P // 2].bitcast(BF16) for s in scoresT]

        def turn_bank(lc):
            return 4 * (lc * KB + CUT + 2) % 3

        block = ctx.enter_context(nc.Block())

        @block.sync
        def _(sp):
            for s in (pv_done, att_copied, maxA_done, maxB_done, *max_loaded, *att_stored):
                sp.sem_inc(s, 1)
            def load_qk(p, g, c=0, u=0):
                for i in range(len(Q_PARTS)):
                    sp.dma_start(Q[p][16 * i:16 * i + 16, c:].rearrange("d c u t -> d c (u t)"),
                                 qd.rearrange("g s c (d u) t -> g s d c (u t)", u=UNITS)[g, Q_PARTS[i]][:, c:]
                                 ).then_inc(qk_loaded[p], 16)
                    sp.dma_start(K[p][16 * i:16 * i + 16, u:],
                                 kd.rearrange("g s (d u) t -> g s d u t", u=UNITS)[g, K_PARTS[i]][:, u:]
                                 ).then_inc(qk_loaded[p], 16)

            def load_v(p, g):
                sp.dma_start(V[p][:], vd.rearrange("g p k (h f) -> g p k h f", h=2)[g]).then_inc(v_loaded[p], 16)

            def load_max(done, lc):
                p, c = lc // CH % 2, lc % CH
                sp.wait_ge(max_rows_copied, done)
                for s in range(3):
                    sp.dma_start(Q[p][KR + s:KR + s + 1, c, :, :].rearrange("o u (t q) -> o (u t) q", q=P),
                                 max_rows[lc % 2][16 * s:16 * s + 16, :]
                                 ).then_inc(max_loaded[lc % 2], 16)

            for i in range(len(Q_PARTS)):
                sp.dma_start(Q[0][16 * i:16 * i + 16, 0],
                             qd.rearrange("g s c (d u) t -> g s d c u t", u=UNITS)[0, Q_PARTS[i], :, 0]
                             ).then_inc(first_loaded, 16)
                sp.dma_start(K[0][16 * i:16 * i + 16, 0],
                             kd.rearrange("g s (d u) t -> g s d u t", u=UNITS)[0, K_PARTS[i], :, 0]
                             ).then_inc(first_loaded, 16)
            load_qk(0, 0, c=1, u=1)
            load_v(0, 0)
            load_max(1, 0)
            with sp.Fori(0, PAIRS) as it:
                def store_att(lc):
                    sp.wait_ge(att_copied, it * RC + lc + 2)
                    sp.dma_start(od.rearrange("(i p) r (c t) -> i p c r t", p=2, c=CH)[it, lc // CH, lc % CH],
                                 att[lc % 2][:]).then_inc(att_stored[lc % 2], 16)

                sp.wait_ge(pv_done, it * RS + 1)
                load_qk(1, it * 2 + 1)
                load_v(1, it * 2 + 1)
                for lc in range(RC):
                    if lc > 0:
                        store_att(lc - 1)
                    if lc == CH:
                        load_qk(0, (it * 2 + 2) % (NB * G))
                        load_v(0, (it * 2 + 2) % (NB * G))
                    load_max(it * RC + lc + 2, lc + 1)
                store_att(RC - 1)
            for p in range(2):
                sp.wait_ge(att_stored[p], 16 * PAIRS * CH + 1)
                sp.wait_ge(v_loaded[p], 16 * (PAIRS + (p == 0)))
                sp.wait_ge(max_loaded[p], MXD * (PAIRS * CH + (p == 0)) + 1)

        @block.gpsimd
        def _(pool):
            for i in range(2):
                nc.gpsimd.memset(K[i][KR:KM], 1.0).then_inc(ones_set, 1)
            pool.wait_ge(ones_set, 2)
            pool.wait_ge(max_loaded[0], MXD + 1)
            pool.sem_inc(gate_pool, 1)
            nc.gpsimd.memset(zeros[:], 0.0).then_inc(zeros_set, 1)
            pool.wait_ge(zeros_set, 1)
            with pool.Fori(0, NZ) as n:
                pool.dma_start(xgd.rearrange("(n p j) d -> n p (j d)", n=NZ, p=P)[n], zeros[:]).then_inc(zeroed, 16)
            pool.wait_ge(zeroed, 16 * NZ)

        @block.tensor
        def _(pe):
            def score_rows(item, lc, i):
                p, c, u, t = lc // CH % 2, lc % CH, i // 4, i % 4
                lhsT = Q[p][0:KR, c, u, t * P:(t + 1) * P]
                for h, ready, used in ((0, scoresA_ready, maxA_done), (1, scoresB_ready, maxB_done)):
                    pe.wait_ge(used, item + 1)
                    for k in range(2):
                        at = h * SH + k * TC
                        mm = nc.tensor.matmul(scores[:, at:at + TC], lhsT, K[p][0:KR, u, at:at + TC],
                                              start=True, stop=True)
                    mm.then_inc(ready, 1)

            def turn_maxima(done, bank, used):
                pe.wait_ge(max_parts_ready, done)
                if used is not None:
                    pe.wait_ge(exp_done, used)
                pe.sem_inc(gate_pe, 1)
                nc.tensor.transpose(turned[bank], max_parts[:].rearrange("p s i -> p (s i)"), identb[:]
                                    ).then_inc(max_rows_turned, 1)

            pe.wait_ge(first_loaded, QKD)
            for i in range(AHEAD):
                if i == 4:
                    pe.wait_ge(qk_loaded[0], QKD)
                if i == KB + 2:
                    turn_maxima(1, 0, None)
                score_rows(i, i // KB, i % KB)
            pe.wait_ge(max_rows_copied, 1)
            pe.wait_ge(ones_set, 2)
            with pe.Fori(0, PAIRS) as it:
                for lc in range(RC):
                    p, c = lc // CH, lc % CH
                    for kb in range(KB):
                        ls = lc * KB + kb
                        ahead = (ls + AHEAD) % RS
                        item = it * RS + ls + AHEAD
                        if kb == 0:
                            pe.wait_ge(max_loaded[lc % 2], MXD * (it * CH + lc // 2 + 1) + 1)
                            if c == 0:
                                pe.wait_ge(v_loaded[p], 16 * (it + 1))
                        if ahead == CH * KB:
                            pe.wait_ge(qk_loaded[1], QKD * (it + 1))
                        if ahead == 0:
                            pe.wait_ge(qk_loaded[0], QKD * (it + 2))
                        if kb == CUT + 2:
                            pe.wait_ge(max_rows_copied, it * RC + lc + 2)

                        def scores_of(u):
                            i = 4 * ls + u
                            if i >= 3:
                                pe.wait_ge(exp_done, it * 4 * RS + i - 2)
                            nc.tensor.matmul(scoresT[i % 3][:], K[p][:, u, kb * P:(kb + 1) * P], Q[p][:, c, u, :],
                                             start=True, stop=True).then_inc(scoresT_ready, 1)

                        def weigh(s):
                            wp, wk = s // KB // CH, s % KB
                            pe.wait_ge(exp_done, it * 4 * RS + 4 * s + 4)
                            if wk == 0:
                                pe.wait_ge(att_copied, it * RC + s // KB + 1)
                            for u in range(UNITS):
                                mm = nc.tensor.matmul(attT[32 * u:32 * u + 32, :], V[wp][:, wk, u // 2, :],
                                                      probs[:, 4 * (s % 2) + u, :],
                                                      start=(wk == 0), stop=(wk == KB - 1), skip_group_check=True)
                            mm.then_inc(pv_done, 1)

                        for u in range(3):
                            scores_of(u)
                        score_rows(item, ahead // KB, ahead % KB)
                        scores_of(3)
                        if kb == CUT + 1:
                            turn_maxima(it * RC + lc + 2, turn_bank(lc), it * 4 * RS + 4 * ls + 2)
                        if ls > 0:
                            weigh(ls - 1)
                weigh(RS - 1)

        @block.scalar
        def _(act):
            with act.Fori(0, PAIRS) as it:
                for ls in range(RS):
                    act.wait_ge(pv_done, it * RS + max(ls - 1, 0) + 1)
                    for u in range(UNITS):
                        i = 4 * ls + u
                        act.wait_ge(scoresT_ready, it * 4 * RS + i + 1)
                        nc.scalar.activation(probs[:, i % 8, :], scoresT[i % 3][:], ACT.Exp,
                                             scale=HD ** -0.5).then_inc(exp_done, 1)

        @block.vector
        def _(dve):
            def maxima(item, lc, i, between=None):
                for h, ready, done in ((0, scoresA_ready, maxA_done), (1, scoresB_ready, maxB_done)):
                    if h == 1 and between is not None:
                        copy_rows(*between)
                    dve.wait_ge(ready, item + 1)
                    nc.vector.tensor_reduce(half_max[lc % 2][:, h, i:i + 1], scores[:, h * SH:(h + 1) * SH],
                                            AX.X, ALU.max).then_inc(done, 1)

            def cut_maxima(done, lc):
                hm, chain = half_max[lc % 2], 4 * (done - 1)
                nc.vector.tensor_tensor(row_max[:], hm[:, 0, :], hm[:, 1, :], ALU.max).then_inc(parts_chain, 1)
                dve.wait_ge(parts_chain, chain + 1)
                nc.vector.tensor_scalar(max_parts[:, 0, :], row_max[:], -1.0, None, ALU.mult).then_inc(parts_chain, 1)
                dve.wait_ge(parts_chain, chain + 2)
                nc.vector.scalar_tensor_tensor(max_rest[:], row_max[:], -1.0, max_parts[:, 0, :],
                                               ALU.mult, ALU.subtract).then_inc(parts_chain, 1)
                dve.wait_ge(parts_chain, chain + 3)
                nc.vector.tensor_copy(max_parts[:, 1, :], max_rest[:]).then_inc(parts_chain, 1)
                dve.wait_ge(parts_chain, chain + 4)
                nc.vector.tensor_tensor(max_parts[:, 2, :], max_rest[:], max_parts[:, 1, :],
                                        ALU.subtract).then_inc(max_parts_ready, 1)

            def copy_rows(done, lc, loaded, bank):
                dve.wait_ge(max_rows_turned, done)
                dve.wait_ge(max_loaded[lc % 2], loaded + 1)
                nc.vector.tensor_copy(max_rows[lc % 2][:], turned[bank]).then_inc(max_rows_copied, 1)

            for i in range(AHEAD):
                if i == KB:
                    dve.wait_ge(maxA_done, KB + 1)
                    dve.wait_ge(maxB_done, KB + 1)
                    cut_maxima(1, 0)
                maxima(i, i // KB, i % KB, (1, 0, 0, 0) if i == KB + 2 else None)
            with dve.Fori(0, PAIRS) as it:
                def copy_att(lc):
                    dve.wait_ge(pv_done, it * RS + (lc + 1) * KB + 1)
                    dve.wait_ge(att_stored[lc % 2], 16 * (it * CH + lc // 2) + 1)
                    nc.vector.tensor_copy(att[lc % 2][:], attT[:]).then_inc(att_copied, 1)

                for lc in range(RC):
                    for kb in range(KB):
                        ahead = (lc * KB + kb + AHEAD) % RS
                        item = it * RS + lc * KB + kb + AHEAD
                        between = None
                        if kb == CUT:
                            dve.wait_ge(maxA_done, item + 1)
                            dve.wait_ge(maxB_done, item + 1)
                            cut_maxima(it * RC + lc + 2, lc + 1)
                        if kb == 1 and lc > 0:
                            copy_att(lc - 1)
                        if kb == CUT + 1:
                            between = (it * RC + lc + 2, lc + 1, MXD * (it * CH + (lc + 1) // 2), turn_bank(lc))
                        maxima(item, ahead // KB, ahead % KB, between)
                copy_att(RC - 1)


class Chain:

    def __init__(self, eng, sem, base=0):
        self.eng, self.sem, self.base, self.n = eng, sem, base, 0

    def add(self, ins):
        ins.then_inc(self.sem, 1)
        self.n += 1

    def wait(self):
        self.eng.wait_ge(self.sem, self.base + self.n)


def stage_join(nc, a):
    x, Wo, od, x1d, xhd, lgd = (a[n] for n in ("x", "Wo", "od", "x1d", "xhd", "lgd"))
    lams = [a[n] for n in ("lq1", "lk1", "lq2", "lk2")]
    gamma, beta, rn_g, rn_b, router_w, router_b = (a[n] for n in ("gamma", "beta", "rn_g", "rn_b", "router_w", "router_b"))
    NB, CH, KD, G, D, E, ident = (a[n] for n in ("NB", "CH", "KD", "G", "D", "E", "ident"))
    NU = G * UNITS
    TPC = 8
    TC = TPC * P
    CH = a["S"] // TC
    NL = 4 + 1 + 3 + 4
    with ExitStack() as ctx:
        sb, ps, sem = opener(nc, ctx)
        wo = sb("wo", [P, KD, D], F32)
        lam_in = sb("lam_in", [P, 4, HD], F32)
        lam_mul = sb("lam_mul", [P, 2, HD], F32)
        lam_sum = sb("lam_sum", [P, 2], F32)
        lam_exp = sb("lam_exp", [P, 2], F32)
        lam_neg = sb("lam_neg", [P, 1], F32)
        coef = sb("coef", [P, NU], F32)
        gam = sb("gam", [P, D], F32)
        bet = sb("bet", [P, D], F32)
        rnb = sb("rnb", [P, D], F32)
        rw_all = sb("rw_all", [P, E, D], F32)
        rbias = sb("rbias", [P, E], F32)
        rbias_in = sb("rbias_in", [P, E], F32)
        rw_rows = sb("rw_rows", [E, D], F32)
        rg_rows = sb("rg_rows", [E, D], F32)
        rw_T = sb("rw_T", [P, KD, E], F32)
        xs = sb("join_x", [P, TPC, D], F32)
        xb = sb("join_xb", [P, TPC, D], F32)
        heads = sb("heads", [P, G, TC], F32)
        rcp = sb("rcp", [P, TPC, NU], F32)
        rcc = sb("rcc", [P, TPC, NU], F32)
        scaled = sb("scaled", [P, 2, NU, HD], F32)
        att = sb("join_att", [P, TPC, D], F32)
        attT = sb("join_attT", [P, TPC, D], F32)
        zg = sb("zg", [P, TPC, D], F32)
        zs = sb("zs", [P, TPC, D], F32)
        x1 = sb("x1s", [P, TPC, D], F32)
        xh = sb("join_xh", [P, TPC, D], F32)
        xhT = sb("join_xhT", [P, KD, TC], F32)
        lgs = sb("lgs", [P, TPC, E], F32)
        st = [sb(f"st{i}", [P, TPC, 6], F32) for i in range(3)]
        mv = [sb(f"mv{i}", [P, TPC, 2], F32) for i in range(3)]
        rs = [sb(f"rs{i}", [P, TPC], F32) for i in range(3)]
        ve = [sb(f"ve{i}", [P, TPC], F32) for i in range(3)]
        minus_half = sb("minus_half", [P, TPC], F32)
        token_major = [ps(f"token_major{i}", [P, NU, 32], F32) for i in range(2)]
        turn = [ps(f"turn{i}", [P, 512], F32) for i in range(2)]
        prod = [ps(f"prod{i}", [P, 512], F32) for i in range(2)]
        names = ("consts_loaded", "setup_chain", "coef_ones", "lam_summed", "lam_exped", "coef_ready", "rw_scaled",
                 "rw_turned", "rw_ready", "rbias_ready", "in_loaded", "x_used", "turned", "scaled_ready", "att_ready",
                 "att_turned", "attT_ready", "y_ready", "z_ready", "zs_ready", "ln_chain", "x1_ready",
                 "xh_ready", "xh_turned", "xhT_ready", "logits_ready", "lgs_ready", "out_stored")
        (consts_loaded, setup_chain, coef_ones, lam_summed, lam_exped, coef_ready, rw_scaled, rw_turned, rw_ready,
         rbias_ready, in_loaded, x_used, turned, scaled_ready, att_ready, att_turned, attT_ready, y_ready, z_ready,
         zs_ready, ln_chain, x1_ready, xh_ready, xh_turned, xhT_ready, logits_ready, lgs_ready,
         out_stored) = (sem("j_" + n) for n in names)
        W2, w2, w2_loaded = a["W2"], a["w2"], sem("j_w2_loaded")
        half_set, j_gate_pool, j_gate_dve = sem("j_half_set"), sem("j_gate_pool"), sem("j_gate_dve")
        var_ready, ve_ready, rs_ready = ([sem(f"j_{n}{i}") for i in range(3)] for n in ("var", "ve", "rs"))
        NC = NB * CH
        block = ctx.enter_context(nc.Block())

        @block.sync
        def _(sp):
            for s in (turned, x_used, scaled_ready, zs_ready, att_ready, attT_ready, z_ready,
                      lgs_ready, xhT_ready, out_stored, logits_ready):
                sp.sem_inc(s, 1)
            def row(v, n, parts=P):
                return v.rearrange("(o d) -> o d", o=1).to_broadcast((parts, n))
            consts = [(wo[:], Wo.rearrange("(k p) f -> p k f", p=P)), (rw_rows[:], router_w),
                      (gam[:], row(gamma, D)), (bet[:], row(beta, D)), (rnb[:], row(rn_b, D)),
                      (rbias_in[:], row(router_b, E)), (rg_rows[:], row(rn_g, D, E)),
                      (rw_all[:].rearrange("p e d -> p (e d)"),
                       router_w.rearrange("(o e) d -> o (e d)", o=1).to_broadcast((P, E * D)))]
            consts += [(lam_in[:, i, :], row(l, HD)) for i, l in enumerate(lams)]
            assert len(consts) == NL
            for dst, src in consts:
                sp.dma_start(dst, src).then_inc(consts_loaded, 16)

            def load_chunk(n):
                b, c = n // CH, n % CH
                sp.dma_start(heads[:], od.rearrange("(b g) p (c t) -> b c p g t", b=NB, c=CH)[b, c]
                             ).then_inc(in_loaded, 16)
                sp.dma_start(xs[:], x.rearrange("b (c j p) d -> b c p j d", j=TPC, p=P)[b, c]
                             ).then_inc(in_loaded, 16)

            load_chunk(0)
            for e in range(E):
                sp.dma_start(W2[:, e], w2[e].rearrange("(c p) d -> p c d", p=P)).then_inc(w2_loaded, 16)
            with sp.Fori(0, NB) as b:
                with sp.Fori(0, CH) as c:
                    n = b * CH + c
                    sp.wait_ge(turned, TPC * (n + 1) + 1)
                    sp.wait_ge(x_used, TPC * (n + 1) + 1)
                    load_chunk((n + 1) % NC)
                    sp.wait_ge(x1_ready, TPC * (n + 1))
                    sp.dma_start(x1d.rearrange("(b c j p) d -> b c p j d", b=NB, j=TPC, p=P)[b, c], x1[:]
                                 ).then_inc(out_stored, 16)
                    sp.wait_ge(xh_ready, TPC * (n + 1))
                    sp.dma_start(xhd.rearrange("(b c j p) d -> b c p j d", b=NB, j=TPC, p=P)[b, c], xh[:]
                                 ).then_inc(out_stored, 16)
                    sp.wait_ge(lgs_ready, TPC * (n + 1) + 1)
                    sp.dma_start(lgd.rearrange("p (b c j) e -> b c p j e", b=NB, c=CH)[b, c], lgs[:]
                                 ).then_inc(out_stored, 16)
            sp.wait_ge(out_stored, 48 * NC + 1)
            sp.wait_ge(in_loaded, 32 * (NC + 1))
            sp.wait_ge(w2_loaded, 16 * E)

        @block.gpsimd
        def _(pool):
            nc.gpsimd.memset(coef[:], 1.0).then_inc(coef_ones, 1)
            nc.gpsimd.memset(minus_half[:], -0.5).then_inc(half_set, 1)
            pool.wait_ge(half_set, 1)
            pool.wait_ge(consts_loaded, 16 * NL)
            with pool.Fori(0, NC) as n:
                pool.wait_ge(in_loaded, 32 * (n + 1))
                pool.wait_ge(zs_ready, TPC * n + 1)
                for j in range(TPC):
                    nc.gpsimd.tensor_tensor(xb[:, j, :], xs[:, j, :], bet[:], ALU.add).then_inc(x_used, 1)
                for j in range(TPC):
                    pool.wait_ge(scaled_ready, TPC * n + j + 2)
                    s = scaled[:, j % 2].rearrange("p (h c) d -> p h c d", c=2)
                    nc.gpsimd.tensor_tensor(att[:, j, :].rearrange("p (h d) -> p h d", d=HD), s[:, :, 0, :],
                                            s[:, :, 1, :], ALU.add).then_inc(att_ready, 1)
                def rsqrt(i, tiles):
                    pool.wait_ge(var_ready[i], TPC * n + tiles.stop)
                    pool.sem_inc(j_gate_pool, 1)
                    nc.gpsimd.tensor_scalar(ve[i][:, tiles.start:tiles.stop], mv[i][:, tiles.start:tiles.stop, 1],
                                            EPS, None, ALU.add).then_inc(ve_ready[i], 1)
                    pool.wait_ge(ve_ready[i], TPC // len(tiles) * n + tiles.stop // len(tiles))
                    nc.gpsimd.tensor_tensor(rs[i][:, tiles.start:tiles.stop], ve[i][:, tiles.start:tiles.stop],
                                            minus_half[:, tiles.start:tiles.stop], ALU.pow).then_inc(rs_ready[i], 1)

                for i in range(3):
                    rsqrt(i, range(TPC))

        @block.scalar
        def _(act):
            act.wait_ge(lam_summed, 1)
            nc.scalar.activation(lam_exp[:], lam_sum[:], ACT.Exp).then_inc(lam_exped, 1)
            with act.Fori(0, NC) as n:
                for j in range(TPC):
                    act.wait_ge(att_turned, TPC * n + j + 1)
                    nc.scalar.copy(attT[:, j, :], turn[j % 2][:, 0:D]).then_inc(attT_ready, 1)
                act.wait_ge(out_stored, 48 * n + 1)
                act.wait_ge(logits_ready, TPC * n + 1)
                for j in range(TPC):
                    act.wait_ge(xh_turned, TPC * n + j + 1)
                    nc.scalar.copy(xhT[:, :, j * P:(j + 1) * P],
                                   turn[j % 2][:, 0:D].rearrange("p (k t) -> p k t", k=KD)).then_inc(xhT_ready, 1)

        @block.tensor
        def _(pe):
            pe.wait_ge(rw_scaled, 1)
            for k in range(KD):
                mm = nc.tensor.transpose(turn[0][:, k * E:(k + 1) * E], rw_rows[:, k * P:(k + 1) * P], ident[0:E, 0:E])
            mm.then_inc(rw_turned, 1)
            pe.wait_ge(rw_ready, 1)
            with pe.Fori(0, NC) as n:
                pe.wait_ge(in_loaded, 32 * (n + 1))
                for j in range(TPC):
                    pe.wait_ge(scaled_ready, TPC * n + max(j - 1, 0) + 1)
                    for g in range(G):
                        mm = nc.tensor.transpose(token_major[j % 2][:, g * UNITS:(g + 1) * UNITS, :],
                                                 heads[:, g, j * P:(j + 1) * P], ident[:])
                    mm.then_inc(turned, 1)
                pe.wait_ge(xhT_ready, TPC * n + 1)
                pe.wait_ge(lgs_ready, TPC * n + 1)

                def turn_att(j):
                    pe.wait_ge(att_ready, TPC * n + j + 2)
                    pe.wait_ge(attT_ready, TPC * n + max(j - 1, 0) + 1)
                    for k in range(KD):
                        mm = nc.tensor.transpose(turn[j % 2][:, k * P:(k + 1) * P], att[:, j, k * P:(k + 1) * P],
                                                 ident[:])
                    mm.then_inc(att_turned, 1)

                def turn_xh(j):
                    pe.wait_ge(xh_ready, TPC * n + j + 1)
                    pe.wait_ge(xhT_ready, TPC * n + max(j - 1, 0) + 1)
                    for k in range(KD):
                        mm = nc.tensor.transpose(turn[j % 2][:, k * P:(k + 1) * P], xh[:, j, k * P:(k + 1) * P],
                                                 ident[:])
                    mm.then_inc(xh_turned, 1)

                turn_att(0)
                for j in range(TPC):
                    if j + 1 < TPC:
                        turn_att(j + 1)
                    pe.wait_ge(attT_ready, TPC * n + j + 2)
                    pe.wait_ge(z_ready, TPC * n + max(j - 1, 0) + 1)
                    for k in range(KD):
                        mm = nc.tensor.matmul(prod[j % 2][:, 0:D], attT[:, j, k * P:(k + 1) * P], wo[:, k, :],
                                              start=(k == 0), stop=(k == KD - 1))
                    mm.then_inc(y_ready, 1)
                pe.wait_ge(z_ready, TPC * (n + 1) + 1)
                turn_xh(0)
                for j in range(TPC):
                    if j + 1 < TPC:
                        turn_xh(j + 1)
                    pe.wait_ge(xhT_ready, TPC * n + j + 2)
                    pe.wait_ge(lgs_ready, TPC * n + max(j - 1, 0) + 1)
                    for k in range(KD):
                        mm = nc.tensor.matmul(prod[j % 2][:, 0:E], xhT[:, k, j * P:(j + 1) * P], rw_T[:, k, :],
                                              start=(k == 0), stop=(k == KD - 1))
                    mm.then_inc(logits_ready, 1)

        @block.vector
        def _(dve):
            setup = Chain(dve, setup_chain)
            dve.wait_ge(consts_loaded, 16 * NL)
            setup.add(nc.vector.tensor_tensor(lam_mul[:], lam_in[:, 0:4:2, :], lam_in[:, 1:4:2, :], ALU.mult))
            setup.wait()
            nc.vector.tensor_reduce(lam_sum[:], lam_mul[:], AX.X, ALU.add).then_inc(lam_summed, 1)
            dve.wait_ge(lam_exped, 1)
            setup.add(nc.vector.tensor_tensor(lam_neg[:], lam_exp[:, 1:2], lam_exp[:, 0:1], ALU.subtract))
            dve.wait_ge(coef_ones, 1)
            setup.wait()
            setup.add(nc.vector.tensor_scalar(lam_neg[:], lam_neg[:], LAMBDA_INIT, None, ALU.subtract))
            setup.wait()
            setup.add(nc.vector.tensor_scalar(coef[:, 1:NU:2], coef[:, 1:NU:2], lam_neg[:, 0:1], None, ALU.mult))
            setup.add(nc.vector.tensor_tensor(rw_all[:], rw_all[:], rnb[:].rearrange("p (o d) -> p o d", o=1)
                                              .to_broadcast((P, E, D)), ALU.mult))
            setup.wait()
            setup.add(nc.vector.tensor_reduce(rbias[:], rw_all[:], AX.X, ALU.add))
            nc.vector.tensor_tensor(rw_rows[:], rw_rows[:], rg_rows[:], ALU.mult).then_inc(rw_scaled, 1)
            setup.wait()
            setup.add(nc.vector.tensor_tensor(rbias[:], rbias[:], rbias_in[:], ALU.add))
            dve.wait_ge(rw_turned, 1)
            nc.vector.tensor_copy(rw_T[:].rearrange("p k e -> p (k e)"), turn[0][:, 0:KD * E]).then_inc(rw_ready, 1)
            setup.wait()

            LINKS = 5 * TPC
            with dve.Fori(0, NC) as n:
                chain = Chain(dve, ln_chain, n * LINKS)

                def layernorm(i, src, dst, done, before, tiles=range(TPC)):
                    for j in tiles:
                        before(j)
                        chain.add(nc.vector.bn_stats(st[i][:, j, :], src(j)))
                    chain.wait()
                    dve.sem_inc(j_gate_dve, 1)
                    for j in tiles:
                        nc.vector.bn_aggr(mv[i][:, j, :], st[i][:, j, :]).then_inc(var_ready[i], 1)
                    dve.wait_ge(var_ready[i], TPC * n + tiles[-1] + 1)
                    dve.wait_ge(rs_ready[i], TPC // len(tiles) * n + tiles.stop // len(tiles))
                    for j in tiles:
                        nc.vector.tensor_scalar(dst[:, j, :], src(j), mv[i][:, j, 0:1], rs[i][:, j:j + 1],
                                                ALU.subtract, ALU.mult).then_inc(done, 1)

                for j in range(TPC):
                    dve.wait_ge(turned, TPC * n + j + 2)
                    tm = token_major[j % 2]
                    chain.add(nc.vector.reciprocal(rcp[:, j, :], tm[:, :, HD]))
                    chain.wait()
                    chain.add(nc.vector.tensor_tensor(rcc[:, j, :], rcp[:, j, :], coef[:], ALU.mult))
                    chain.wait()
                    dve.wait_ge(att_ready, TPC * n + max(j - 1, 0) + 1)
                    nc.vector.tensor_tensor(scaled[:, j % 2], tm[:, :, 0:HD],
                                            rcc[:, j, :].rearrange("p (u o) -> p u o", o=1).to_broadcast((P, NU, HD)),
                                            ALU.mult).then_inc(scaled_ready, 1)
                for j in range(TPC):
                    dve.wait_ge(y_ready, TPC * n + j + 1)
                    y = prod[j % 2][:, 0:D]
                    chain.add(nc.vector.bn_stats(st[0][:, j, :], y))
                    chain.wait()
                    dve.sem_inc(j_gate_dve, 1)
                    nc.vector.bn_aggr(mv[0][:, j, :], st[0][:, j, :]).then_inc(var_ready[0], 1)
                    dve.wait_ge(var_ready[0], TPC * n + j + 1)
                    nc.vector.scalar_tensor_tensor(zg[:, j, :], y, mv[0][:, j, 0:1], gam[:], ALU.subtract, ALU.mult
                                                   ).then_inc(z_ready, 1)
                dve.wait_ge(z_ready, TPC * (n + 1) + 1)
                dve.wait_ge(rs_ready[0], n + 1)
                for j in range(TPC):
                    dve.wait_ge(x_used, TPC * n + j + 2)
                    nc.vector.scalar_tensor_tensor(zs[:, j, :], zg[:, j, :], rs[0][:, j:j + 1], xb[:, j, :],
                                                   ALU.mult, ALU.add).then_inc(zs_ready, 1)
                dve.wait_ge(out_stored, 48 * n + 1)
                layernorm(1, lambda j: zs[:, j, :], x1, x1_ready, lambda j: dve.wait_ge(zs_ready, TPC * n + j + 2))
                layernorm(2, lambda j: x1[:, j, :], xh, xh_ready, lambda j: dve.wait_ge(x1_ready, TPC * n + j + 1))
                for j in range(TPC):
                    dve.wait_ge(logits_ready, TPC * n + j + 2)
                    nc.vector.tensor_tensor(lgs[:, j, :], prod[j % 2][:, 0:E], rbias[:], ALU.add).then_inc(lgs_ready, 1)
                assert chain.n == LINKS, chain.n


def stage_route(nc, a):
    lgd, ln_g, ln_b, owner_i, ln_cols = (a[n] for n in ("lgd", "ln_g", "ln_b", "owner_i", "ln_cols"))
    NT, KD, IC, D, E, T, TS, NTL, ident = (a[n] for n in ("NT", "KD", "IC", "D", "E", "T", "TS", "NTL", "ident"))
    share, slot = a["share"], a["slot"]
    TM = T // TS
    with ExitStack() as ctx:
        sb, ps, sem = opener(nc, ctx)
        lg = sb("lg", [P, NT, E], F32)
        lg2 = sb("lg2", [P, NT, E], F32)
        order = sb("order", [P, E], F32)
        thr = sb("thr", [P, TM], F32)
        tau = sb("tau", [P, NTL], F32)
        tau_i = sb("tau_i", [P, NTL], mybir.dt.int32)
        upper = sb("upper", [P, P], F32)
        ones = sb("ones", [P, P], F32)
        pick = [sb(f"pick{i}", [P, NT, E], F32) for i in range(2)]
        rank = [sb(f"rank{i}", [P, NT, E], F32) for i in range(2)]
        hot = [sb(f"hot{i}", [P, NT, E], F32) for i in range(2)]
        best = [sb(f"best{i}", [P, NT], F32) for i in range(2)]
        first = [sb(f"first{i}", [P, NT], F32) for i in range(2)]
        gap = sb("gap", [P, NT], F32)
        eg = sb("eg", [P, NT], F32)
        den = sb("den", [P, NT], F32)
        both = sb("both", [P, NT, E], F32)
        total = sb("total", [P, NT, E], F32)
        run = [sb(f"run{i}", [P, NT, E], F32) for i in range(2)]
        place = sb("place", [P, NT, E], F32)
        over = sb("over", [P, E, TM], F32)
        tiles = sb("tiles", [P, E], F32)
        ends = [sb(f"ends{i}", [P, E], F32) for i in range(2)]
        base = sb("base", [P, E], F32)
        past = sb("past", [P, NTL, E], F32)
        owner = sb("owner", [P, NTL], F32)
        took = [sb(f"took{i}", [P, NT, E], F32) for i in range(2)]
        slot_f = [sb(f"slot_f{i}", [P, NT], F32) for i in range(2)]
        ln_rows = sb("ln_rows", [2 * E * KD, P], F32)
        counted = ps("counted", [P, NT * E], F32)
        totals = ps("totals", [P, NT * E], F32)
        turned = ps("cols_turned", [P, TC], F32)
        names = ("loaded", "rows_loaded", "ones_set", "upper_set", "consts_set", "chain", "gap_ready",
                 "eg_ready", "both_ready", "counted_ready", "turned_ready", "owner_ready", "slots_ready")
        (loaded, rows_loaded, ones_set, upper_set, consts_set, chain_sem, gap_ready, eg_ready,
         both_ready, counted_ready, turned_ready, owner_ready, slots_ready) = (sem("r_" + n) for n in names)
        block = ctx.enter_context(nc.Block())

        @block.sync
        def _(sp):
            sp.dma_start(lg[:], lgd).then_inc(loaded, 16)
            sp.dma_start(ln_rows[0:E * KD], ln_g.rearrange("e (k d) -> (e k) d", d=P)).then_inc(rows_loaded, 16)
            sp.dma_start(ln_rows[E * KD:2 * E * KD], ln_b.rearrange("e (k d) -> (e k) d", d=P)).then_inc(rows_loaded, 16)

        @block.gpsimd
        def _(pool):
            nc.gpsimd.memset(ones[:], 1.0).then_inc(ones_set, 1)
            pool.wait_ge(ones_set, 1)
            nc.gpsimd.affine_select(out=upper[:], in_=ones[:], compare_op=ALU.is_gt, fill=0.0, base=0,
                                    pattern=[[1, P]], channel_multiplier=-1).then_inc(upper_set, 1)
            nc.gpsimd.iota(tau_i[:], pattern=[[1, NTL]], base=0, channel_multiplier=0).then_inc(consts_set, 1)

        @block.scalar
        def _(act):
            act.wait_ge(gap_ready, 1)
            nc.scalar.activation(eg[:], gap[:], ACT.Exp).then_inc(eg_ready, 1)
            act.wait_ge(turned_ready, 1)
            nc.scalar.copy(ln_cols[:].rearrange("p w e k -> p (w e k)"), turned[:, 0:2 * E * KD])

        @block.tensor
        def _(pe):
            pe.wait_ge(rows_loaded, 32)
            nc.tensor.transpose(turned[:, 0:2 * E * KD], ln_rows[:], ident[0:2 * E * KD, 0:2 * E * KD]
                                ).then_inc(turned_ready, 1)
            pe.wait_ge(upper_set, 1)
            pe.wait_ge(both_ready, 1)
            rhs = both[:].rearrange("p t e -> p (t e)")
            nc.tensor.matmul(counted[:], upper[:], rhs, start=True, stop=True)
            nc.tensor.matmul(totals[:], ones[:], rhs, start=True, stop=True).then_inc(counted_ready, 1)

        @block.vector
        def _(dve):
            chain = Chain(dve, chain_sem)

            def step(ins):
                chain.add(ins)
                chain.wait()

            def over_e(v):
                return v.rearrange("p (t o) -> p t o", o=1).to_broadcast((P, NT, E))

            dve.wait_ge(loaded, 16)
            dve.wait_ge(consts_set, 1)
            step(nc.vector.tensor_copy(tau[:], tau_i[:]))
            step(nc.vector.tensor_scalar(order[:], tau[:, 0:E], -1.0, float(E), ALU.mult, ALU.add))
            step(nc.vector.tensor_scalar(thr[:], tau[:, 0:TM], float(TS), None, ALU.mult))
            order_b = order[:].rearrange("p (o e) -> p o e", o=1).to_broadcast((P, NT, E))
            for r, src in ((0, lg), (1, lg2)):
                step(nc.vector.tensor_reduce(best[r][:], src[:], AX.X, ALU.max))
                step(nc.vector.tensor_tensor(pick[r][:], src[:], over_e(best[r][:]), ALU.is_equal))
                step(nc.vector.tensor_tensor(rank[r][:], pick[r][:], order_b, ALU.mult))
                step(nc.vector.tensor_reduce(first[r][:], rank[r][:], AX.X, ALU.max))
                step(nc.vector.tensor_tensor(hot[r][:], rank[r][:], over_e(first[r][:]), ALU.is_equal))
                if r == 0:
                    step(nc.vector.scalar_tensor_tensor(lg2[:], hot[0][:], -3.0e38, lg[:], ALU.mult, ALU.add))
            nc.vector.tensor_tensor(both[:], hot[0][:], hot[1][:], ALU.add).then_inc(both_ready, 1)
            nc.vector.tensor_tensor(gap[:], best[1][:], best[0][:], ALU.subtract).then_inc(gap_ready, 1)
            dve.wait_ge(eg_ready, 1)
            step(nc.vector.tensor_scalar(den[:], eg[:], 1.0, None, ALU.add))
            step(nc.vector.reciprocal(share[0][:], den[:]))
            step(nc.vector.tensor_tensor(share[1][:], share[0][:], eg[:], ALU.mult))
            dve.wait_ge(counted_ready, 1)
            step(nc.vector.tensor_copy(total[:].rearrange("p t e -> p (t e)"), totals[:]))
            src, d, i = total, 1, 0
            while d < NT:
                chain.add(nc.vector.tensor_copy(run[i][:, 0:d, :], src[:, 0:d, :]))
                step(nc.vector.tensor_tensor(run[i][:, d:NT, :], src[:, d:NT, :], src[:, 0:NT - d, :], ALU.add))
                src, d, i = run[i], 2 * d, 1 - i
            count = src[:, NT - 1, :].rearrange("p (e o) -> p e o", o=1).to_broadcast((P, E, TM))
            step(nc.vector.tensor_tensor(over[:], count, thr[:].rearrange("p (o m) -> p o m", o=1)
                                         .to_broadcast((P, E, TM)), ALU.is_gt))
            step(nc.vector.tensor_reduce(tiles[:], over[:], AX.X, ALU.add))
            end, d, i = tiles, 1, 0
            while d < E:
                chain.add(nc.vector.tensor_copy(ends[i][:, 0:d], end[:, 0:d]))
                step(nc.vector.tensor_tensor(ends[i][:, d:E], end[:, d:E], end[:, 0:E - d], ALU.add))
                end, d, i = ends[i], 2 * d, 1 - i
            step(nc.vector.tensor_tensor(past[:], end[:].rearrange("p (o e) -> p o e", o=1).to_broadcast((P, NTL, E)),
                                         tau[:].rearrange("p (m o) -> p m o", o=1).to_broadcast((P, NTL, E)),
                                         ALU.is_le))
            step(nc.vector.tensor_reduce(owner[:], past[:], AX.X, ALU.add))
            nc.vector.tensor_scalar(owner_i[:], owner[:], float(E - 1), None, ALU.min).then_inc(owner_ready, 1)
            step(nc.vector.tensor_tensor(base[:], end[:], tiles[:], ALU.subtract))
            step(nc.vector.tensor_tensor(place[:], src[:], total[:], ALU.subtract))
            step(nc.vector.scalar_tensor_tensor(place[:], base[:].rearrange("p (o e) -> p o e", o=1)
                                                .to_broadcast((P, NT, E)), float(TS), place[:], ALU.mult, ALU.add))
            step(nc.vector.tensor_tensor(place[:], counted[:].rearrange("p (t e) -> p t e", e=E), place[:], ALU.add))
            for r in range(2):
                step(nc.vector.tensor_tensor(took[r][:], hot[r][:], place[:], ALU.mult))
                step(nc.vector.tensor_reduce(slot_f[r][:], took[r][:], AX.X, ALU.add))
                nc.vector.tensor_copy(slot[r][:], slot_f[r][:]).then_inc(slots_ready, 1)


def stage_scatter(nc, a):
    xhd, xgd, slot, D, E, KD, I, NCH = (a[n] for n in ("xhd", "xgd", "slot", "D", "E", "KD", "I", "NCH"))
    w1, b1, b2, W1, b1s, b2s, ln_cols = (a[n] for n in ("w1", "b1", "b2", "W1", "b1s", "b2s", "ln_cols"))
    with ExitStack() as ctx:
        sb, ps, sem = opener(nc, ctx)
        xh = sb("scatter_xh", [P, 2, TPC, D], F32)
        cur = sb("scatter_cur", [P, 2, 2, TPC], mybir.dt.int32)
        cur_ready, gate, buffer_free = sem("s_cur_ready"), sem("s_gate"), sem("s_buffer_free")
        xh_loaded = [sem(f"s_xh_loaded{i}") for i in range(2)]
        scattered = [sem(f"s_scattered{i}") for i in range(2)]
        SC = 16 * 2 * TPC
        ones = sb("scatter_ones", [P, P], F32)
        lnb = sb("lnb", [P, E, KD, P], F32)
        shift = [[ps(f"shift{i}{h}", [P, TC], F32) for h in range(2)] for i in range(2)]
        w1_loaded = [sem(f"w1_loaded{i}") for i in range(2)]
        biases_loaded, ones_set, lnb_ready, shift_ready, shifted = (
            sem("s_" + n) for n in ("biases_loaded", "ones_set", "lnb_ready", "shift_ready", "shifted"))
        block = ctx.enter_context(nc.Block())

        @block.sync
        def _(sp):
            sp.sem_inc(buffer_free, 2)
            sp.dma_start(b1s[:].rearrange("p e i -> p (e i)"),
                         b1.rearrange("(o e) i -> o (e i)", o=1).to_broadcast((P, E * I))).then_inc(biases_loaded, 16)
            sp.dma_start(b2s[:].rearrange("p e d -> p (e d)"),
                         b2.rearrange("(o e) d -> o (e d)", o=1).to_broadcast((P, E * D))).then_inc(biases_loaded, 16)
            with sp.Fori(0, NCH // 2) as it:
                for h in range(2):
                    sp.wait_ge(buffer_free, 2 * (it + 1))
                    sp.dma_start(xh[:, h], xhd.rearrange("(i h j p) d -> i h p j d", h=2, j=TPC, p=P)[it, h]
                                 ).then_inc(xh_loaded[h], 16)

        @block.scalar
        def _(act):
            for e in range(E):
                if e >= 2:
                    act.wait_ge(w1_loaded[e % 2], 16 * (e // 2))
                act.dma_start(W1[:, e], w1[e].rearrange("(k p) i -> p k i", p=P)).then_inc(w1_loaded[e % 2], 16)

        @block.tensor
        def _(pe):
            pe.wait_ge(lnb_ready, E * KD)
            for e in range(E):
                pe.wait_ge(w1_loaded[e % 2], 16 * (e // 2 + 1))
                if e >= 2:
                    pe.wait_ge(shifted, 2 * (e - 1))
                for h in range(2):
                    for k in range(KD):
                        mm = nc.tensor.matmul(shift[e % 2][h][:], lnb[:, e, k, :], W1[:, e, k, h * TC:(h + 1) * TC],
                                              start=(k == 0), stop=(k == KD - 1))
                mm.then_inc(shift_ready, 1)

        @block.vector
        def _(dve):
            nc.vector.memset(ones[:], 1.0).then_inc(ones_set, 1)
            dve.wait_ge(ones_set, 1)
            for e in range(E):
                for k in range(KD):
                    nc.vector.tensor_scalar(lnb[:, e, k, :], ones[:], ln_cols[:, 1, e, k:k + 1], None, ALU.mult
                                            ).then_inc(lnb_ready, 1)
            dve.wait_ge(biases_loaded, 32)
            for e in range(E):
                dve.wait_ge(shift_ready, e + 1)
                for h in range(2):
                    nc.vector.tensor_tensor(b1s[:, e, h * TC:(h + 1) * TC], shift[e % 2][h][:],
                                            b1s[:, e, h * TC:(h + 1) * TC], ALU.add).then_inc(shifted, 1)
                for k in range(KD):
                    nc.vector.tensor_scalar(W1[:, e, k, :], W1[:, e, k, :], ln_cols[:, 0, e, k:k + 1], None, ALU.mult)

        @block.gpsimd
        def _(pool):
            with pool.Fori(0, NCH // 2) as it:
                for h in range(2):
                    for r in range(2):
                        nc.gpsimd.tensor_copy(cur[:, h, r, :], slot[r][:, bass.ds((2 * it + h) * TPC, TPC)]
                                              ).then_inc(cur_ready, 1)
                    pool.wait_ge(cur_ready, 2 * (2 * it + h + 1))
                    pool.wait_ge(xh_loaded[h], 16 * (it + 1))
                    pool.sem_inc(gate, 1)
                    for j in range(TPC):
                        for r in range(2):
                            nc.gpsimd.indirect_dma_start(
                                xgd, bass.IndirectOffsetOnAxis(ap=cur[:, h, r, j:j + 1], axis=0),
                                xh[:, h, j, :], None).then_inc(scattered[h], 16)
                for h in range(2):
                    pool.wait_ge(scattered[h], SC * (it + 1))
                    pool.sem_inc(buffer_free, 1)


def stage_experts(nc, a):
    xgd, ygd, W1, W2, b1s, b2s, owner_i = (a[n] for n in ("xgd", "ygd", "W1", "W2", "b1s", "b2s", "owner_i"))
    KD, IC, D, E, I, NTL, ident = (a[n] for n in ("KD", "IC", "D", "E", "I", "NTL", "ident"))
    HC = IC // 2
    with ExitStack() as ctx:
        sb, ps, sem = opener(nc, ctx)
        xg = [sb(f"xg{i}", [P, D], F32) for i in range(2)]
        xgT = [sb(f"xgT{i}", [P, D], F32) for i in range(2)]
        u = sb("u", [P, I], F32)
        h = [sb(f"h{i}", [P, I], F32) for i in range(2)]
        hT = [sb(f"hT{i}", [P, 2, TC], F32) for i in range(2)]
        y = [sb(f"y{i}", [P, D], F32) for i in range(2)]
        pxT = ps("e_xT", [P, TC], F32)
        pre = ps("pre", [P, I], F32)
        phT = [ps(f"e_hT{i}", [P, TC], F32) for i in range(2)]
        py = [ps(f"py{i}", [P, TC], F32) for i in range(2)]
        names = ("turned", "xgT_ready", "pre_ready", "u_ready", "h_ready", "h_turned", "hT_ready", "py_ready", "y_ready")
        turned, xgT_ready, pre_ready, u_ready, h_ready, h_turned, hT_ready, py_ready, y_ready = (
            sem("e_" + n) for n in names)
        xg_loaded = [sem(f"e_xg_loaded{i}") for i in range(2)]
        y_stored = [sem(f"e_y_stored{i}") for i in range(2)]
        block = ctx.enter_context(nc.Block())

        def run(eng, step):
            with eng.Fori(0, NTL // 2 - 2) as it:
                for p in range(2):
                    step(2 * it + p, it, p, 4)
            for n in range(NTL - 4, NTL):
                step(n, n // 2, n % 2, NTL - 1 - n)

        def owner(eng, tile):
            return eng.value_load(owner_i[0:1, bass.ds(tile, 1)], min_val=0, max_val=E - 1)

        @block.sync
        def _(sp):
            sp.sem_inc(y_ready, 2)
            for s in y_stored:
                sp.sem_inc(s, 1)
            rows = xgd.rearrange("(n p) d -> n p d", p=P)
            results = ygd.rearrange("(n p) d -> n p d", p=P)

            def load(n, p):
                sp.dma_start(xg[p][:], rows[n]).then_inc(xg_loaded[p], 16)

            def step(n, it, p, left):
                if left >= 4:
                    sp.wait_ge(turned, n + 3)
                    load(n + 4, p)
                sp.wait_ge(y_ready, n + 3)
                sp.dma_start(results[n], y[p][:]).then_inc(y_stored[p], 16)

            for n in range(2):
                load(n, n)
            for n in range(2):
                sp.wait_ge(turned, n + 1)
                load(n + 2, n)
            run(sp, step)
            for p in range(2):
                sp.wait_ge(y_stored[p], 16 * (NTL // 2) + 1)

        @block.tensor
        def _(pe):
            def turn_rows(n, it, p):
                pe.wait_ge(xg_loaded[p], 16 * (it + 1))
                for k in range(KD):
                    mm = nc.tensor.transpose(pxT[:, k * P:(k + 1) * P], xg[p][:, k * P:(k + 1) * P], ident[:])
                mm.then_inc(turned, 1)

            def times_w1(n, p):
                e = owner(pe, n)
                pe.wait_ge(xgT_ready, n + 1)
                for c in range(2):
                    for k in range(KD):
                        mm = nc.tensor.matmul(pre[:, c * TC:(c + 1) * TC], xgT[p][:, k * P:(k + 1) * P],
                                              W1[:, bass.ds(e, 1), k, c * TC:(c + 1) * TC],
                                              start=(k == 0), stop=(k == KD - 1))
                mm.then_inc(pre_ready, 1)

            def step(n, it, p, left):
                pe.wait_ge(h_ready, n + 1)
                for c in range(IC):
                    mm = nc.tensor.transpose(phT[c // HC][:, c % HC * P:(c % HC + 1) * P],
                                             h[p][:, c * P:(c + 1) * P], ident[:])
                    if c % HC == HC - 1:
                        mm.then_inc(h_turned, 1)
                if left >= 1:
                    times_w1(n + 1, 1 - p)
                if left >= 2:
                    turn_rows(n + 2, it + 1, p)
                e = owner(pe, n)
                pe.wait_ge(hT_ready, 2 * (n + 1))
                pe.wait_ge(y_ready, n + 1)
                for c in range(IC):
                    mm = nc.tensor.matmul(py[p][:, 0:D], hT[p][:, c // HC, c % HC * P:(c % HC + 1) * P],
                                          W2[:, bass.ds(e, 1), c, :], start=(c == 0), stop=(c == IC - 1))
                mm.then_inc(py_ready, 1)

            turn_rows(0, 0, 0)
            times_w1(0, 0)
            turn_rows(1, 0, 1)
            run(pe, step)

        @block.scalar
        def _(act):
            def copy_rows(n, p):
                act.wait_ge(turned, n + 1)
                nc.scalar.copy(xgT[p][:], pxT[:, 0:D]).then_inc(xgT_ready, 1)

            def gelu(n, p):
                act.wait_ge(u_ready, n + 1)
                nc.scalar.activation(h[p][:], u[:], ACT.Gelu).then_inc(h_ready, 1)

            def step(n, it, p, left):
                act.wait_ge(h_turned, 2 * n + 1)
                nc.scalar.copy(hT[p][:, 0, :], phT[0][:]).then_inc(hT_ready, 1)
                if left >= 1:
                    gelu(n + 1, 1 - p)
                if left >= 2:
                    copy_rows(n + 2, p)

            copy_rows(0, 0)
            gelu(0, 0)
            copy_rows(1, 1)
            run(act, step)

        @block.vector
        def _(dve):
            def add_b1(n):
                e = owner(dve, n)
                dve.wait_ge(pre_ready, n + 1)
                nc.vector.tensor_tensor(u[:], pre[:], b1s[:, bass.ds(e, 1), :].rearrange("p o i -> p (o i)"), ALU.add
                                        ).then_inc(u_ready, 1)

            def step(n, it, p, left):
                dve.wait_ge(h_turned, 2 * n + 2)
                nc.vector.tensor_copy(hT[p][:, 1, :], phT[1][:]).then_inc(hT_ready, 1)
                if left >= 1:
                    dve.wait_ge(h_ready, n + 1)
                    add_b1(n + 1)
                e = owner(dve, n)
                dve.wait_ge(y_stored[p], 16 * it + 1)
                dve.wait_ge(py_ready, n + 1)
                nc.vector.tensor_tensor(y[p][:], py[p][:, 0:D], b2s[:, bass.ds(e, 1), :].rearrange("p o d -> p (o d)"),
                                        ALU.add).then_inc(y_ready, 1)

            add_b1(0)
            run(dve, step)


def stage_finish(nc, a):
    x1d, ygd, out, slot, share = (a[n] for n in ("x1d", "ygd", "out", "slot", "share"))
    NCH, D = a["NCH"], a["D"]
    with ExitStack() as ctx:
        sb, ps, sem = opener(nc, ctx)
        x1 = sb("f_x1", [P, TPC, D], F32)
        got = sb("f_got", [P, TPC, 2, D], F32)
        cur = sb("f_cur", [P, 2, TPC], mybir.dt.int32)
        part = sb("f_part", [P, 2, TPC], F32)
        one = sb("f_one", [P, TPC, D], F32)
        two = sb("f_two", [P, TPC, D], F32)
        fin = sb("f_fin", [P, TPC, D], F32)
        st, mv = sb("f_st", [P, TPC, 6], F32), sb("f_mv", [P, TPC, 2], F32)
        ve, rs = sb("f_ve", [P, TPC], F32), sb("f_rs", [P, TPC], F32)
        minus_half = sb("f_minus_half", [P, TPC], F32)
        names = ("cur_ready", "part_ready", "half_set", "gate_pool", "gate_dve", "one_ready", "two_ready", "st_ready",
                 "var_ready", "ve_ready", "rs_ready", "fin_ready")
        (cur_ready, part_ready, half_set, gate_pool, gate_dve, one_ready, two_ready, st_ready,
         var_ready, ve_ready, rs_ready, fin_ready) = (sem("f_" + n) for n in names)
        x1_loaded, gathered, stored = ([sem(f"f_{n}{j}") for j in range(TPC)] for n in ("x1_loaded", "gathered", "stored"))
        block = ctx.enter_context(nc.Block())

        @block.sync
        def _(sp):
            for s in (two_ready, fin_ready, *stored):
                sp.sem_inc(s, 1)

            def load(n, j):
                sp.dma_start(x1[:, j, :], x1d.rearrange("(n j p) d -> n j p d", j=TPC, p=P)[n, j]
                             ).then_inc(x1_loaded[j], 16)

            def store(n, j):
                sp.wait_ge(fin_ready, TPC * n + j + 2)
                sp.dma_start(out.rearrange("b (c j p) d -> (b c) j p d", j=TPC, p=P)[n, j], fin[:, j, :]
                             ).then_inc(stored[j], 16)

            for j in range(TPC):
                load(0, j)
            with sp.Fori(0, NCH - 1) as n:
                for j in range(TPC):
                    sp.wait_ge(two_ready, TPC * n + j + 2)
                    load(n + 1, j)
                for j in range(TPC):
                    store(n, j)
            for j in range(TPC):
                store(NCH - 1, j)
            for j in range(TPC):
                sp.wait_ge(stored[j], 16 * NCH + 1)

        @block.gpsimd
        def _(pool):
            nc.gpsimd.memset(minus_half[:], -0.5).then_inc(half_set, 1)
            pool.wait_ge(half_set, 1)

            def gather(n, free):
                if free:
                    pool.wait_ge(one_ready, TPC * n)
                    pool.wait_ge(two_ready, TPC * n + 1)
                    pool.sem_inc(gate_pool, 1)
                for r in range(2):
                    nc.gpsimd.tensor_copy(cur[:, r, :], slot[r][:, bass.ds(n * TPC, TPC)]).then_inc(cur_ready, 1)
                pool.wait_ge(cur_ready, 2 * (n + 1))
                pool.sem_inc(gate_pool, 1)
                for j in range(TPC):
                    for r in range(2):
                        nc.gpsimd.indirect_dma_start(
                            got[:, j, r, :], None, ygd,
                            bass.IndirectOffsetOnAxis(ap=cur[:, r, j:j + 1], axis=0)).then_inc(gathered[j], 16)

            def rsqrt(n):
                pool.wait_ge(var_ready, TPC * (n + 1))
                pool.sem_inc(gate_pool, 1)
                nc.gpsimd.tensor_scalar(ve[:], mv[:, :, 1], EPS, None, ALU.add).then_inc(ve_ready, 1)
                pool.wait_ge(ve_ready, n + 1)
                nc.gpsimd.tensor_tensor(rs[:], ve[:], minus_half[:], ALU.pow).then_inc(rs_ready, 1)

            gather(0, False)
            with pool.Fori(0, NCH - 1) as n:
                gather(n + 1, True)
                rsqrt(n)
            rsqrt(NCH - 1)

        @block.vector
        def _(dve):
            with dve.Fori(0, NCH) as n:
                dve.wait_ge(fin_ready, TPC * n + 1)
                for r in range(2):
                    nc.vector.tensor_copy(part[:, r, :], share[r][:, bass.ds(n * TPC, TPC)]).then_inc(part_ready, 1)
                dve.wait_ge(part_ready, 2 * (n + 1))
                for j in range(TPC):
                    dve.wait_ge(x1_loaded[j], 16 * (n + 1))
                    dve.wait_ge(gathered[j], 32 * (n + 1))
                    nc.vector.scalar_tensor_tensor(one[:, j, :], got[:, j, 0, :], part[:, 0, j:j + 1], x1[:, j, :],
                                                   ALU.mult, ALU.add).then_inc(one_ready, 1)
                    dve.wait_ge(one_ready, TPC * n + j + 1)
                    nc.vector.scalar_tensor_tensor(two[:, j, :], got[:, j, 1, :], part[:, 1, j:j + 1], one[:, j, :],
                                                   ALU.mult, ALU.add).then_inc(two_ready, 1)
                for j in range(TPC):
                    dve.wait_ge(two_ready, TPC * n + j + 2)
                    nc.vector.bn_stats(st[:, j, :], two[:, j, :]).then_inc(st_ready, 1)
                dve.wait_ge(st_ready, TPC * (n + 1))
                dve.sem_inc(gate_dve, 1)
                for j in range(TPC):
                    nc.vector.bn_aggr(mv[:, j, :], st[:, j, :]).then_inc(var_ready, 1)
                dve.wait_ge(var_ready, TPC * (n + 1))
                dve.wait_ge(rs_ready, n + 1)
                for j in range(TPC):
                    dve.wait_ge(stored[j], 16 * n + 1)
                    nc.vector.tensor_scalar(fin[:, j, :], two[:, j, :], mv[:, j, 0:1], rs[:, j:j + 1],
                                            ALU.subtract, ALU.mult).then_inc(fin_ready, 1)


_INS = ["L0_attn_x", "L0_attn_Wq", "L0_attn_Wk", "L0_attn_Wv", "L0_attn_Wo", "L0_attn_lambda_q1",
        "L0_attn_lambda_k1", "L0_attn_lambda_q2", "L0_attn_lambda_k2", "L0_attn_gamma", "L0_attn_beta",
        "L0_ffn_rn_g", "L0_ffn_rn_b", "L0_ffn_router_w", "L0_ffn_router_b", "L0_ffn_ln_g", "L0_ffn_ln_b",
        "L0_ffn_w1", "L0_ffn_b1", "L0_ffn_w2", "L0_ffn_b2"]


def kernel(**inputs):
    import numpy as _np
    import concourse.bacc as _bacc
    from concourse import mybir as _mybir
    from concourse.bass_utils import run_bass_kernel_spmd as _run

    nc = _bacc.Bacc("TRN2", target_bir_lowering=False, num_devices=1)
    arrays, args = {}, []
    for name in _INS:
        a = _np.ascontiguousarray(inputs[name])
        arrays[f"in_{name}_dram"] = a
        args.append(nc.dram_tensor(f"in_{name}_dram", a.shape, _mybir.dt.from_np(a.dtype), kind="ExternalInput").ap())
    shape = inputs["L0_attn_x"].shape
    args.append(nc.dram_tensor("out_0_dram", shape, _mybir.dt.float32, kind="ExternalOutput").ap())
    diff_attention_moe(nc, *args)
    r = _run(nc, [arrays], core_ids=[0])
    return r.results[0]["out_0_dram"]
```

```python
import math
from contextlib import ExitStack

import concourse.bass as bass
from concourse import mybir

ALU = mybir.AluOpType
ACT = mybir.ActivationFunctionType
AX = mybir.AxisListType
F32 = mybir.dt.float32
BF16 = mybir.dt.bfloat16

P = 128
TC = 512
TPC = TC // P
EPS = 1e-5
HD = 16
UNITS = 4
GF = UNITS * HD
LAMBDA_INIT = 0.8 - 0.6 * math.exp(-0.3 * 11)
Q_PARTS = (0, 0, 0, 1, 1, 2)
K_PARTS = (0, 1, 2, 0, 1, 0)
KR = 16 * len(Q_PARTS)
KM = KR + 3


def diff_attention_moe(nc, x, Wq, Wk, Wv, Wo, lq1, lk1, lq2, lk2, gamma, beta, rn_g, rn_b,
                       router_w, router_b, ln_g, ln_b, w1, b1, w2, b2, out):
    NB, S, D = x.shape
    T = NB * S
    KD = D // P
    E, _, I = w1.shape
    IC = I // P
    G = D // HD // 2
    CH = S // TC
    KB = S // P
    NT = T // P
    NCH = T // TC
    assert D == 256 and S == 2048 and E == 8 and I == 1024 and KB == 16 and CH == 4

    qd = nc.dram_tensor("q_parts", (NB * G, 3, CH, HD * UNITS, TC), BF16, kind="Internal").ap()
    kd = nc.dram_tensor("k_parts", (NB * G, 3, HD * UNITS, S), BF16, kind="Internal").ap()
    vd = nc.dram_tensor("v_groups", (NB * G, P, KB, 64), F32, kind="Internal").ap()
    od = nc.dram_tensor("attended", (NB * G, P, S), F32, kind="Internal").ap()
    x1d = nc.dram_tensor("x1", (T, D), F32, kind="Internal").ap()
    xhd = nc.dram_tensor("xh", (T, D), F32, kind="Internal").ap()
    lgd = nc.dram_tensor("logits", (P, NT, E), F32, kind="Internal").ap()

    TS = P
    USED = (2 * T + E * (TS - 1)) // TS
    NTL = USED + USED % 2
    xgd = nc.dram_tensor("slot_rows", (NTL * TS, D), F32, kind="Internal").ap()
    ygd = nc.dram_tensor("slot_results", (USED * TS, D), F32, kind="Internal").ap()

    with ExitStack() as top:
        ident = top.enter_context(nc.sbuf_tensor("ident", [P, P], F32))
        identb = top.enter_context(nc.sbuf_tensor("identb", [P, P], BF16))

        stage_project(nc, locals())
        stage_attend(nc, locals())
        W2 = top.enter_context(nc.sbuf_tensor("W2", [P, E, IC, D], F32))
        stage_join(nc, locals())
        W1 = top.enter_context(nc.sbuf_tensor("W1", [P, E, KD, I], F32))
        b1c = top.enter_context(nc.sbuf_tensor("b1c", [P, E, IC], F32))
        b2s = top.enter_context(nc.sbuf_tensor("b2s", [P, E, D], F32))
        owner_i = top.enter_context(nc.sbuf_tensor("owner_i", [P, NTL], mybir.dt.int32))
        slot = [top.enter_context(nc.sbuf_tensor(f"slot{r}", [P, NT], mybir.dt.int32)) for r in range(2)]
        share = [top.enter_context(nc.sbuf_tensor(f"share{r}", [P, NT], F32)) for r in range(2)]
        ln_cols = top.enter_context(nc.sbuf_tensor("ln_cols", [P, 2, E, KD], F32))
        EARLY = 3 * E // 4
        stage_route(nc, locals())
        stage_scatter(nc, locals())
        stage_experts(nc, locals())
        stage_finish(nc, locals())


def opener(nc, ctx):
    return (lambda n, s, d: ctx.enter_context(nc.sbuf_tensor(n, s, d)),
            lambda n, s, d: ctx.enter_context(nc.psum_tensor(n, s, d)),
            lambda n: ctx.enter_context(nc.semaphore(n)))


def stage_project(nc, a):
    x, Wq, Wk, Wv, qd, kd, vd = (a[n] for n in ("x", "Wq", "Wk", "Wv", "qd", "kd", "vd"))
    NB, CH, KD, G, D, ident, identb = (a[n] for n in ("NB", "CH", "KD", "G", "D", "ident", "identb"))
    MC = 2 * D // P
    ITEMS = 2 * MC
    with ExitStack() as ctx:
        sb, ps, sem = opener(nc, ctx)
        wraw = sb("wraw", [P, KD, 2, 2 * D], F32)
        wqk = sb("wqk", [P, KD, 2, 2 * D], F32)
        wv = sb("wv", [P, KD, D], F32)
        xs = sb("xs", [P, TPC, D], F32)
        xT = sb("xT", [P, KD, TC], F32)
        parts = sb("parts", [P, 4, 3, TC], BF16)
        rest = sb("rest", [P, 4, TC], F32)
        vst = sb("vst", [P, G, TPC, 2, 32], F32)
        pxT = [ps(f"pxT{i}", [P, TC], F32) for i in range(KD)]
        pj = [ps(f"pj{i}", [P, TC], F32) for i in range(4)]
        pv = [ps(f"pv{i}", [P, 2, D], F32) for i in range(2)]
        names = ("w_loaded", "zeroed", "ident_ready", "identb_ready", "wqk_ready", "vst_preset", "x_loaded",
                 "x_turned", "xT_ready", "proj_ready", "hi_ready", "rest_ready", "mid_ready", "lo_ready",
                 "v_ready", "vst_ready", "v_stored")
        (w_loaded, zeroed, ident_ready, identb_ready, wqk_ready, vst_preset, x_loaded, x_turned, xT_ready,
         proj_ready, hi_ready, rest_ready, mid_ready, lo_ready, v_ready, vst_ready,
         v_stored) = (sem(n) for n in names)
        parts_stored = [sem(f"parts_stored{i}") for i in range(4)]
        gate_pool = sem("gate_pool")
        block = ctx.enter_context(nc.Block())

        @block.sync
        def _(sp):
            for s in (x_turned, xT_ready, v_stored, v_ready, vst_ready, rest_ready, lo_ready,
                      *parts_stored):
                sp.sem_inc(s, 1)
            sp.dma_start(wraw[:, :, 0, :], Wq.rearrange("(k p) f -> p k f", p=P)).then_inc(w_loaded, 16)
            sp.dma_start(wraw[:, :, 1, :], Wk.rearrange("(k p) f -> p k f", p=P)).then_inc(w_loaded, 16)
            sp.dma_start(wv[:], Wv.rearrange("(k p) f -> p k f", p=P)).then_inc(w_loaded, 16)

            def load_x(n):
                sp.dma_start(xs[:], x.rearrange("b (c j p) d -> (b c) p j d", j=TPC, p=P)[n]).then_inc(x_loaded, 16)

            load_x(0)
            with sp.Fori(0, NB) as b:
                with sp.Fori(0, CH) as c:
                    n = b * CH + c
                    sp.wait_ge(x_turned, n + 2)
                    load_x((n + 1) % (NB * CH))
                    for i in range(ITEMS):
                        sp.wait_ge(lo_ready, n * ITEMS + i + 2)
                        if i < MC:
                            dst = qd.rearrange("(b g) s c r t -> b c g r s t", b=NB)
                        else:
                            dst = kd.rearrange("(b g) s r (c t) -> b c g r s t", b=NB, c=CH)
                        for h in range(2):
                            g = 2 * (i % MC) + h
                            sp.dma_start(
                                dst[b, c, g], parts[64 * h:64 * h + 64, i % 4, :, :]).then_inc(parts_stored[i % 4], 16)
                    sp.wait_ge(vst_ready, 4 * (n + 1) + 1)
                    sp.dma_start(vd.rearrange("(b g) p (c k) f -> b c p g (k f)", b=NB, c=CH)[b, c],
                                 vst[:].rearrange("p g k h f -> p g (k h f)")).then_inc(v_stored, 16)
            for stored in parts_stored:
                sp.wait_ge(stored, 32 * NB * CH * (ITEMS // 4) + 1)
            sp.wait_ge(v_stored, 16 * NB * CH + 1)
            sp.wait_ge(x_loaded, 16 * (NB * CH + 1))

        @block.gpsimd
        def _(pool):
            nc.gpsimd.memset(ident[:], 0.0).then_inc(zeroed, 1)
            nc.gpsimd.memset(vst[:], 0.0).then_inc(zeroed, 1)
            pool.wait_ge(zeroed, 2)
            nc.gpsimd.affine_select(out=ident[:], in_=ident[:], compare_op=ALU.not_equal, fill=1.0, base=0,
                                    pattern=[[-1, P]], channel_multiplier=1).then_inc(ident_ready, 1)
            nc.gpsimd.memset(vst[:, :, :, :, HD:HD + 1], 1.0).then_inc(vst_preset, 1)
            pool.wait_ge(ident_ready, 1)
            nc.gpsimd.tensor_copy(identb[:], ident[:]).then_inc(identb_ready, 1)
            with pool.Fori(0, NB * CH) as n:
                for i in range(ITEMS):
                    pool.wait_ge(rest_ready, n * ITEMS + i + 2)
                    pool.sem_inc(gate_pool, 1)
                    nc.gpsimd.tensor_copy(parts[:, i % 4, 1, :], rest[:, i % 4, :]).then_inc(mid_ready, 1)

        @block.scalar
        def _(act):
            with act.Fori(0, NB * CH) as n:
                act.wait_ge(x_turned, n + 2)
                act.wait_ge(v_ready, 2 * n + 1)
                for k in range(KD):
                    nc.scalar.copy(xT[:, k, :], pxT[k][:]).then_inc(xT_ready, 1)
                for i in range(ITEMS):
                    act.wait_ge(proj_ready, n * ITEMS + i + 1)
                    act.wait_ge(parts_stored[i % 4], 32 * (n * (ITEMS // 4) + i // 4) + 1)
                    nc.scalar.copy(parts[:, i % 4, 0, :], pj[i % 4][:]).then_inc(hi_ready, 1)
                act.wait_ge(v_stored, 16 * n + 1)
                act.wait_ge(vst_preset, 1)
                for j in range(TPC):
                    act.wait_ge(v_ready, 2 * n + j // 2 + 2)
                    nc.scalar.copy(vst[:, :, j, :, 0:HD],
                                   pv[j // 2][:, j % 2, :].rearrange("p (g h d) -> p g h d", h=2, d=HD)
                                   ).then_inc(vst_ready, 1)

        @block.tensor
        def _(pe):
            pe.wait_ge(ident_ready, 1)
            pe.wait_ge(wqk_ready, 2 * KD)
            with pe.Fori(0, NB * CH) as n:
                pe.wait_ge(x_loaded, 16 * (n + 1))
                pe.wait_ge(xT_ready, KD * n + 1)
                for k in range(KD):
                    for j in range(TPC):
                        mm = nc.tensor.transpose(pxT[k][:, j * P:(j + 1) * P], xs[:, j, k * P:(k + 1) * P], ident[:])
                mm.then_inc(x_turned, 1)
                pe.wait_ge(xT_ready, KD * (n + 1) + 1)
                for i in range(ITEMS):
                    pe.wait_ge(rest_ready, n * ITEMS + max(i - 3, 0) + 1)
                    for k in range(KD):
                        mm = nc.tensor.matmul(pj[i % 4][:], wqk[:, k, i // MC, (i % MC) * P:(i % MC + 1) * P],
                                              xT[:, k, :], start=(k == 0), stop=(k == KD - 1))
                    mm.then_inc(proj_ready, 1)
                pe.wait_ge(vst_ready, TPC * n + 1)
                for j in range(TPC):
                    for k in range(KD):
                        mm = nc.tensor.matmul(pv[j // 2][:, j % 2, :], xT[:, k, j * P:(j + 1) * P], wv[:, k, :],
                                              start=(k == 0), stop=(k == KD - 1), skip_group_check=True)
                    if j % 2 == 1:
                        mm.then_inc(v_ready, 1)

        @block.vector
        def _(dve):
            dve.wait_ge(w_loaded, 48)
            for k in range(KD):
                for m in range(2):
                    nc.vector.tensor_copy(
                        wqk[:, k, m, :].rearrange("p (g d u) -> p g d u", d=HD, u=UNITS),
                        wraw[:, k, m, :].rearrange("p (g u d) -> p g d u", d=HD, u=UNITS)).then_inc(wqk_ready, 1)
            with dve.Fori(0, NB * CH) as n:
                for i in range(ITEMS + 1):
                    if i < ITEMS:
                        dve.wait_ge(lo_ready, n * ITEMS + max(i - 3, 0) + 1)
                        dve.wait_ge(hi_ready, n * ITEMS + i + 1)
                        nc.vector.tensor_tensor(rest[:, i % 4, :], pj[i % 4][:], parts[:, i % 4, 0, :],
                                                ALU.subtract).then_inc(rest_ready, 1)
                    if i > 0:
                        j = i - 1
                        dve.wait_ge(mid_ready, n * ITEMS + j + 1)
                        nc.vector.tensor_tensor(parts[:, j % 4, 2, :], rest[:, j % 4, :], parts[:, j % 4, 1, :],
                                                ALU.subtract).then_inc(lo_ready, 1)


def stage_attend(nc, a):
    qd, kd, vd, od = (a[n] for n in ("qd", "kd", "vd", "od"))
    NB, CH, G, KB, S, identb = (a[n] for n in ("NB", "CH", "G", "KB", "S", "identb"))
    PAIRS = NB * G // 2
    RC = 2 * CH
    RS = RC * KB
    AHEAD = KB + 4
    CUT = 2 * KB - AHEAD
    SH = S // 2
    with ExitStack() as ctx:
        sb, ps, sem = opener(nc, ctx)
        Q = [sb(f"Q{i}", [KM, CH, UNITS, TC], BF16) for i in range(2)]
        K = [sb(f"K{i}", [KM, UNITS, S], BF16) for i in range(2)]
        V = [sb(f"V{i}", [P, KB, 2, 32], F32) for i in range(2)]
        probs = sb("probs", [P, 2 * UNITS, TC], F32)
        att = [sb(f"att{i}", [P, TC], F32) for i in range(2)]
        half_max = [sb(f"half_max{i}", [P, 2, 16], F32) for i in range(2)]
        row_max = sb("row_max", [P, 16], F32)
        max_rest = sb("max_rest", [P, 16], F32)
        max_parts = sb("max_parts", [P, 3, 16], BF16)
        max_rows = [sb(f"max_rows{i}", [48, P], BF16) for i in range(2)]
        scores = ps("scores", [P, S], F32)
        scoresT = [ps(f"scoresT{i}", [P, TC], F32) for i in range(3)]
        attT = ps("attT", [P, TC], F32)
        names = ("ones_set", "parts_chain", "max_parts_ready", "max_rows_turned", "max_rows_copied",
                 "scoresA_ready", "scoresB_ready", "maxA_done", "maxB_done", "scoresT_ready", "exp_done",
                 "pv_done", "att_copied")
        (ones_set, parts_chain, max_parts_ready, max_rows_turned, max_rows_copied,
         scoresA_ready, scoresB_ready, maxA_done, maxB_done, scoresT_ready, exp_done,
         pv_done, att_copied) = (sem(n) for n in names)
        qk_loaded = [sem(f"qk_loaded{i}") for i in range(2)]
        v_loaded = [sem(f"v_loaded{i}") for i in range(2)]
        max_loaded = [sem(f"max_loaded{i}") for i in range(2)]
        att_stored = [sem(f"att_stored{i}") for i in range(2)]
        first_loaded = sem("first_loaded")
        gate_pe, gate_pool, zeros_set, zeroed = sem("gate_pe"), sem("gate_pool"), sem("zeros_set"), sem("slots_zeroed")
        xgd, TS, NTL, D = (a[n] for n in ("xgd", "TS", "NTL", "D"))
        ZT = 2
        NZ = NTL // ZT
        zeros = sb("zeros", [P, ZT * TS // P * D], F32)
        QKD = 16 * 2 * len(Q_PARTS)
        MXD = 16 * 3
        turned = [s[0:48, 0:P // 2].bitcast(BF16) for s in scoresT]

        def turn_bank(lc):
            return 4 * (lc * KB + CUT + 2) % 3

        block = ctx.enter_context(nc.Block())

        @block.sync
        def _(sp):
            for s in (pv_done, att_copied, maxA_done, maxB_done, *max_loaded, *att_stored):
                sp.sem_inc(s, 1)
            def load_qk(p, g, c=0, u=0):
                for i in range(len(Q_PARTS)):
                    sp.dma_start(Q[p][16 * i:16 * i + 16, c:].rearrange("d c u t -> d c (u t)"),
                                 qd.rearrange("g s c (d u) t -> g s d c (u t)", u=UNITS)[g, Q_PARTS[i]][:, c:]
                                 ).then_inc(qk_loaded[p], 16)
                    sp.dma_start(K[p][16 * i:16 * i + 16, u:],
                                 kd.rearrange("g s (d u) t -> g s d u t", u=UNITS)[g, K_PARTS[i]][:, u:]
                                 ).then_inc(qk_loaded[p], 16)

            def load_v(p, g):
                sp.dma_start(V[p][:], vd.rearrange("g p k (h f) -> g p k h f", h=2)[g]).then_inc(v_loaded[p], 16)

            def load_max(done, lc):
                p, c = lc // CH % 2, lc % CH
                sp.wait_ge(max_rows_copied, done)
                for s in range(3):
                    sp.dma_start(Q[p][KR + s:KR + s + 1, c, :, :].rearrange("o u (t q) -> o (u t) q", q=P),
                                 max_rows[lc % 2][16 * s:16 * s + 16, :]
                                 ).then_inc(max_loaded[lc % 2], 16)

            for i in range(len(Q_PARTS)):
                sp.dma_start(Q[0][16 * i:16 * i + 16, 0],
                             qd.rearrange("g s c (d u) t -> g s d c u t", u=UNITS)[0, Q_PARTS[i], :, 0]
                             ).then_inc(first_loaded, 16)
                sp.dma_start(K[0][16 * i:16 * i + 16, 0],
                             kd.rearrange("g s (d u) t -> g s d u t", u=UNITS)[0, K_PARTS[i], :, 0]
                             ).then_inc(first_loaded, 16)
            load_qk(0, 0, c=1, u=1)
            load_v(0, 0)
            load_max(1, 0)
            with sp.Fori(0, PAIRS) as it:
                def store_att(lc):
                    sp.wait_ge(att_copied, it * RC + lc + 2)
                    sp.dma_start(od.rearrange("(i p) r (c t) -> i p c r t", p=2, c=CH)[it, lc // CH, lc % CH],
                                 att[lc % 2][:]).then_inc(att_stored[lc % 2], 16)

                sp.wait_ge(pv_done, it * RS + 1)
                load_qk(1, it * 2 + 1)
                load_v(1, it * 2 + 1)
                for lc in range(RC):
                    if lc > 0:
                        store_att(lc - 1)
                    if lc == CH:
                        load_qk(0, (it * 2 + 2) % (NB * G))
                        load_v(0, (it * 2 + 2) % (NB * G))
                    load_max(it * RC + lc + 2, lc + 1)
                store_att(RC - 1)
            for p in range(2):
                sp.wait_ge(att_stored[p], 16 * PAIRS * CH + 1)
                sp.wait_ge(v_loaded[p], 16 * (PAIRS + (p == 0)))
                sp.wait_ge(max_loaded[p], MXD * (PAIRS * CH + (p == 0)) + 1)

        @block.gpsimd
        def _(pool):
            for i in range(2):
                nc.gpsimd.memset(K[i][KR:KM], 1.0).then_inc(ones_set, 1)
            pool.wait_ge(ones_set, 2)
            pool.wait_ge(max_loaded[0], MXD + 1)
            pool.sem_inc(gate_pool, 1)
            nc.gpsimd.memset(zeros[:], 0.0).then_inc(zeros_set, 1)
            pool.wait_ge(zeros_set, 1)
            with pool.Fori(0, NZ) as n:
                pool.dma_start(xgd.rearrange("(n p j) d -> n p (j d)", n=NZ, p=P)[n], zeros[:]).then_inc(zeroed, 16)
            pool.wait_ge(zeroed, 16 * NZ)

        @block.tensor
        def _(pe):
            def score_rows(item, lc, i):
                p, c, u, t = lc // CH % 2, lc % CH, i // 4, i % 4
                lhsT = Q[p][0:KR, c, u, t * P:(t + 1) * P]
                for h, ready, used in ((0, scoresA_ready, maxA_done), (1, scoresB_ready, maxB_done)):
                    pe.wait_ge(used, item + 1)
                    for k in range(2):
                        at = h * SH + k * TC
                        mm = nc.tensor.matmul(scores[:, at:at + TC], lhsT, K[p][0:KR, u, at:at + TC],
                                              start=True, stop=True)
                    mm.then_inc(ready, 1)

            def turn_maxima(done, bank, used):
                pe.wait_ge(max_parts_ready, done)
                if used is not None:
                    pe.wait_ge(exp_done, used)
                pe.sem_inc(gate_pe, 1)
                nc.tensor.transpose(turned[bank], max_parts[:].rearrange("p s i -> p (s i)"), identb[:]
                                    ).then_inc(max_rows_turned, 1)

            pe.wait_ge(first_loaded, QKD)
            for i in range(AHEAD):
                if i == 4:
                    pe.wait_ge(qk_loaded[0], QKD)
                if i == KB + 2:
                    turn_maxima(1, 0, None)
                score_rows(i, i // KB, i % KB)
            pe.wait_ge(max_rows_copied, 1)
            pe.wait_ge(ones_set, 2)
            with pe.Fori(0, PAIRS) as it:
                for lc in range(RC):
                    p, c = lc // CH, lc % CH
                    for kb in range(KB):
                        ls = lc * KB + kb
                        ahead = (ls + AHEAD) % RS
                        item = it * RS + ls + AHEAD
                        if kb == 0:
                            pe.wait_ge(max_loaded[lc % 2], MXD * (it * CH + lc // 2 + 1) + 1)
                            if c == 0:
                                pe.wait_ge(v_loaded[p], 16 * (it + 1))
                        if ahead == CH * KB:
                            pe.wait_ge(qk_loaded[1], QKD * (it + 1))
                        if ahead == 0:
                            pe.wait_ge(qk_loaded[0], QKD * (it + 2))
                        if kb == CUT + 2:
                            pe.wait_ge(max_rows_copied, it * RC + lc + 2)

                        def scores_of(u):
                            i = 4 * ls + u
                            if i >= 3:
                                pe.wait_ge(exp_done, it * 4 * RS + i - 2)
                            nc.tensor.matmul(scoresT[i % 3][:], K[p][:, u, kb * P:(kb + 1) * P], Q[p][:, c, u, :],
                                             start=True, stop=True).then_inc(scoresT_ready, 1)

                        def weigh(s):
                            wp, wk = s // KB // CH, s % KB
                            pe.wait_ge(exp_done, it * 4 * RS + 4 * s + 4)
                            if wk == 0:
                                pe.wait_ge(att_copied, it * RC + s // KB + 1)
                            for u in range(UNITS):
                                mm = nc.tensor.matmul(attT[32 * u:32 * u + 32, :], V[wp][:, wk, u // 2, :],
                                                      probs[:, 4 * (s % 2) + u, :],
                                                      start=(wk == 0), stop=(wk == KB - 1), skip_group_check=True)
                            mm.then_inc(pv_done, 1)

                        for u in range(3):
                            scores_of(u)
                        score_rows(item, ahead // KB, ahead % KB)
                        scores_of(3)
                        if kb == CUT + 1:
                            turn_maxima(it * RC + lc + 2, turn_bank(lc), it * 4 * RS + 4 * ls + 2)
                        if ls > 0:
                            weigh(ls - 1)
                weigh(RS - 1)

        @block.scalar
        def _(act):
            with act.Fori(0, PAIRS) as it:
                for ls in range(RS):
                    act.wait_ge(pv_done, it * RS + max(ls - 1, 0) + 1)
                    for u in range(UNITS):
                        i = 4 * ls + u
                        act.wait_ge(scoresT_ready, it * 4 * RS + i + 1)
                        nc.scalar.activation(probs[:, i % 8, :], scoresT[i % 3][:], ACT.Exp,
                                             scale=HD ** -0.5).then_inc(exp_done, 1)

        @block.vector
        def _(dve):
            def maxima(item, lc, i, between=None):
                for h, ready, done in ((0, scoresA_ready, maxA_done), (1, scoresB_ready, maxB_done)):
                    if h == 1 and between is not None:
                        copy_rows(*between)
                    dve.wait_ge(ready, item + 1)
                    nc.vector.tensor_reduce(half_max[lc % 2][:, h, i:i + 1], scores[:, h * SH:(h + 1) * SH],
                                            AX.X, ALU.max).then_inc(done, 1)

            def cut_maxima(done, lc):
                hm, chain = half_max[lc % 2], 4 * (done - 1)
                nc.vector.tensor_tensor(row_max[:], hm[:, 0, :], hm[:, 1, :], ALU.max).then_inc(parts_chain, 1)
                dve.wait_ge(parts_chain, chain + 1)
                nc.vector.tensor_scalar(max_parts[:, 0, :], row_max[:], -1.0, None, ALU.mult).then_inc(parts_chain, 1)
                dve.wait_ge(parts_chain, chain + 2)
                nc.vector.scalar_tensor_tensor(max_rest[:], row_max[:], -1.0, max_parts[:, 0, :],
                                               ALU.mult, ALU.subtract).then_inc(parts_chain, 1)
                dve.wait_ge(parts_chain, chain + 3)
                nc.vector.tensor_copy(max_parts[:, 1, :], max_rest[:]).then_inc(parts_chain, 1)
                dve.wait_ge(parts_chain, chain + 4)
                nc.vector.tensor_tensor(max_parts[:, 2, :], max_rest[:], max_parts[:, 1, :],
                                        ALU.subtract).then_inc(max_parts_ready, 1)

            def copy_rows(done, lc, loaded, bank):
                dve.wait_ge(max_rows_turned, done)
                dve.wait_ge(max_loaded[lc % 2], loaded + 1)
                nc.vector.tensor_copy(max_rows[lc % 2][:], turned[bank]).then_inc(max_rows_copied, 1)

            for i in range(AHEAD):
                if i == KB:
                    dve.wait_ge(maxA_done, KB + 1)
                    dve.wait_ge(maxB_done, KB + 1)
                    cut_maxima(1, 0)
                maxima(i, i // KB, i % KB, (1, 0, 0, 0) if i == KB + 2 else None)
            with dve.Fori(0, PAIRS) as it:
                def copy_att(lc):
                    dve.wait_ge(pv_done, it * RS + (lc + 1) * KB + 1)
                    dve.wait_ge(att_stored[lc % 2], 16 * (it * CH + lc // 2) + 1)
                    nc.vector.tensor_copy(att[lc % 2][:], attT[:]).then_inc(att_copied, 1)

                for lc in range(RC):
                    for kb in range(KB):
                        ahead = (lc * KB + kb + AHEAD) % RS
                        item = it * RS + lc * KB + kb + AHEAD
                        between = None
                        if kb == CUT:
                            dve.wait_ge(maxA_done, item + 1)
                            dve.wait_ge(maxB_done, item + 1)
                            cut_maxima(it * RC + lc + 2, lc + 1)
                        if kb == 1 and lc > 0:
                            copy_att(lc - 1)
                        if kb == CUT + 1:
                            between = (it * RC + lc + 2, lc + 1, MXD * (it * CH + (lc + 1) // 2), turn_bank(lc))
                        maxima(item, ahead // KB, ahead % KB, between)
                copy_att(RC - 1)


class Chain:

    def __init__(self, eng, sem, base=0):
        self.eng, self.sem, self.base, self.n = eng, sem, base, 0

    def add(self, ins):
        ins.then_inc(self.sem, 1)
        self.n += 1

    def wait(self):
        self.eng.wait_ge(self.sem, self.base + self.n)


def stage_join(nc, a):
    x, Wo, od, x1d, xhd, lgd = (a[n] for n in ("x", "Wo", "od", "x1d", "xhd", "lgd"))
    lams = [a[n] for n in ("lq1", "lk1", "lq2", "lk2")]
    gamma, beta, rn_g, rn_b, router_w, router_b = (a[n] for n in ("gamma", "beta", "rn_g", "rn_b", "router_w", "router_b"))
    NB, CH, KD, G, D, E, ident = (a[n] for n in ("NB", "CH", "KD", "G", "D", "E", "ident"))
    NU = G * UNITS
    TPC = 8
    TC = TPC * P
    CH = a["S"] // TC
    NL = 4 + 1 + 3 + 4
    with ExitStack() as ctx:
        sb, ps, sem = opener(nc, ctx)
        wo = sb("wo", [P, KD, D], F32)
        lam_in = sb("lam_in", [P, 4, HD], F32)
        lam_mul = sb("lam_mul", [P, 2, HD], F32)
        lam_sum = sb("lam_sum", [P, 2], F32)
        lam_exp = sb("lam_exp", [P, 2], F32)
        lam_neg = sb("lam_neg", [P, 1], F32)
        coef = sb("coef", [P, NU], F32)
        gam = sb("gam", [P, D], F32)
        bet = sb("bet", [P, D], F32)
        rnb = sb("rnb", [P, D], F32)
        rw_all = sb("rw_all", [P, E, D], F32)
        rbias = sb("rbias", [P, E], F32)
        rbias_in = sb("rbias_in", [P, E], F32)
        rw_rows = sb("rw_rows", [E, D], F32)
        rg_rows = sb("rg_rows", [E, D], F32)
        rw_T = sb("rw_T", [P, KD, E], F32)
        xs = sb("join_x", [P, TPC, D], F32)
        xb = sb("join_xb", [P, TPC, D], F32)
        heads = sb("heads", [P, G, TC], F32)
        rcp = sb("rcp", [P, TPC, NU], F32)
        rcc = sb("rcc", [P, TPC, NU], F32)
        scaled = sb("scaled", [P, 2, NU, HD], F32)
        att = sb("join_att", [P, TPC, D], F32)
        attT = sb("join_attT", [P, TPC, D], F32)
        zg = sb("zg", [P, TPC, D], F32)
        zs = sb("zs", [P, TPC, D], F32)
        x1 = sb("x1s", [P, TPC, D], F32)
        xh = sb("join_xh", [P, TPC, D], F32)
        xhT = sb("join_xhT", [P, KD, TC], F32)
        lgs = sb("lgs", [P, TPC, E], F32)
        st = [sb(f"st{i}", [P, TPC, 6], F32) for i in range(3)]
        mv = [sb(f"mv{i}", [P, TPC, 2], F32) for i in range(3)]
        rs = [sb(f"rs{i}", [P, TPC], F32) for i in range(3)]
        ve = [sb(f"ve{i}", [P, TPC], F32) for i in range(3)]
        minus_half = sb("minus_half", [P, TPC], F32)
        token_major = [ps(f"token_major{i}", [P, NU, 32], F32) for i in range(2)]
        turn = [ps(f"turn{i}", [P, 512], F32) for i in range(2)]
        prod = [ps(f"prod{i}", [P, 2, D], F32) for i in range(2)]

        def product(j):
            return prod[j // 2 % 2][:, j % 2]

        names = ("consts_loaded", "setup_chain", "coef_ones", "lam_summed", "lam_exped", "rw_scaled",
                 "rw_turned", "rw_ready", "in_loaded", "x_used", "turned", "scaled_ready", "att_ready",
                 "att_turned", "attT_ready", "y_ready", "z_ready", "zs_ready", "ln_chain", "x1_ready",
                 "xh_ready", "xh_turned", "xhT_ready", "logits_ready", "lgs_ready", "out_stored")
        (consts_loaded, setup_chain, coef_ones, lam_summed, lam_exped, rw_scaled, rw_turned, rw_ready,
         in_loaded, x_used, turned, scaled_ready, att_ready, att_turned, attT_ready, y_ready, z_ready,
         zs_ready, ln_chain, x1_ready, xh_ready, xh_turned, xhT_ready, logits_ready, lgs_ready,
         out_stored) = (sem("j_" + n) for n in names)
        W2, w2, w2_loaded = a["W2"], a["w2"], sem("j_w2_loaded")
        half_set, j_gate_pool, j_gate_dve = sem("j_half_set"), sem("j_gate_pool"), sem("j_gate_dve")
        var_ready, ve_ready, rs_ready = ([sem(f"j_{n}{i}") for i in range(3)] for n in ("var", "ve", "rs"))
        NC = NB * CH
        block = ctx.enter_context(nc.Block())

        @block.sync
        def _(sp):
            for s in (turned, x_used, scaled_ready, zs_ready, att_ready, attT_ready, z_ready,
                      lgs_ready, xhT_ready, out_stored, logits_ready):
                sp.sem_inc(s, 1)
            def row(v, n, parts=P):
                return v.rearrange("(o d) -> o d", o=1).to_broadcast((parts, n))
            consts = [(wo[:], Wo.rearrange("(k p) f -> p k f", p=P)), (rw_rows[:], router_w),
                      (gam[:], row(gamma, D)), (bet[:], row(beta, D)), (rnb[:], row(rn_b, D)),
                      (rbias_in[:], row(router_b, E)), (rg_rows[:], row(rn_g, D, E)),
                      (rw_all[:].rearrange("p e d -> p (e d)"),
                       router_w.rearrange("(o e) d -> o (e d)", o=1).to_broadcast((P, E * D)))]
            consts += [(lam_in[:, i, :], row(l, HD)) for i, l in enumerate(lams)]
            assert len(consts) == NL
            for dst, src in consts:
                sp.dma_start(dst, src).then_inc(consts_loaded, 16)

            def load_chunk(n):
                b, c = n // CH, n % CH
                sp.dma_start(heads[:], od.rearrange("(b g) p (c t) -> b c p g t", b=NB, c=CH)[b, c]
                             ).then_inc(in_loaded, 16)
                sp.dma_start(xs[:], x.rearrange("b (c j p) d -> b c p j d", j=TPC, p=P)[b, c]
                             ).then_inc(in_loaded, 16)

            load_chunk(0)
            for e in range(E):
                sp.dma_start(W2[:, e], w2[e].rearrange("(c p) d -> p c d", p=P)).then_inc(w2_loaded, 16)
            with sp.Fori(0, NB) as b:
                with sp.Fori(0, CH) as c:
                    n = b * CH + c
                    sp.wait_ge(turned, TPC * (n + 1) + 1)
                    sp.wait_ge(x_used, TPC * (n + 1) + 1)
                    load_chunk((n + 1) % NC)
                    sp.wait_ge(x1_ready, TPC * (n + 1))
                    sp.dma_start(x1d.rearrange("(b c j p) d -> b c p j d", b=NB, j=TPC, p=P)[b, c], x1[:]
                                 ).then_inc(out_stored, 16)
                    sp.wait_ge(xh_ready, TPC * (n + 1))
                    sp.dma_start(xhd.rearrange("(b c j p) d -> b c p j d", b=NB, j=TPC, p=P)[b, c], xh[:]
                                 ).then_inc(out_stored, 16)
                    sp.wait_ge(lgs_ready, TPC * (n + 1) + 1)
                    sp.dma_start(lgd.rearrange("p (b c j) e -> b c p j e", b=NB, c=CH)[b, c], lgs[:]
                                 ).then_inc(out_stored, 16)
            sp.wait_ge(out_stored, 48 * NC + 1)
            sp.wait_ge(in_loaded, 32 * (NC + 1))
            sp.wait_ge(w2_loaded, 16 * E)

        @block.gpsimd
        def _(pool):
            nc.gpsimd.memset(coef[:], 1.0).then_inc(coef_ones, 1)
            nc.gpsimd.memset(minus_half[:], -0.5).then_inc(half_set, 1)
            pool.wait_ge(half_set, 1)
            pool.wait_ge(consts_loaded, 16 * NL)
            with pool.Fori(0, NC) as n:
                pool.wait_ge(in_loaded, 32 * (n + 1))
                pool.wait_ge(zs_ready, TPC * n + 1)
                for j in range(TPC):
                    nc.gpsimd.tensor_tensor(xb[:, j, :], xs[:, j, :], bet[:], ALU.add).then_inc(x_used, 1)
                for j in range(TPC):
                    pool.wait_ge(scaled_ready, TPC * n + j + 2)
                    s = scaled[:, j % 2].rearrange("p (h c) d -> p h c d", c=2)
                    nc.gpsimd.tensor_tensor(att[:, j, :].rearrange("p (h d) -> p h d", d=HD), s[:, :, 0, :],
                                            s[:, :, 1, :], ALU.add).then_inc(att_ready, 1)
                def rsqrt(i, tiles):
                    pool.wait_ge(var_ready[i], TPC * n + tiles.stop)
                    pool.sem_inc(j_gate_pool, 1)
                    nc.gpsimd.tensor_scalar(ve[i][:, tiles.start:tiles.stop], mv[i][:, tiles.start:tiles.stop, 1],
                                            EPS, None, ALU.add).then_inc(ve_ready[i], 1)
                    pool.wait_ge(ve_ready[i], TPC // len(tiles) * n + tiles.stop // len(tiles))
                    nc.gpsimd.tensor_tensor(rs[i][:, tiles.start:tiles.stop], ve[i][:, tiles.start:tiles.stop],
                                            minus_half[:, tiles.start:tiles.stop], ALU.pow).then_inc(rs_ready[i], 1)

                for i in range(3):
                    rsqrt(i, range(TPC))

        @block.scalar
        def _(act):
            act.wait_ge(lam_summed, 1)
            nc.scalar.activation(lam_exp[:], lam_sum[:], ACT.Exp).then_inc(lam_exped, 1)
            with act.Fori(0, NC) as n:
                for j in range(TPC):
                    act.wait_ge(att_turned, TPC * n + j + 1)
                    nc.scalar.copy(attT[:, j, :], turn[j % 2][:, 0:D]).then_inc(attT_ready, 1)
                act.wait_ge(out_stored, 48 * n + 1)
                act.wait_ge(logits_ready, TPC * n + 1)
                for j in range(TPC):
                    act.wait_ge(xh_turned, TPC * n + j + 1)
                    nc.scalar.copy(xhT[:, :, j * P:(j + 1) * P],
                                   turn[j % 2][:, 0:D].rearrange("p (k t) -> p k t", k=KD)).then_inc(xhT_ready, 1)

        @block.tensor
        def _(pe):
            pe.wait_ge(rw_scaled, 1)
            for k in range(KD):
                mm = nc.tensor.transpose(turn[0][:, k * E:(k + 1) * E], rw_rows[:, k * P:(k + 1) * P], ident[0:E, 0:E])
            mm.then_inc(rw_turned, 1)
            pe.wait_ge(rw_ready, 1)
            with pe.Fori(0, NC) as n:
                pe.wait_ge(in_loaded, 32 * (n + 1))
                for j in range(TPC):
                    pe.wait_ge(scaled_ready, TPC * n + max(j - 1, 0) + 1)
                    for g in range(G):
                        mm = nc.tensor.transpose(token_major[j % 2][:, g * UNITS:(g + 1) * UNITS, :],
                                                 heads[:, g, j * P:(j + 1) * P], ident[:])
                    mm.then_inc(turned, 1)
                pe.wait_ge(xhT_ready, TPC * n + 1)
                pe.wait_ge(lgs_ready, TPC * n + 1)

                def turn_att(j):
                    pe.wait_ge(att_ready, TPC * n + j + 2)
                    pe.wait_ge(attT_ready, TPC * n + max(j - 1, 0) + 1)
                    for k in range(KD):
                        mm = nc.tensor.transpose(turn[j % 2][:, k * P:(k + 1) * P], att[:, j, k * P:(k + 1) * P],
                                                 ident[:])
                    mm.then_inc(att_turned, 1)

                def turn_xh(j):
                    pe.wait_ge(xh_ready, TPC * n + j + 1)
                    pe.wait_ge(xhT_ready, TPC * n + max(j - 1, 0) + 1)
                    for k in range(KD):
                        mm = nc.tensor.transpose(turn[j % 2][:, k * P:(k + 1) * P], xh[:, j, k * P:(k + 1) * P],
                                                 ident[:])
                    mm.then_inc(xh_turned, 1)

                turn_att(0)
                for j in range(TPC):
                    if j + 1 < TPC:
                        turn_att(j + 1)
                    pe.wait_ge(attT_ready, TPC * n + j + 2)
                    if j >= 4 and j % 2 == 0:
                        pe.wait_ge(z_ready, TPC * n + j - 1)
                    for k in range(KD):
                        mm = nc.tensor.matmul(product(j), attT[:, j, k * P:(k + 1) * P], wo[:, k, :],
                                              start=(k == 0), stop=(k == KD - 1), skip_group_check=True)
                    mm.then_inc(y_ready, 1)
                pe.wait_ge(z_ready, TPC * (n + 1) + 1)
                turn_xh(0)
                for j in range(TPC):
                    if j + 1 < TPC:
                        turn_xh(j + 1)
                    pe.wait_ge(xhT_ready, TPC * n + j + 2)
                    if j >= 4 and j % 2 == 0:
                        pe.wait_ge(lgs_ready, TPC * n + j - 1)
                    for k in range(KD):
                        mm = nc.tensor.matmul(product(j)[:, 0:E], xhT[:, k, j * P:(j + 1) * P], rw_T[:, k, :],
                                              start=(k == 0), stop=(k == KD - 1), skip_group_check=True)
                    mm.then_inc(logits_ready, 1)

        @block.vector
        def _(dve):
            setup = Chain(dve, setup_chain)
            dve.wait_ge(consts_loaded, 16 * NL)
            setup.add(nc.vector.tensor_tensor(lam_mul[:], lam_in[:, 0:4:2, :], lam_in[:, 1:4:2, :], ALU.mult))
            setup.wait()
            nc.vector.tensor_reduce(lam_sum[:], lam_mul[:], AX.X, ALU.add).then_inc(lam_summed, 1)
            dve.wait_ge(lam_exped, 1)
            setup.add(nc.vector.tensor_tensor(lam_neg[:], lam_exp[:, 1:2], lam_exp[:, 0:1], ALU.subtract))
            dve.wait_ge(coef_ones, 1)
            setup.wait()
            setup.add(nc.vector.tensor_scalar(lam_neg[:], lam_neg[:], LAMBDA_INIT, None, ALU.subtract))
            setup.wait()
            setup.add(nc.vector.tensor_scalar(coef[:, 1:NU:2], coef[:, 1:NU:2], lam_neg[:, 0:1], None, ALU.mult))
            setup.add(nc.vector.tensor_tensor(rw_all[:], rw_all[:], rnb[:].rearrange("p (o d) -> p o d", o=1)
                                              .to_broadcast((P, E, D)), ALU.mult))
            setup.wait()
            setup.add(nc.vector.tensor_reduce(rbias[:], rw_all[:], AX.X, ALU.add))
            nc.vector.tensor_tensor(rw_rows[:], rw_rows[:], rg_rows[:], ALU.mult).then_inc(rw_scaled, 1)
            setup.wait()
            setup.add(nc.vector.tensor_tensor(rbias[:], rbias[:], rbias_in[:], ALU.add))
            dve.wait_ge(rw_turned, 1)
            nc.vector.tensor_copy(rw_T[:].rearrange("p k e -> p (k e)"), turn[0][:, 0:KD * E]).then_inc(rw_ready, 1)
            setup.wait()

            LINKS = 5 * TPC
            with dve.Fori(0, NC) as n:
                chain = Chain(dve, ln_chain, n * LINKS)

                def layernorm(i, src, dst, done, before, tiles=range(TPC)):
                    for j in tiles:
                        before(j)
                        chain.add(nc.vector.bn_stats(st[i][:, j, :], src(j)))
                    chain.wait()
                    dve.sem_inc(j_gate_dve, 1)
                    for j in tiles:
                        nc.vector.bn_aggr(mv[i][:, j, :], st[i][:, j, :]).then_inc(var_ready[i], 1)
                    dve.wait_ge(var_ready[i], TPC * n + tiles[-1] + 1)
                    dve.wait_ge(rs_ready[i], TPC // len(tiles) * n + tiles.stop // len(tiles))
                    for j in tiles:
                        nc.vector.tensor_scalar(dst[:, j, :], src(j), mv[i][:, j, 0:1], rs[i][:, j:j + 1],
                                                ALU.subtract, ALU.mult).then_inc(done, 1)

                for j in range(TPC):
                    dve.wait_ge(turned, TPC * n + j + 2)
                    tm = token_major[j % 2]
                    chain.add(nc.vector.reciprocal(rcp[:, j, :], tm[:, :, HD]))
                    chain.wait()
                    chain.add(nc.vector.tensor_tensor(rcc[:, j, :], rcp[:, j, :], coef[:], ALU.mult))
                    chain.wait()
                    dve.wait_ge(att_ready, TPC * n + max(j - 1, 0) + 1)
                    nc.vector.tensor_tensor(scaled[:, j % 2], tm[:, :, 0:HD],
                                            rcc[:, j, :].rearrange("p (u o) -> p u o", o=1).to_broadcast((P, NU, HD)),
                                            ALU.mult).then_inc(scaled_ready, 1)
                for pair in (range(j, j + 2) for j in range(0, TPC, 2)):
                    dve.wait_ge(y_ready, TPC * n + pair.stop)
                    for j in pair:
                        chain.add(nc.vector.bn_stats(st[0][:, j, :], product(j)))
                    chain.wait()
                    dve.sem_inc(j_gate_dve, 1)
                    for j in pair:
                        nc.vector.bn_aggr(mv[0][:, j, :], st[0][:, j, :]).then_inc(var_ready[0], 1)
                    dve.wait_ge(var_ready[0], TPC * n + pair.stop)
                    for j in pair:
                        nc.vector.scalar_tensor_tensor(zg[:, j, :], product(j), mv[0][:, j, 0:1], gam[:], ALU.subtract,
                                                       ALU.mult).then_inc(z_ready, 1)
                dve.wait_ge(z_ready, TPC * (n + 1) + 1)
                dve.wait_ge(rs_ready[0], n + 1)
                for j in range(TPC):
                    dve.wait_ge(x_used, TPC * n + j + 2)
                    nc.vector.scalar_tensor_tensor(zs[:, j, :], zg[:, j, :], rs[0][:, j:j + 1], xb[:, j, :],
                                                   ALU.mult, ALU.add).then_inc(zs_ready, 1)
                dve.wait_ge(out_stored, 48 * n + 1)
                layernorm(1, lambda j: zs[:, j, :], x1, x1_ready, lambda j: dve.wait_ge(zs_ready, TPC * n + j + 2))
                layernorm(2, lambda j: x1[:, j, :], xh, xh_ready, lambda j: dve.wait_ge(x1_ready, TPC * n + j + 1))
                for j in range(TPC):
                    dve.wait_ge(logits_ready, TPC * n + j // 2 * 2 + 3)
                    nc.vector.tensor_tensor(lgs[:, j, :], product(j)[:, 0:E], rbias[:], ALU.add).then_inc(lgs_ready, 1)
                assert chain.n == LINKS, chain.n


def stage_route(nc, a):
    lgd, ln_g, ln_b, b1, owner_i, ln_cols, b1c = (
        a[n] for n in ("lgd", "ln_g", "ln_b", "b1", "owner_i", "ln_cols", "b1c"))
    NT, KD, IC, E, T, TS, NTL, ident = (a[n] for n in ("NT", "KD", "IC", "E", "T", "TS", "NTL", "ident"))
    share, slot, W1, w1, EARLY = (a[n] for n in ("share", "slot", "W1", "w1", "EARLY"))
    TM = T // TS
    with ExitStack() as ctx:
        sb, ps, sem = opener(nc, ctx)
        lg = sb("lg", [P, NT, E], F32)
        lg2 = sb("lg2", [P, NT, E], F32)
        order = sb("order", [P, E], F32)
        thr = sb("thr", [P, TM], F32)
        tau = sb("tau", [P, NTL], F32)
        tau_i = sb("tau_i", [P, NTL], mybir.dt.int32)
        upper = sb("upper", [P, P], F32)
        ones = sb("ones", [P, P], F32)
        pick = [sb(f"pick{i}", [P, NT, E], F32) for i in range(2)]
        rank = [sb(f"rank{i}", [P, NT, E], F32) for i in range(2)]
        hot = [sb(f"hot{i}", [P, NT, E], F32) for i in range(2)]
        best = [sb(f"best{i}", [P, NT], F32) for i in range(2)]
        first = [sb(f"first{i}", [P, NT], F32) for i in range(2)]
        gap = sb("gap", [P, NT], F32)
        eg = sb("eg", [P, NT], F32)
        den = sb("den", [P, NT], F32)
        both = sb("both", [P, NT, E], F32)
        total = sb("total", [P, NT, E], F32)
        run = [sb(f"run{i}", [P, NT, E], F32) for i in range(2)]
        place = sb("place", [P, NT, E], F32)
        over = sb("over", [P, E, TM], F32)
        tiles = sb("tiles", [P, E], F32)
        ends = [sb(f"ends{i}", [P, E], F32) for i in range(2)]
        base = sb("base", [P, E], F32)
        past = sb("past", [P, NTL, E], F32)
        owner = sb("owner", [P, NTL], F32)
        took = [sb(f"took{i}", [P, NT, E], F32) for i in range(2)]
        slot_f = [sb(f"slot_f{i}", [P, NT], F32) for i in range(2)]
        LR = 2 * E * KD
        BR = E * IC
        rows = sb("rows", [LR + BR, P], F32)
        counted = ps("counted", [P, NT * E], F32)
        totals = ps("totals", [P, NT * E], F32)
        turned = ps("cols_turned", [P, TC], F32)
        names = ("loaded", "rows_loaded", "ones_set", "upper_set", "consts_set", "chain", "gap_ready",
                 "eg_ready", "both_ready", "counted_ready", "turned_ready", "owner_ready", "slots_ready")
        (loaded, rows_loaded, ones_set, upper_set, consts_set, chain_sem, gap_ready, eg_ready,
         both_ready, counted_ready, turned_ready, owner_ready, slots_ready) = (sem("r_" + n) for n in names)
        w1_early = sem("r_w1_early")
        block = ctx.enter_context(nc.Block())

        @block.sync
        def _(sp):
            sp.dma_start(lg[:], lgd).then_inc(loaded, 16)
            sp.dma_start(rows[0:E * KD], ln_g.rearrange("e (k d) -> (e k) d", d=P)).then_inc(rows_loaded, 16)
            sp.dma_start(rows[E * KD:LR], ln_b.rearrange("e (k d) -> (e k) d", d=P)).then_inc(rows_loaded, 16)
            sp.dma_start(rows[LR:LR + BR], b1.rearrange("e (c d) -> (e c) d", d=P)).then_inc(rows_loaded, 16)
            for e in range(EARLY):
                sp.dma_start(W1[:, e], w1[e].rearrange("(k p) i -> p k i", p=P)).then_inc(w1_early, 16)
            sp.wait_ge(w1_early, 16 * EARLY)

        @block.gpsimd
        def _(pool):
            nc.gpsimd.memset(ones[:], 1.0).then_inc(ones_set, 1)
            pool.wait_ge(ones_set, 1)
            nc.gpsimd.affine_select(out=upper[:], in_=ones[:], compare_op=ALU.is_gt, fill=0.0, base=0,
                                    pattern=[[1, P]], channel_multiplier=-1).then_inc(upper_set, 1)
            nc.gpsimd.iota(tau_i[:], pattern=[[1, NTL]], base=0, channel_multiplier=0).then_inc(consts_set, 1)

        @block.scalar
        def _(act):
            act.wait_ge(gap_ready, 1)
            nc.scalar.activation(eg[:], gap[:], ACT.Exp).then_inc(eg_ready, 1)
            act.wait_ge(turned_ready, 1)
            nc.scalar.copy(ln_cols[:].rearrange("p w e k -> p (w e k)"), turned[:, 0:LR])
            nc.scalar.copy(b1c[:].rearrange("p e c -> p (e c)"), turned[:, LR:LR + BR])

        @block.tensor
        def _(pe):
            pe.wait_ge(rows_loaded, 48)
            nc.tensor.transpose(turned[:, 0:LR + BR], rows[:], ident[0:LR + BR, 0:LR + BR]
                                ).then_inc(turned_ready, 1)
            pe.wait_ge(upper_set, 1)
            pe.wait_ge(both_ready, 1)
            rhs = both[:].rearrange("p t e -> p (t e)")
            nc.tensor.matmul(counted[:], upper[:], rhs, start=True, stop=True)
            nc.tensor.matmul(totals[:], ones[:], rhs, start=True, stop=True).then_inc(counted_ready, 1)

        @block.vector
        def _(dve):
            chain = Chain(dve, chain_sem)

            def step(ins):
                chain.add(ins)
                chain.wait()

            def over_e(v):
                return v.rearrange("p (t o) -> p t o", o=1).to_broadcast((P, NT, E))

            dve.wait_ge(loaded, 16)
            dve.wait_ge(consts_set, 1)
            step(nc.vector.tensor_copy(tau[:], tau_i[:]))
            step(nc.vector.tensor_scalar(order[:], tau[:, 0:E], -1.0, float(E), ALU.mult, ALU.add))
            step(nc.vector.tensor_scalar(thr[:], tau[:, 0:TM], float(TS), None, ALU.mult))
            order_b = order[:].rearrange("p (o e) -> p o e", o=1).to_broadcast((P, NT, E))
            for r, src in ((0, lg), (1, lg2)):
                step(nc.vector.tensor_reduce(best[r][:], src[:], AX.X, ALU.max))
                step(nc.vector.tensor_tensor(pick[r][:], src[:], over_e(best[r][:]), ALU.is_equal))
                step(nc.vector.tensor_tensor(rank[r][:], pick[r][:], order_b, ALU.mult))
                step(nc.vector.tensor_reduce(first[r][:], rank[r][:], AX.X, ALU.max))
                step(nc.vector.tensor_tensor(hot[r][:], rank[r][:], over_e(first[r][:]), ALU.is_equal))
                if r == 0:
                    step(nc.vector.scalar_tensor_tensor(lg2[:], hot[0][:], -3.0e38, lg[:], ALU.mult, ALU.add))
            nc.vector.tensor_tensor(both[:], hot[0][:], hot[1][:], ALU.add).then_inc(both_ready, 1)
            nc.vector.tensor_tensor(gap[:], best[1][:], best[0][:], ALU.subtract).then_inc(gap_ready, 1)
            dve.wait_ge(eg_ready, 1)
            step(nc.vector.tensor_scalar(den[:], eg[:], 1.0, None, ALU.add))
            step(nc.vector.reciprocal(share[0][:], den[:]))
            step(nc.vector.tensor_tensor(share[1][:], share[0][:], eg[:], ALU.mult))
            dve.wait_ge(counted_ready, 1)
            step(nc.vector.tensor_copy(total[:].rearrange("p t e -> p (t e)"), totals[:]))
            src, d, i = total, 1, 0
            while d < NT:
                chain.add(nc.vector.tensor_copy(run[i][:, 0:d, :], src[:, 0:d, :]))
                step(nc.vector.tensor_tensor(run[i][:, d:NT, :], src[:, d:NT, :], src[:, 0:NT - d, :], ALU.add))
                src, d, i = run[i], 2 * d, 1 - i
            count = src[:, NT - 1, :].rearrange("p (e o) -> p e o", o=1).to_broadcast((P, E, TM))
            step(nc.vector.tensor_tensor(over[:], count, thr[:].rearrange("p (o m) -> p o m", o=1)
                                         .to_broadcast((P, E, TM)), ALU.is_gt))
            step(nc.vector.tensor_reduce(tiles[:], over[:], AX.X, ALU.add))
            end, d, i = tiles, 1, 0
            while d < E:
                chain.add(nc.vector.tensor_copy(ends[i][:, 0:d], end[:, 0:d]))
                step(nc.vector.tensor_tensor(ends[i][:, d:E], end[:, d:E], end[:, 0:E - d], ALU.add))
                end, d, i = ends[i], 2 * d, 1 - i
            step(nc.vector.tensor_tensor(past[:], end[:].rearrange("p (o e) -> p o e", o=1).to_broadcast((P, NTL, E)),
                                         tau[:].rearrange("p (m o) -> p m o", o=1).to_broadcast((P, NTL, E)),
                                         ALU.is_le))
            step(nc.vector.tensor_reduce(owner[:], past[:], AX.X, ALU.add))
            nc.vector.tensor_scalar(owner_i[:], owner[:], float(E - 1), None, ALU.min).then_inc(owner_ready, 1)
            step(nc.vector.tensor_tensor(base[:], end[:], tiles[:], ALU.subtract))
            step(nc.vector.tensor_tensor(place[:], src[:], total[:], ALU.subtract))
            step(nc.vector.scalar_tensor_tensor(place[:], base[:].rearrange("p (o e) -> p o e", o=1)
                                                .to_broadcast((P, NT, E)), float(TS), place[:], ALU.mult, ALU.add))
            step(nc.vector.tensor_tensor(place[:], counted[:].rearrange("p (t e) -> p t e", e=E), place[:], ALU.add))
            for r in range(2):
                step(nc.vector.tensor_tensor(took[r][:], hot[r][:], place[:], ALU.mult))
                step(nc.vector.tensor_reduce(slot_f[r][:], took[r][:], AX.X, ALU.add))
                nc.vector.tensor_copy(slot[r][:], slot_f[r][:]).then_inc(slots_ready, 1)


def stage_scatter(nc, a):
    xhd, xgd, slot, D, E, KD, NCH = (a[n] for n in ("xhd", "xgd", "slot", "D", "E", "KD", "NCH"))
    EARLY = a["EARLY"]
    w1, b2, W1, b1c, b2s, ln_cols, IC = (a[n] for n in ("w1", "b2", "W1", "b1c", "b2s", "ln_cols", "IC"))
    with ExitStack() as ctx:
        sb, ps, sem = opener(nc, ctx)
        xh = sb("scatter_xh", [P, 2, TPC, D], F32)
        cur = sb("scatter_cur", [P, 2, 2, TPC], mybir.dt.int32)
        cur_ready, gate = sem("s_cur_ready"), sem("s_gate")
        xh_loaded = [sem(f"s_xh_loaded{i}") for i in range(2)]
        scattered = [sem(f"s_scattered{i}") for i in range(2)]
        SC = 16 * 2 * TPC
        shift = ps("shift", [P, E, IC, 2], F32)
        w1_loaded = [sem(f"w1_loaded{i}") for i in range(2)]
        b2_loaded, shift_ready = sem("s_b2_loaded"), sem("s_shift_ready")
        block = ctx.enter_context(nc.Block())

        @block.sync
        def _(sp):
            def load(n, h):
                sp.dma_start(xh[:, h], xhd.rearrange("(n j p) d -> n p j d", j=TPC, p=P)[n]).then_inc(xh_loaded[h], 16)

            for h in range(2):
                load(h, h)
            sp.dma_start(b2s[:].rearrange("p e d -> p (e d)"),
                         b2.rearrange("(o e) d -> o (e d)", o=1).to_broadcast((P, E * D))).then_inc(b2_loaded, 16)
            with sp.Fori(0, NCH // 2 - 1) as it:
                for h in range(2):
                    sp.wait_ge(scattered[h], SC * (it + 1))
                    load(2 * it + h + 2, h)
            for h in range(2):
                sp.wait_ge(scattered[h], SC * (NCH // 2))
            sp.wait_ge(b2_loaded, 16)

        @block.scalar
        def _(act):
            act.wait_ge(xh_loaded[1], 16)
            for e in range(EARLY, E):
                if e >= EARLY + 2:
                    act.wait_ge(w1_loaded[e % 2], 16 * ((e - EARLY) // 2))
                act.dma_start(W1[:, e], w1[e].rearrange("(k p) i -> p k i", p=P)).then_inc(w1_loaded[e % 2], 16)

        @block.tensor
        def _(pe):
            for e in range(E):
                if e >= EARLY:
                    pe.wait_ge(w1_loaded[e % 2], 16 * ((e - EARLY) // 2 + 1))
                for c in range(IC):
                    for k in range(KD):
                        mm = nc.tensor.matmul(shift[:, e, c, :], W1[:, e, k, c * P:(c + 1) * P], ln_cols[:, :, e, k],
                                              start=(k == 0), stop=(k == KD - 1), skip_group_check=True)
                mm.then_inc(shift_ready, 1)

        @block.vector
        def _(dve):
            for e in range(E):
                dve.wait_ge(shift_ready, e + 1)
                for k in range(KD):
                    nc.vector.tensor_scalar(W1[:, e, k, :], W1[:, e, k, :], ln_cols[:, 0, e, k:k + 1], None, ALU.mult)
            nc.vector.tensor_tensor(b1c[:], shift[:, :, :, 1], b1c[:], ALU.add)

        @block.gpsimd
        def _(pool):
            with pool.Fori(0, NCH // 2) as it:
                for h in range(2):
                    pool.wait_ge(xh_loaded[h], 16 * (it + 1))
                    pool.sem_inc(gate, 1)
                    for r in range(2):
                        nc.gpsimd.tensor_copy(cur[:, h, r, :], slot[r][:, bass.ds((2 * it + h) * TPC, TPC)]
                                              ).then_inc(cur_ready, 1)
                    pool.wait_ge(cur_ready, 2 * (2 * it + h + 1))
                    pool.sem_inc(gate, 1)
                    for j in range(TPC):
                        for r in range(2):
                            nc.gpsimd.indirect_dma_start(
                                xgd, bass.IndirectOffsetOnAxis(ap=cur[:, h, r, j:j + 1], axis=0),
                                xh[:, h, j, :], None).then_inc(scattered[h], 16)


def stage_experts(nc, a):
    xgd, ygd, W1, W2, b1c, b2s, owner_i = (a[n] for n in ("xgd", "ygd", "W1", "W2", "b1c", "b2s", "owner_i"))
    KD, IC, D, E, I, USED, ident = (a[n] for n in ("KD", "IC", "D", "E", "I", "USED", "ident"))
    with ExitStack() as ctx:
        sb, ps, sem = opener(nc, ctx)
        xg = [sb(f"xg{i}", [P, D], F32) for i in range(2)]
        xgT = [sb(f"xgT{i}", [P, D], F32) for i in range(2)]
        w1 = [sb(f"w1_{i}", [P, KD, I], F32) for i in range(2)]
        u = sb("u", [P, IC, P], F32)
        h = [sb(f"h{i}", [P, IC, P], F32) for i in range(2)]
        y = [sb(f"y{i}", [P, D], F32) for i in range(2)]
        pxT = ps("e_xT", [P, TC], F32)
        pre = ps("pre", [P, IC, P], F32)
        py = [ps(f"py{i}", [P, TC], F32) for i in range(2)]
        names = ("turned", "xgT_ready", "pre_ready", "u_ready", "h_ready", "py_ready", "y_ready",
                 "w1_ready")
        turned, xgT_ready, pre_ready, u_ready, h_ready, py_ready, y_ready, w1_ready = (
            sem("e_" + n) for n in names)
        xg_loaded = [sem(f"e_xg_loaded{i}") for i in range(2)]
        y_stored = [sem(f"e_y_stored{i}") for i in range(2)]
        block = ctx.enter_context(nc.Block())

        def run(eng, step):
            rounds = (USED - 4) // 2
            with eng.Fori(0, rounds) as it:
                for p in range(2):
                    step(2 * it + p, it, p, 4)
            for n in range(2 * rounds, USED):
                step(n, n // 2, n % 2, min(4, USED - 1 - n))

        def owner(eng, tile):
            return eng.value_load(owner_i[0:1, bass.ds(tile, 1)], min_val=0, max_val=E - 1)

        @block.sync
        def _(sp):
            sp.sem_inc(y_ready, 2)
            for s in y_stored:
                sp.sem_inc(s, 1)
            rows = xgd.rearrange("(n p) d -> n p d", p=P)
            results = ygd.rearrange("(n p) d -> n p d", p=P)

            def load(n, p):
                sp.dma_start(xg[p][:], rows[n]).then_inc(xg_loaded[p], 16)

            def step(n, it, p, left):
                if left >= 4:
                    sp.wait_ge(turned, n + 3)
                    load(n + 4, p)
                sp.wait_ge(y_ready, n + 3)
                sp.dma_start(results[n], y[p][:]).then_inc(y_stored[p], 16)

            for n in range(2):
                load(n, n)
            for n in range(2):
                sp.wait_ge(turned, n + 1)
                load(n + 2, n)
            run(sp, step)
            for p in range(2):
                sp.wait_ge(y_stored[p], 16 * ((USED + 1 - p) // 2) + 1)

        @block.tensor
        def _(pe):
            def turn_rows(n, it, p):
                pe.wait_ge(xg_loaded[p], 16 * (it + 1))
                for k in range(KD):
                    mm = nc.tensor.transpose(pxT[:, k * P:(k + 1) * P], xg[p][:, k * P:(k + 1) * P], ident[:])
                mm.then_inc(turned, 1)

            def times_w1(n, p):
                pe.wait_ge(w1_ready, n + 1)
                pe.wait_ge(xgT_ready, n + 1)
                for c in range(IC):
                    for k in range(KD):
                        mm = nc.tensor.matmul(pre[:, c, :], w1[p][:, k, c * P:(c + 1) * P],
                                              xgT[p][:, k * P:(k + 1) * P], start=(k == 0), stop=(k == KD - 1))
                mm.then_inc(pre_ready, 1)

            def step(n, it, p, left):
                if left >= 1:
                    pe.wait_ge(u_ready, n + 1)
                    times_w1(n + 1, 1 - p)
                if left >= 2:
                    turn_rows(n + 2, it + 1, p)
                e = owner(pe, n)
                pe.wait_ge(h_ready, n + 1)
                pe.wait_ge(y_ready, n + 1)
                for c in range(IC):
                    mm = nc.tensor.matmul(py[p][:, 0:D], h[p][:, c, :],
                                          W2[:, bass.ds(e, 1), c, :], start=(c == 0), stop=(c == IC - 1))
                mm.then_inc(py_ready, 1)

            turn_rows(0, 0, 0)
            times_w1(0, 0)
            turn_rows(1, 0, 1)
            run(pe, step)

        @block.scalar
        def _(act):
            def copy_rows(n, p):
                act.wait_ge(turned, n + 1)
                nc.scalar.copy(xgT[p][:], pxT[:, 0:D]).then_inc(xgT_ready, 1)

            def gelu(n, p):
                act.wait_ge(u_ready, n + 1)
                nc.scalar.activation(h[p][:], u[:], ACT.Gelu).then_inc(h_ready, 1)

            def step(n, it, p, left):
                if left >= 1:
                    gelu(n + 1, 1 - p)
                if left >= 2:
                    copy_rows(n + 2, p)

            copy_rows(0, 0)
            gelu(0, 0)
            copy_rows(1, 1)
            run(act, step)

        @block.vector
        def _(dve):
            def take_w1(n, p, used):
                e = owner(dve, n)
                if used is not None:
                    dve.wait_ge(pre_ready, used)
                nc.vector.tensor_copy(w1[p][:], W1[:, bass.ds(e, 1), :, :].rearrange("p o k i -> p (o k) i")
                                      ).then_inc(w1_ready, 1)

            def add_b1(n, used):
                e = owner(dve, n)
                if used is not None:
                    dve.wait_ge(h_ready, used)
                dve.wait_ge(pre_ready, n + 1)
                nc.vector.tensor_tensor(u[:], pre[:], b1c[:, bass.ds(e, 1), :].rearrange("p o c -> p c o")
                                        .to_broadcast((P, IC, P)), ALU.add).then_inc(u_ready, 1)

            def step(n, it, p, left):
                if left >= 2:
                    take_w1(n + 2, p, n + 1)
                if left >= 1:
                    add_b1(n + 1, n + 1)
                e = owner(dve, n)
                dve.wait_ge(y_stored[p], 16 * it + 1)
                dve.wait_ge(py_ready, n + 1)
                nc.vector.tensor_tensor(y[p][:], py[p][:, 0:D], b2s[:, bass.ds(e, 1), :].rearrange("p o d -> p (o d)"),
                                        ALU.add).then_inc(y_ready, 1)

            take_w1(0, 0, None)
            take_w1(1, 1, None)
            add_b1(0, None)
            run(dve, step)


def stage_finish(nc, a):
    x1d, ygd, out, slot, share = (a[n] for n in ("x1d", "ygd", "out", "slot", "share"))
    NCH, D = a["NCH"], a["D"]
    with ExitStack() as ctx:
        sb, ps, sem = opener(nc, ctx)
        x1 = sb("f_x1", [P, TPC, D], F32)
        got = sb("f_got", [P, 2, TPC, 2, D], F32)
        cur = sb("f_cur", [P, 2, 2, TPC], mybir.dt.int32)
        part = sb("f_part", [P, 2, TPC], F32)
        one = sb("f_one", [P, TPC, D], F32)
        two = sb("f_two", [P, TPC, D], F32)
        fin = sb("f_fin", [P, TPC, D], F32)
        st, mv = sb("f_st", [P, TPC, 6], F32), sb("f_mv", [P, TPC, 2], F32)
        ve, rs = sb("f_ve", [P, TPC], F32), sb("f_rs", [P, TPC], F32)
        minus_half = sb("f_minus_half", [P, TPC], F32)
        names = ("cur_ready", "part_ready", "half_set", "gate_pool", "gate_dve", "one_ready", "two_ready", "st_ready",
                 "var_ready", "ve_ready", "rs_ready", "fin_ready")
        (cur_ready, part_ready, half_set, gate_pool, gate_dve, one_ready, two_ready, st_ready,
         var_ready, ve_ready, rs_ready, fin_ready) = (sem("f_" + n) for n in names)
        x1_loaded, stored = ([sem(f"f_{n}{j}") for j in range(TPC)] for n in ("x1_loaded", "stored"))
        gathered = [[sem(f"f_gathered{h}{j}") for j in range(TPC)] for h in range(2)]
        block = ctx.enter_context(nc.Block())

        @block.sync
        def _(sp):
            for s in (two_ready, fin_ready, *stored):
                sp.sem_inc(s, 1)

            def load(n, j):
                sp.dma_start(x1[:, j, :], x1d.rearrange("(n j p) d -> n j p d", j=TPC, p=P)[n, j]
                             ).then_inc(x1_loaded[j], 16)

            def store(n, j):
                sp.wait_ge(fin_ready, TPC * n + j + 2)
                sp.dma_start(out.rearrange("b (c j p) d -> (b c) j p d", j=TPC, p=P)[n, j], fin[:, j, :]
                             ).then_inc(stored[j], 16)

            for j in range(TPC):
                load(0, j)
            with sp.Fori(0, NCH - 1) as n:
                for j in range(TPC):
                    sp.wait_ge(two_ready, TPC * n + j + 2)
                    load(n + 1, j)
                for j in range(TPC):
                    store(n, j)
            for j in range(TPC):
                store(NCH - 1, j)
            for j in range(TPC):
                sp.wait_ge(stored[j], 16 * NCH + 1)

        @block.gpsimd
        def _(pool):
            nc.gpsimd.memset(minus_half[:], -0.5).then_inc(half_set, 1)
            pool.wait_ge(half_set, 1)

            def gather(n, h, used):
                if used is not None:
                    pool.wait_ge(one_ready, used)
                    pool.wait_ge(two_ready, used + 1)
                    pool.sem_inc(gate_pool, 1)
                for r in range(2):
                    nc.gpsimd.tensor_copy(cur[:, h, r, :], slot[r][:, bass.ds(n * TPC, TPC)]).then_inc(cur_ready, 1)
                pool.wait_ge(cur_ready, 2 * (n + 1))
                pool.sem_inc(gate_pool, 1)
                for j in range(TPC):
                    for r in range(2):
                        nc.gpsimd.indirect_dma_start(
                            got[:, h, j, r, :], None, ygd,
                            bass.IndirectOffsetOnAxis(ap=cur[:, h, r, j:j + 1], axis=0)).then_inc(gathered[h][j], 16)

            def rsqrt(n):
                pool.wait_ge(var_ready, TPC * (n + 1))
                pool.sem_inc(gate_pool, 1)
                nc.gpsimd.tensor_scalar(ve[:], mv[:, :, 1], EPS, None, ALU.add).then_inc(ve_ready, 1)
                pool.wait_ge(ve_ready, n + 1)
                nc.gpsimd.tensor_tensor(rs[:], ve[:], minus_half[:], ALU.pow).then_inc(rs_ready, 1)

            for h in range(2):
                gather(h, h, None)
            with pool.Fori(0, NCH // 2 - 1) as it:
                for h in range(2):
                    rsqrt(2 * it + h)
                    gather(2 * it + h + 2, h, TPC * (2 * it + h + 1))
            for h in range(2):
                rsqrt(NCH - 2 + h)

        @block.vector
        def _(dve):
            with dve.Fori(0, NCH // 2) as it:
                for h in range(2):
                    n = 2 * it + h
                    dve.wait_ge(fin_ready, TPC * n + 1)
                    for r in range(2):
                        nc.vector.tensor_copy(part[:, r, :], share[r][:, bass.ds(n * TPC, TPC)]).then_inc(part_ready, 1)
                    dve.wait_ge(part_ready, 2 * (n + 1))
                    for j in range(TPC):
                        dve.wait_ge(x1_loaded[j], 16 * (n + 1))
                        dve.wait_ge(gathered[h][j], 32 * (it + 1))
                        nc.vector.scalar_tensor_tensor(one[:, j, :], got[:, h, j, 0, :], part[:, 0, j:j + 1], x1[:, j, :],
                                                       ALU.mult, ALU.add).then_inc(one_ready, 1)
                        dve.wait_ge(one_ready, TPC * n + j + 1)
                        nc.vector.scalar_tensor_tensor(two[:, j, :], got[:, h, j, 1, :], part[:, 1, j:j + 1], one[:, j, :],
                                                       ALU.mult, ALU.add).then_inc(two_ready, 1)
                    for j in range(TPC):
                        dve.wait_ge(two_ready, TPC * n + j + 2)
                        nc.vector.bn_stats(st[:, j, :], two[:, j, :]).then_inc(st_ready, 1)
                    dve.wait_ge(st_ready, TPC * (n + 1))
                    dve.sem_inc(gate_dve, 1)
                    for j in range(TPC):
                        nc.vector.bn_aggr(mv[:, j, :], st[:, j, :]).then_inc(var_ready, 1)
                    dve.wait_ge(var_ready, TPC * (n + 1))
                    dve.wait_ge(rs_ready, n + 1)
                    for j in range(TPC):
                        dve.wait_ge(stored[j], 16 * n + 1)
                        nc.vector.tensor_scalar(fin[:, j, :], two[:, j, :], mv[:, j, 0:1], rs[:, j:j + 1],
                                                ALU.subtract, ALU.mult).then_inc(fin_ready, 1)


_INS = ["L0_attn_x", "L0_attn_Wq", "L0_attn_Wk", "L0_attn_Wv", "L0_attn_Wo", "L0_attn_lambda_q1",
        "L0_attn_lambda_k1", "L0_attn_lambda_q2", "L0_attn_lambda_k2", "L0_attn_gamma", "L0_attn_beta",
        "L0_ffn_rn_g", "L0_ffn_rn_b", "L0_ffn_router_w", "L0_ffn_router_b", "L0_ffn_ln_g", "L0_ffn_ln_b",
        "L0_ffn_w1", "L0_ffn_b1", "L0_ffn_w2", "L0_ffn_b2"]


def kernel(**inputs):
    import numpy as _np
    import concourse.bacc as _bacc
    from concourse import mybir as _mybir
    from concourse.bass_utils import run_bass_kernel_spmd as _run

    nc = _bacc.Bacc("TRN2", target_bir_lowering=False, num_devices=1)
    arrays, args = {}, []
    for name in _INS:
        a = _np.ascontiguousarray(inputs[name])
        arrays[f"in_{name}_dram"] = a
        args.append(nc.dram_tensor(f"in_{name}_dram", a.shape, _mybir.dt.from_np(a.dtype), kind="ExternalInput").ap())
    shape = inputs["L0_attn_x"].shape
    args.append(nc.dram_tensor("out_0_dram", shape, _mybir.dt.float32, kind="ExternalOutput").ap())
    diff_attention_moe(nc, *args)
    r = _run(nc, [arrays], core_ids=[0])
    return r.results[0]["out_0_dram"]
```
